# Optimizing a Trainium2 kernel written in Bass

```python
import numpy as np
import jax
import jax.numpy as jnp

def _softmax(x, axis=-1):
    return jax.nn.softmax(x, axis=axis)

def _gelu(x):
    return jax.nn.gelu(x, approximate=True)

def _silu(x):
    return jax.nn.silu(x)

def _sigmoid(x):
    return jax.nn.sigmoid(x)

def _layernorm(x, axis=-1, eps=1e-05):
    m = jnp.mean(x, axis=axis, keepdims=True)
    v = jnp.var(x, axis=axis, keepdims=True)
    return (x - m) / jnp.sqrt(v + eps)

def _scatter_add(tgt, idx, src, axis=0):
    return tgt.at[idx].add(src)

def _segment_sum(src, seg, n):
    return jax.ops.segment_sum(src, seg, n)
kernel_name = 'mk_macaron_d2_jaxref_r8_55f65a'

def setup_inputs(seed: int=0):
    np.random.seed(seed)
    _w = jnp.asarray

    def _L0_attn_setup():
        import jax, jax.numpy as jnp
        import numpy as np
        B, T, D = (2, 256, 128)
        H, DK, DV = (16, 64, 64)

        def _hla(x, W_q, W_k, W_v, W_o):
            b, t, _ = x.shape
            q = (x @ W_q).reshape(b, t, H, DK).transpose(1, 0, 2, 3)
            k = (x @ W_k).reshape(b, t, H, DK).transpose(1, 0, 2, 3)
            v = (x @ W_v).reshape(b, t, H, DV).transpose(1, 0, 2, 3)
            S_K0 = jnp.zeros((b, H, DK, DK), x.dtype)
            C_QV0 = jnp.zeros((b, H, DK, DV), x.dtype)
            G0 = jnp.zeros((b, H, DK, DV), x.dtype)

            def step(carry, qkv):
                S_K, C_QV, G = carry
                q_t, k_t, v_t = qkv
                k_C = jnp.einsum('bhk,bhkv->bhv', k_t, C_QV)
                G = G + k_t[..., :, None] * k_C[..., None, :]
                S_K = S_K + k_t[..., :, None] * k_t[..., None, :]
                C_QV = C_QV + q_t[..., :, None] * v_t[..., None, :]
                S_C = jnp.einsum('bhkj,bhjv->bhkv', S_K, C_QV)
                o_t = jnp.einsum('bhk,bhkv->bhv', q_t, S_C - G)
                return ((S_K, C_QV, G), o_t)
            _, outs = jax.lax.scan(step, (S_K0, C_QV0, G0), (q, k, v))
            out = outs.transpose(1, 0, 2, 3).reshape(b, t, H * DV)
            return out @ W_o
        key = jax.random.key(seed)
        ks = jax.random.split(key, 5)
        scale = 0.1 * (6.0 / (D + D)) ** 0.5
        return {'x': jax.random.normal(ks[0], (B, T, D), dtype=jnp.float32), 'W_q': jax.random.normal(ks[1], (D, H * DK), dtype=jnp.float32) * scale, 'W_k': jax.random.normal(ks[2], (D, H * DK), dtype=jnp.float32) * scale, 'W_v': jax.random.normal(ks[3], (D, H * DV), dtype=jnp.float32) * scale, 'W_o': jax.random.normal(ks[4], (H * DV, D), dtype=jnp.float32) * scale}
    _L0_attn_in = _L0_attn_setup()

    def _L0_ffn_setup():
        import jax, jax.numpy as jnp
        import numpy as np
        TOP_K = 2
        CAPACITY = 512
        EPS = 1e-06
        W_SCALE = 0.02

        def _rms(x, w):
            return x * jax.lax.rsqrt(jnp.mean(x * x, axis=-1, keepdims=True) + EPS) * w
        key = jax.random.key(seed)
        ks = jax.random.split(key, 8)
        B, S, H, F, E = (8, 512, 128, 256, 8)
        F4 = F // 4
        return {'hidden_states': jax.random.normal(ks[0], (B, S, H), jnp.float32), 'Wr': jax.random.normal(ks[1], (H, E), jnp.float32) * W_SCALE, 'norm_w': jnp.ones((E, H), jnp.float32), 'Wg': jax.random.normal(ks[2], (E, H, F), jnp.float32) * W_SCALE, 'Wu': jax.random.normal(ks[3], (E, H, F), jnp.float32) * W_SCALE, 'Wd': jax.random.normal(ks[4], (E, F, H), jnp.float32) * W_SCALE, 'f_norm': jnp.ones((H,), jnp.float32), 'fWg': jax.random.normal(ks[5], (H, F4), jnp.float32) * W_SCALE, 'fWu': jax.random.normal(ks[6], (H, F4), jnp.float32) * W_SCALE, 'fWd': jax.random.normal(ks[7], (F4, H), jnp.float32) * W_SCALE}
    _L0_ffn_in = _L0_ffn_setup()

    def _L1_attn_setup():
        import jax, jax.numpy as jnp
        import numpy as np
        B, T, D, H = (2, 256, 128, 16)
        DH = D // H
        ROPE_BASE = 10000.0

        def _rope(Xh, cos, sin):
            x0 = Xh[..., 0::2]
            x1 = Xh[..., 1::2]
            r0 = cos * x0 - sin * x1
            r1 = sin * x0 + cos * x1
            return jnp.stack((r0, r1), axis=-1).reshape(Xh.shape)
        key = jax.random.key(seed)
        ks = jax.random.split(key, 5)
        s = 1.0 / np.sqrt(D)
        return {'X': jax.random.normal(ks[0], (B, T, D), dtype=jnp.float32), 'W_q': jax.random.normal(ks[1], (D, D), dtype=jnp.float32) * s, 'W_k': jax.random.normal(ks[2], (D, D), dtype=jnp.float32) * s, 'W_v': jax.random.normal(ks[3], (D, D), dtype=jnp.float32) * s, 'W_o': jax.random.normal(ks[4], (D, D), dtype=jnp.float32) * s}
    _L1_attn_in = _L1_attn_setup()

    def _L1_ffn_setup():
        import jax, jax.numpy as jnp
        import numpy as np
        TOP_K = 2

        def _mlp(x, w1, b1, w2, b2):
            h = jax.nn.gelu(jnp.einsum('bsd,di->bsi', x, w1) + b1)
            return jnp.einsum('bsi,id->bsd', h, w2) + b2
        key = jax.random.key(seed)
        ks = jax.random.split(key, 8)
        B, S, D, I, E = (2, 256, 128, 512, 8)
        s_in = 1.0 / np.sqrt(D)
        s_mid = 1.0 / np.sqrt(I)
        return {'x': jax.random.normal(ks[0], (B, S, D), jnp.float32), 'gate_w': jax.random.normal(ks[1], (D, E), jnp.float32) * s_in, 'gate_b': jnp.zeros((E,), jnp.float32), 'sh_w1': jax.random.normal(ks[2], (D, I), jnp.float32) * s_in, 'sh_b1': jnp.zeros((I,), jnp.float32), 'sh_w2': jax.random.normal(ks[3], (I, D), jnp.float32) * s_mid, 'sh_b2': jnp.zeros((D,), jnp.float32), 'ew1': jax.random.normal(ks[4], (E, D, I), jnp.float32) * s_in, 'eb1': jnp.zeros((E, I), jnp.float32), 'ew2': jax.random.normal(ks[5], (E, I, D), jnp.float32) * s_mid, 'eb2': jnp.zeros((E, D), jnp.float32)}
    _L1_ffn_in = _L1_ffn_setup()
    _d = {'L0_attn_x': _L0_attn_in['x'], 'L0_attn_W_q': _L0_attn_in['W_q'], 'L0_attn_W_k': _L0_attn_in['W_k'], 'L0_attn_W_v': _L0_attn_in['W_v'], 'L0_attn_W_o': _L0_attn_in['W_o'], 'L0_ffn_Wr': _L0_ffn_in['Wr'], 'L0_ffn_norm_w': _L0_ffn_in['norm_w'], 'L0_ffn_Wg': _L0_ffn_in['Wg'], 'L0_ffn_Wu': _L0_ffn_in['Wu'], 'L0_ffn_Wd': _L0_ffn_in['Wd'], 'L0_ffn_f_norm': _L0_ffn_in['f_norm'], 'L0_ffn_fWg': _L0_ffn_in['fWg'], 'L0_ffn_fWu': _L0_ffn_in['fWu'], 'L0_ffn_fWd': _L0_ffn_in['fWd'], 'L1_attn_W_q': _L1_attn_in['W_q'], 'L1_attn_W_k': _L1_attn_in['W_k'], 'L1_attn_W_v': _L1_attn_in['W_v'], 'L1_attn_W_o': _L1_attn_in['W_o'], 'L1_ffn_gate_w': _L1_ffn_in['gate_w'], 'L1_ffn_gate_b': _L1_ffn_in['gate_b'], 'L1_ffn_sh_w1': _L1_ffn_in['sh_w1'], 'L1_ffn_sh_b1': _L1_ffn_in['sh_b1'], 'L1_ffn_sh_w2': _L1_ffn_in['sh_w2'], 'L1_ffn_sh_b2': _L1_ffn_in['sh_b2'], 'L1_ffn_ew1': _L1_ffn_in['ew1'], 'L1_ffn_eb1': _L1_ffn_in['eb1'], 'L1_ffn_ew2': _L1_ffn_in['ew2'], 'L1_ffn_eb2': _L1_ffn_in['eb2']}
    _x0 = _d['L0_attn_x']
    _d['L0_attn_x'] = jax.random.normal(jax.random.fold_in(jax.random.key(seed), 1), (8, 256, 128), dtype=_x0.dtype)
    del _x0
    return _d

def reference(L0_attn_x, L0_attn_W_q, L0_attn_W_k, L0_attn_W_v, L0_attn_W_o, L0_ffn_Wr, L0_ffn_norm_w, L0_ffn_Wg, L0_ffn_Wu, L0_ffn_Wd, L0_ffn_f_norm, L0_ffn_fWg, L0_ffn_fWu, L0_ffn_fWd, L1_attn_W_q, L1_attn_W_k, L1_attn_W_v, L1_attn_W_o, L1_ffn_gate_w, L1_ffn_gate_b, L1_ffn_sh_w1, L1_ffn_sh_b1, L1_ffn_sh_w2, L1_ffn_sh_b2, L1_ffn_ew1, L1_ffn_eb1, L1_ffn_ew2, L1_ffn_eb2):

    def _L0_attn_ref(x, W_q, W_k, W_v, W_o):
        import jax, jax.numpy as jnp
        import numpy as np
        B, T, D = (2, 256, 128)
        H, DK, DV = (16, 64, 64)

        def _hla(x, W_q, W_k, W_v, W_o):
            b, t, _ = x.shape
            q = (x @ W_q).reshape(b, t, H, DK).transpose(1, 0, 2, 3)
            k = (x @ W_k).reshape(b, t, H, DK).transpose(1, 0, 2, 3)
            v = (x @ W_v).reshape(b, t, H, DV).transpose(1, 0, 2, 3)
            S_K0 = jnp.zeros((b, H, DK, DK), x.dtype)
            C_QV0 = jnp.zeros((b, H, DK, DV), x.dtype)
            G0 = jnp.zeros((b, H, DK, DV), x.dtype)

            def step(carry, qkv):
                S_K, C_QV, G = carry
                q_t, k_t, v_t = qkv
                k_C = jnp.einsum('bhk,bhkv->bhv', k_t, C_QV)
                G = G + k_t[..., :, None] * k_C[..., None, :]
                S_K = S_K + k_t[..., :, None] * k_t[..., None, :]
                C_QV = C_QV + q_t[..., :, None] * v_t[..., None, :]
                S_C = jnp.einsum('bhkj,bhjv->bhkv', S_K, C_QV)
                o_t = jnp.einsum('bhk,bhkv->bhv', q_t, S_C - G)
                return ((S_K, C_QV, G), o_t)
            _, outs = jax.lax.scan(step, (S_K0, C_QV0, G0), (q, k, v))
            out = outs.transpose(1, 0, 2, 3).reshape(b, t, H * DV)
            return out @ W_o
        return _hla(x, W_q, W_k, W_v, W_o)

    def _L0_ffn_ref(hidden_states, Wr, norm_w, Wg, Wu, Wd, f_norm, fWg, fWu, fWd):
        import jax, jax.numpy as jnp
        import numpy as np
        TOP_K = 2
        CAPACITY = 512
        EPS = 1e-06
        W_SCALE = 0.02

        def _rms(x, w):
            return x * jax.lax.rsqrt(jnp.mean(x * x, axis=-1, keepdims=True) + EPS) * w
        B, S, H = hidden_states.shape
        E = Wr.shape[1]
        N = B * S
        x = hidden_states.reshape(N, H)
        probs = jax.nn.softmax(x @ Wr, axis=-1)
        w_topk, e_topk = jax.lax.top_k(probs, TOP_K)
        e_flat = e_topk.reshape(-1)
        oh = jax.nn.one_hot(e_flat, E, dtype=jnp.int32)
        pos = jnp.take_along_axis(jnp.cumsum(oh, axis=0) - 1, e_flat[:, None], axis=1)[:, 0]
        keep = pos < CAPACITY
        x_rep = jnp.repeat(x, TOP_K, axis=0)
        buf = jnp.zeros((E, CAPACITY, H), x.dtype).at[e_flat, pos].set(x_rep, mode='drop')
        h = _rms(buf, norm_w[:, None, :])
        gate = jax.nn.gelu(jnp.einsum('ech,ehf->ecf', h, Wg), approximate=False)
        up = jnp.einsum('ech,ehf->ecf', h, Wu)
        buf_out = jnp.einsum('ecf,efh->ech', gate * up, Wd) + buf
        exp_out = buf_out[e_flat, jnp.minimum(pos, CAPACITY - 1)]
        contrib = w_topk.reshape(-1)[:, None] * exp_out * keep[:, None].astype(x.dtype)
        combined = x + contrib.reshape(N, TOP_K, H).sum(axis=1)
        overflow = (~keep).reshape(N, TOP_K).any(axis=1)
        fh = _rms(x, f_norm)
        fout = jax.nn.gelu(fh @ fWg, approximate=False) * (fh @ fWu) @ fWd + x
        out = jnp.where(overflow[:, None], fout, combined)
        return out.reshape(B, S, H)

    def _L1_attn_ref(X, W_q, W_k, W_v, W_o):
        import jax, jax.numpy as jnp
        import numpy as np
        B, T, D, H = (2, 256, 128, 16)
        DH = D // H
        ROPE_BASE = 10000.0

        def _rope(Xh, cos, sin):
            x0 = Xh[..., 0::2]
            x1 = Xh[..., 1::2]
            r0 = cos * x0 - sin * x1
            r1 = sin * x0 + cos * x1
            return jnp.stack((r0, r1), axis=-1).reshape(Xh.shape)
        b, t, d = X.shape
        Q = X @ W_q.T
        K = X @ W_k.T
        V = X @ W_v.T
        Qh = Q.reshape(b, t, H, DH).transpose(0, 2, 1, 3)
        Kh = K.reshape(b, t, H, DH).transpose(0, 2, 1, 3)
        Vh = V.reshape(b, t, H, DH).transpose(0, 2, 1, 3)
        theta = ROPE_BASE ** (-2.0 * jnp.arange(DH // 2, dtype=jnp.float32) / DH)
        pos = jnp.arange(t, dtype=jnp.float32)
        angles = pos[:, None] * theta[None, :]
        cos = jnp.cos(angles).astype(Qh.dtype)
        sin = jnp.sin(angles).astype(Qh.dtype)
        Qr = _rope(Qh, cos, sin)
        Kr = _rope(Kh, cos, sin)
        scores = jnp.einsum('bhqd,bhkd->bhqk', Qr, Kr) * DH ** (-0.5)
        causal = jnp.triu(jnp.ones((t, t), dtype=bool), 1)
        neg = jnp.finfo(scores.dtype).min
        scores = jnp.where(causal[None, None], neg, scores)
        pattern = jax.nn.softmax(scores, axis=-1)
        heads = jnp.einsum('bhqk,bhkd->bhqd', pattern, Vh)
        out = heads.transpose(0, 2, 1, 3).reshape(b, t, d)
        return out @ W_o.T

    def _L1_ffn_ref(x, gate_w, gate_b, sh_w1, sh_b1, sh_w2, sh_b2, ew1, eb1, ew2, eb2):
        import jax, jax.numpy as jnp
        import numpy as np
        TOP_K = 2

        def _mlp(x, w1, b1, w2, b2):
            h = jax.nn.gelu(jnp.einsum('bsd,di->bsi', x, w1) + b1)
            return jnp.einsum('bsi,id->bsd', h, w2) + b2
        E = ew1.shape[0]
        router_probs = jax.nn.softmax(jnp.einsum('bsd,de->bse', x, gate_w) + gate_b, axis=-1)
        expert_values, expert_indices = jax.lax.top_k(router_probs, k=TOP_K)
        expert_values = expert_values / (jnp.sum(expert_values, axis=-1, keepdims=True) + 1e-09)
        h = jax.nn.gelu(jnp.einsum('bsd,edi->bsei', x, ew1) + eb1)
        all_outputs = jnp.einsum('bsei,eid->bsed', h, ew2) + eb2
        one_hot = jax.nn.one_hot(expert_indices, E, dtype=x.dtype)
        weights_E = (one_hot * expert_values[..., None]).sum(axis=2)
        moe_out = jnp.einsum('bse,bsed->bsd', weights_E, all_outputs)
        return x + _mlp(x, sh_w1, sh_b1, sh_w2, sh_b2) + moe_out
    x = L0_attn_x
    x = x + 0.5 * _L0_ffn_ref(_layernorm(x, axis=-1), L0_ffn_Wr, L0_ffn_norm_w, L0_ffn_Wg, L0_ffn_Wu, L0_ffn_Wd, L0_ffn_f_norm, L0_ffn_fWg, L0_ffn_fWu, L0_ffn_fWd)
    x = x + _L0_attn_ref(_layernorm(x, axis=-1), L0_attn_W_q, L0_attn_W_k, L0_attn_W_v, L0_attn_W_o)
    x = x + 0.5 * _L0_ffn_ref(_layernorm(x, axis=-1), L0_ffn_Wr, L0_ffn_norm_w, L0_ffn_Wg, L0_ffn_Wu, L0_ffn_Wd, L0_ffn_f_norm, L0_ffn_fWg, L0_ffn_fWu, L0_ffn_fWd)
    x = x + 0.5 * _L1_ffn_ref(_layernorm(x, axis=-1), L1_ffn_gate_w, L1_ffn_gate_b, L1_ffn_sh_w1, L1_ffn_sh_b1, L1_ffn_sh_w2, L1_ffn_sh_b2, L1_ffn_ew1, L1_ffn_eb1, L1_ffn_ew2, L1_ffn_eb2)
    x = x + _L1_attn_ref(_layernorm(x, axis=-1), L1_attn_W_q, L1_attn_W_k, L1_attn_W_v, L1_attn_W_o)
    x = x + 0.5 * _L1_ffn_ref(_layernorm(x, axis=-1), L1_ffn_gate_w, L1_ffn_gate_b, L1_ffn_sh_w1, L1_ffn_sh_b1, L1_ffn_sh_w2, L1_ffn_sh_b2, L1_ffn_ew1, L1_ffn_eb1, L1_ffn_ew2, L1_ffn_eb2)
    return x

_drawn_inputs = setup_inputs


def setup_inputs(seed=0):
    import zlib

    import numpy as np

    out = dict(_drawn_inputs(seed))
    spreads = {'L0_ffn_norm_w': (1.0, 0.6),
     'L0_ffn_f_norm': (1.0, 0.6),
     'L1_ffn_gate_b': (0.0, 0.411),
     'L1_ffn_sh_b1': (0.0, 0.479),
     'L1_ffn_sh_b2': (0.0, 0.29),
     'L1_ffn_eb1': (0.0, 0.635),
     'L1_ffn_eb2': (0.0, 0.421)}
    factors = {'L0_ffn_Wr': 4.955,
     'L0_ffn_Wg': 8.0,
     'L0_ffn_Wu': 8.0,
     'L0_ffn_Wd': 8.0,
     'L0_ffn_fWg': 8.0,
     'L0_ffn_fWu': 8.0,
     'L0_ffn_fWd': 8.0}
    for name, (base, spread) in spreads.items():
        noise = np.random.default_rng([zlib.crc32(name.encode()), seed]).standard_normal(out[name].shape)
        drawn = base * np.exp(spread * noise) if base else spread * noise
        out[name] = jnp.asarray(drawn.astype(out[name].dtype))
    for name, factor in factors.items():
        out[name] = (out[name] * factor).astype(out[name].dtype)
    return out
```

```python
from contextlib import ExitStack

import concourse.bass as bass
from concourse import mybir

F32 = mybir.dt.float32
F32R = mybir.dt.float32r
BF16 = mybir.dt.bfloat16
ALU = mybir.AluOpType
ACT = mybir.ActivationFunctionType
AX = mybir.AxisListType

P = 128
NB, T = 8, 256
NT = NB * T // P
TOK = NB * T
W512 = 512
NC = TOK // W512
NE = 8
SEQ = NE + 1
CAP = 512
NM = 4
MISC = 8
LN_EPS = 1e-5
RMS_EPS = 1e-6


def normalise(nc, g, tag, mixture):
    x, xr, PS = g["x"], g["xr"], g["PS"]
    with ExitStack() as c:
        def sb(name, shape, dt=F32):
            return c.enter_context(nc.sbuf_tensor(f"{tag}_{name}", shape, dt))

        def sem(name):
            return g["sem"](f"{tag}_{name}")

        st = sb("st", [P, NT, 6])
        mean, diff, m2, var, ms = (sb(n, [P, NT]) for n in ("mean", "diff", "m2", "var", "ms"))
        sd, rstd, rms, rrms, scl = (sb(n, [P, NT]) for n in ("sd", "rstd", "rms", "rrms", "scl"))
        lg, ex, pr, sel, rank = (sb(n, [P, NT, NE]) for n in ("lg", "ex", "pr", "sel", "rank"))
        above, equal = (sb(n, [P, NT, NE, NE]) for n in ("above", "equal"))
        mx, sm, rs = (sb(n, [P, NT]) for n in ("mx", "sm", "rs"))
        tot, tmp = sb("tot", [P, NT, NE]), sb("tmp", [P, NT, NE])
        wfull = sb("wfull", [P, NT, 16])
        whi = sb("whi", [P, NT, 16], F32R)
        wpack = sb("wpack", [P, NT, 32])
        eps_ln, eps_rms = sb("eps_ln", [P, 1]), sb("eps_rms", [P, 1])

        s_eps = sem("s_eps")
        s_var = sem("s_var")
        s_sd = sem("s_sd")
        s_dve = sem("s_dve")
        s_xr = sem("s_xr")
        s_tr = sem("s_tr")
        s_xT = sem("s_xT")
        s_lo = sem("s_lo")
        s_logit = sem("s_logit")
        s_lmax = sem("s_lmax")
        s_ex = sem("s_ex")
        s_sel = sem("s_sel")
        s_cum = sem("s_cum")
        s_wp = sem("s_wp")
        s_wtr = sem("s_wtr")
        s_wT = sem("s_wT")

        block = c.enter_context(nc.Block())

        @block.gpsimd
        def _(pool):
            pool.memset(eps_ln[:], LN_EPS).then_inc(s_eps, 1)
            pool.memset(eps_rms[:], RMS_EPS).then_inc(s_eps, 1)
            if mixture:
                pool.memset(wfull[:], 0.0).then_inc(s_eps, 1)

        @block.vector
        def _(dve):
            n = [0]

            def then(ins):
                n[0] += 1
                ins.then_inc(s_dve, 1)
                dve.wait_ge(s_dve, n[0])

            for t in range(NT - 1):
                dve.bn_stats(st[:, t, :], x[:, t, :])
            then(dve.bn_stats(st[:, NT - 1, :], x[:, NT - 1, :]))
            then(dve.tensor_tensor(mean[:], st[:, :, 1], st[:, :, 4], ALU.add))
            then(dve.tensor_tensor(diff[:], st[:, :, 1], st[:, :, 4], ALU.subtract))
            then(dve.tensor_tensor(m2[:], st[:, :, 2], st[:, :, 5], ALU.add))
            then(dve.tensor_scalar(mean[:], mean[:], 0.5, None, ALU.mult))
            then(dve.tensor_tensor(diff[:], diff[:], diff[:], ALU.mult))
            then(dve.scalar_tensor_tensor(out=m2[:], in0=diff[:], scalar=P / 4.0, in1=m2[:],
                                          op0=ALU.mult, op1=ALU.add))
            dve.tensor_scalar(var[:], m2[:], 1.0 / P, None, ALU.mult).then_inc(s_var, 1)
            dve.wait_ge(s_sd, 1)
            then(dve.reciprocal(rstd[:], sd[:]))
            row_scale = rstd
            if mixture == "A":
                then(dve.tensor_tensor(ms[:], rstd[:], rstd[:], ALU.mult))
                dve.tensor_tensor(ms[:], ms[:], var[:], ALU.mult).then_inc(s_var, 1)
                dve.wait_ge(s_sd, 2)
                then(dve.reciprocal(rrms[:], rms[:]))
                then(dve.tensor_tensor(scl[:], rrms[:], rstd[:], ALU.mult))
                row_scale = scl
            for t in range(NT):
                dve.tensor_scalar(xr[:, t, :], x[:, t, :], mean[:, t:t + 1], row_scale[:, t:t + 1],
                                  ALU.subtract, ALU.mult).then_inc(s_xr, 1)
            for k in range(NC):
                cols = slice(k * W512, (k + 1) * W512)
                dve.wait_ge(s_xT, 2 * (k + 1))
                dve.tensor_tensor(g["xlo"][:, cols], g["xT"][:, cols], g["xhi"][:, cols].bitcast(F32),
                                  ALU.subtract).then_inc(s_lo, 1)
            if not mixture:
                return

            def over(a, k=NE):
                return a.unsqueeze(2).to_broadcast([P, NT, k])

            dve.wait_ge(s_logit, 1)
            logits = PS[:, 4, 0:NT * NE].rearrange("p (t e) -> p t e", e=NE)
            if mixture == "A":
                then(dve.tensor_tensor(lg[:], logits, over(rms[:]), ALU.mult))
            else:
                gb = g["gate_b"][:].unsqueeze(1).to_broadcast([P, NT, NE])
                then(dve.tensor_tensor(lg[:], logits, gb, ALU.add))
            then(dve.tensor_reduce(mx[:], lg[:], AX.X, ALU.max))
            dve.tensor_tensor(lg[:], lg[:], over(mx[:]), ALU.subtract).then_inc(s_lmax, 1)
            dve.wait_ge(s_ex, 1)
            then(dve.tensor_reduce(sm[:], ex[:], AX.X, ALU.add))
            then(dve.reciprocal(rs[:], sm[:]))
            then(dve.tensor_tensor(pr[:], ex[:], over(rs[:]), ALU.mult))
            others = pr[:].unsqueeze(2).to_broadcast([P, NT, NE, NE])
            own = pr[:].unsqueeze(3).to_broadcast([P, NT, NE, NE])
            before = g["before"][:].rearrange("p (e j) -> p e j", j=NE).unsqueeze(1).to_broadcast([P, NT, NE, NE])
            then(dve.tensor_tensor(above[:], others, own, ALU.is_gt))
            then(dve.tensor_tensor(equal[:], others, own, ALU.is_equal))
            then(dve.tensor_tensor(equal[:], equal[:], before, ALU.mult))
            then(dve.tensor_tensor(above[:], above[:], equal[:], ALU.add))
            then(dve.tensor_reduce(rank[:], above[:], AX.X, ALU.add))
            dve.tensor_scalar(sel[:], rank[:], 1.5, None, ALU.is_lt).then_inc(s_sel, 1)
            dve.wait_ge(s_sel, 1)
            then(dve.tensor_tensor(pr[:], pr[:], sel[:], ALU.mult))
            then(dve.tensor_reduce(sm[:], pr[:], AX.X, ALU.add))
            dve.wait_ge(s_eps, 3)
            if mixture == "A":
                dve.wait_ge(s_cum, 2)
                cum = PS[:, 5, 0:NT * NE].rearrange("p (t e) -> p t e", e=NE)
                then(dve.tensor_copy(tot[:], PS[:, 5, NT * NE:2 * NT * NE].rearrange("p (t e) -> p t e", e=NE)))
                then(dve.tensor_tensor(rank[:], cum, tot[:], ALU.subtract))
                a, b = tot, tmp
                step = 1
                while step < NT:
                    then(dve.tensor_copy(b[:, 0:step, :], a[:, 0:step, :]))
                    then(dve.tensor_tensor(b[:, step:, :], a[:, step:, :], a[:, 0:NT - step, :], ALU.add))
                    a, b = b, a
                    step *= 2
                then(dve.tensor_tensor(rank[:], rank[:], a[:], ALU.add))
                then(dve.tensor_scalar(rank[:], rank[:], CAP - 0.5, None, ALU.is_gt))
                then(dve.tensor_tensor(rank[:], rank[:], sel[:], ALU.mult))
                then(dve.tensor_reduce(wfull[:, :, NE], rank[:], AX.X, ALU.max))
                then(dve.tensor_scalar(rs[:], wfull[:, :, NE], -1.0, 1.0, ALU.mult, ALU.add))
                then(dve.tensor_tensor(wfull[:, :, 0:NE], pr[:], over(rs[:]), ALU.mult))
                then(dve.tensor_tensor(sm[:], sm[:], rs[:], ALU.mult))
                then(dve.tensor_scalar(sm[:], sm[:], 1.0, None, ALU.add))
                then(dve.tensor_tensor(g["fscale"][:], sm[:], rms[:], ALU.mult))
            else:
                then(dve.tensor_scalar(sm[:], sm[:], 1e-9, None, ALU.add))
                then(dve.reciprocal(rs[:], sm[:]))
                then(dve.tensor_tensor(wfull[:, :, 1:SEQ], pr[:], over(rs[:]), ALU.mult))
                then(dve.memset(wfull[:, :, 0:1], 1.0))
            then(dve.tensor_copy(whi[:], wfull[:]))
            then(dve.tensor_copy(wpack[:, :, 0:16], whi[:].bitcast(F32)))
            dve.tensor_tensor(wpack[:, :, 16:32], wfull[:], whi[:].bitcast(F32), ALU.subtract).then_inc(s_wp, 1)

        @block.scalar
        def _(act):
            act.wait_ge(s_eps, 2)
            act.wait_ge(s_var, 1)
            act.activation(sd[:], var[:], ACT.Sqrt, bias=eps_ln[:]).then_inc(s_sd, 1)
            if mixture == "A":
                act.wait_ge(s_var, 2)
                act.activation(rms[:], ms[:], ACT.Sqrt, bias=eps_rms[:]).then_inc(s_sd, 1)
            for k in range(NC):
                cols = slice(k * W512, (k + 1) * W512)
                act.wait_ge(s_tr, k + 1)
                act.activation(g["xT"][:, cols], PS[:, k, :], ACT.Copy).then_inc(s_xT, 1)
                act.activation(g["xhi"][:, cols], PS[:, k, :], ACT.Copy).then_inc(s_xT, 1)
            if not mixture:
                return
            act.wait_ge(s_lmax, 1)
            act.activation(ex[:], lg[:], ACT.Exp).then_inc(s_ex, 1)
            for k in range(NC):
                act.wait_ge(s_wtr, k + 1)
                act.activation(g["wT"][:, k * W512:(k + 1) * W512], PS[0:32, k, :], ACT.Copy).then_inc(s_wT, 1)

        @block.tensor
        def _(pe):
            for t in range(NT):
                pe.wait_ge(s_xr, t + 1)
                ins = pe.transpose(PS[:, t // 4, (t % 4) * P:(t % 4 + 1) * P], xr[:, t, :], g["ident"][:])
                if t % 4 == 3:
                    ins.then_inc(s_tr, 1)
            if not mixture:
                return
            for t in range(NT):
                if t % 4 == 0:
                    pe.wait_ge(s_xT, 2 * (t // 4) + 2)
                ins = pe.matmul(PS[:, 4, t * NE:(t + 1) * NE], g["xT"][:, t * P:(t + 1) * P],
                                g["router" + mixture][:], start=True, stop=True)
            ins.then_inc(s_logit, 1)
            if mixture == "A":
                pe.wait_ge(s_sel, 1)
                chosen = sel[:].rearrange("p t e -> p (t e)")
                pe.matmul(PS[:, 5, 0:NT * NE], g["strict"][:], chosen, start=True, stop=True).then_inc(s_cum, 1)
                pe.matmul(PS[:, 5, NT * NE:2 * NT * NE], g["ones"][:], chosen, start=True, stop=True).then_inc(s_cum, 1)
            pe.wait_ge(s_wp, 1)
            for t in range(NT):
                ins = pe.transpose(PS[0:32, t // 4, (t % 4) * P:(t % 4 + 1) * P], wpack[:, t, :], g["ident"][:])
                if t % 4 == 3:
                    ins.then_inc(s_wtr, 1)


def mixture_block(nc, g, tag, kind, weights):
    x, xr, PS = g["x"], g["xr"], g["PS"]
    A = kind == "A"
    NF = 2 if A else 4
    UP = NM * P
    WC = UP + NF * P + MISC
    SLOTS = NC + NC * NM
    ACT_SLOTS = NC + NC * NF
    with ExitStack() as c:
        def sb(name, shape, dt=F32):
            return c.enter_context(nc.sbuf_tensor(f"{tag}_{name}", shape, dt))

        def sem(name):
            return g["sem"](f"{tag}_{name}")

        raw = [sb(f"raw{i}", [P, WC]) for i in range(2)]
        scaled = sb("scaled", [P, UP])
        uphi = [sb(f"uphi{i}", [P, UP], F32R) for i in range(2)]
        uplo = [sb(f"uplo{i}", [P, UP], F32R) for i in range(2)]
        pick = [sb(f"pick{i}", [32, P], F32R) for i in range(2)]
        wrow = [sb(f"wrow{i}", [P, TOK]) for i in range(2)]
        hid = [sb(f"hid{i}", [P, NF, W512]) for i in range(2)]
        gu = sb("gu", [P, NF, W512]) if A else None
        hw = [sb(f"hw{i}", [P, NF, W512]) for i in range(2)]
        accT = sb("accT", [P, TOK])
        fin = sb("fin", [P, 2, P])

        s_raw = [sem(f"s_raw{i}") for i in range(2)]
        s_split = sem("s_split")
        s_ring = sem("s_ring")
        s_actd = sem("s_actd")
        s_upd = sem("s_upd")
        s_hw = sem("s_hw")
        s_down = sem("s_down")
        s_bias = sem("s_bias")
        s_accT = sem("s_accT")
        s_back = sem("s_back")
        s_fin = sem("s_fin")
        SPLIT = 4 if A else 3
        block = c.enter_context(nc.Block())

        @block.sync
        def _(sp):
            def load(n, i):
                sp.dma_start(raw[i][:], weights[bass.ds(n, 1)].rearrange("a p c -> (a p) c")).then_inc(s_raw[i], 16)

            load(0, 0)
            load(1, 1)
            with sp.Fori(2, SEQ - 1, 2) as n:
                sp.wait_ge(s_down, 4 * n - 4)
                load(n, 0)
                sp.wait_ge(s_down, 4 * n)
                load(n + 1, 1)
            sp.wait_ge(s_down, 4 * (SEQ - 2))
            load(SEQ - 1, 0)

        @block.gpsimd
        def _(pool):
            def split(n, i, first):
                at = n * SPLIT
                pool.wait_ge(s_raw[i], 8 * n + (16 if i == 0 else 8))
                if not first:
                    pool.wait_ge(s_ring, (n - 1) * SLOTS)
                pool.tensor_tensor(pick[i][:], g["ones"][0:32, :], raw[i][0:32, WC - 7:WC - 6].to_broadcast([32, P]),
                                   ALU.mult).then_inc(s_split, 1)
                src = raw[i][:, 0:UP]
                if A:
                    norm = raw[i][:, WC - 8:WC - 7].to_broadcast([P, UP])
                    pool.tensor_tensor(uphi[i][:], src, norm, ALU.mult).then_inc(s_split, 1)
                    pool.tensor_tensor(scaled[:], src, norm, ALU.mult).then_inc(s_split, 1)
                    src = scaled[:]
                else:
                    pool.tensor_copy(uphi[i][:], src).then_inc(s_split, 1)
                pool.wait_ge(s_split, at + SPLIT - 1)
                pool.tensor_tensor(uplo[i][:], src, uphi[i][:].bitcast(F32), ALU.subtract).then_inc(s_split, 1)
                if A:
                    pool.wait_ge(s_split, at + SPLIT)

            split(0, 0, True)
            split(1, 1, True)
            with pool.Fori(2, SEQ - 1, 2) as n:
                split(n, 0, False)
                split(n + 1, 1, False)
            split(SEQ - 1, 0, False)

        @block.tensor
        def _(pe):
            def slot_free(n, j, first):
                if first and j < 4:
                    return
                if j < 4:
                    if A:
                        pe.wait_ge(s_actd, (n - 1) * ACT_SLOTS + ACT_SLOTS - (3 - j) // 2)
                        pe.wait_ge(s_upd, (n - 1) * NC * NF + NC * NF - (3 - j + 1) // 2)
                    else:
                        pe.wait_ge(s_actd, (n - 1) * SLOTS + SLOTS - 4 + j + 1)
                    return
                q = j - 4
                if not A:
                    pe.wait_ge(s_actd, n * SLOTS + q + 1)
                elif q < 4:
                    pe.wait_ge(s_actd, n * ACT_SLOTS + q + 1)
                elif q % 2 == 0:
                    pe.wait_ge(s_actd, n * ACT_SLOTS + 4 + (q - 4) // 2 + 1)
                else:
                    pe.wait_ge(s_upd, n * NC * NF + (q - 4) // 2 + 1)

            def rows(n, i, first):
                pe.wait_ge(s_split, n * SPLIT + SPLIT)
                for k in range(NC):
                    slot_free(n, k, first)
                    pe.matmul(PS[:, 4 + k, :], pick[i][:], g["wT"][:, k * W512:(k + 1) * W512],
                              start=True, stop=True).then_inc(s_ring, 1)

            def up(n, i, k, first):
                for m in range(NM):
                    slot_free(n, 4 + 4 * k + m, first)
                    f = (m // 2 + 2 * (m % 2)) if A else m
                    w, cols = slice(f * P, (f + 1) * P), slice(k * W512, (k + 1) * W512)
                    pe.matmul(PS[:, 4 + m, :], uphi[i][:, w], g["xhi"][:, cols], start=True, stop=False)
                    pe.matmul(PS[:, 4 + m, :], uphi[i][:, w], g["xlo"][:, cols], start=False, stop=False)
                    pe.matmul(PS[:, 4 + m, :], uplo[i][:, w], g["xhi"][:, cols],
                              start=False, stop=True).then_inc(s_ring, 1)

            def down(n, i, k, first=False):
                pe.wait_ge(s_hw, 4 * n + k + 1)
                for f in range(NF):
                    ins = pe.matmul(PS[:, k, :], raw[i][:, UP + f * P:UP + (f + 1) * P], hw[k % 2][:, f, :],
                                    start=first and f == 0, stop=False, skip_group_check=True)
                ins.then_inc(s_down, 1)

            def one_pass(n, i, first=False, second=False):
                rows(n, i, first)
                for k in range(NC):
                    up(n, i, k, first)
                    if k:
                        down(n, i, k - 1, first)
                    elif not first:
                        down(n - 1, 1 - i, NC - 1, second)

            one_pass(0, 0, first=True)
            one_pass(1, 1, second=True)
            with pe.Fori(2, SEQ - 1, 2) as n:
                one_pass(n, 0)
                one_pass(n + 1, 1)
            one_pass(SEQ - 1, 0)
            down(SEQ - 1, 0, NC - 1)
            for k in range(NC):
                cols = slice(k * W512, (k + 1) * W512)
                rhs = g["wT"][:, cols].bitcast(F32)
                pe.matmul(PS[:, k, :], g["b2" + kind][:], rhs, start=False, stop=True,
                          skip_group_check=True).then_inc(s_bias, 1)
            for t in range(NT):
                b = 4 + t // 2 % 4
                if t % 4 == 0:
                    pe.wait_ge(s_accT, t // 4 + 1)
                if t % 2 == 0:
                    if t >= 8:
                        pe.wait_ge(s_fin, (t - 8) // 2 * 2 + 2)
                    else:
                        pe.wait_ge(s_accT, 1)
                ins = pe.transpose(PS[:, b, t % 2 * P:(t % 2 + 1) * P], accT[:, t * P:(t + 1) * P], g["ident"][:])
                if t % 2:
                    ins.then_inc(s_back, 1)

        @block.scalar
        def _(act):
            def one_pass(n, i, first=False, second=False):
                if not (first or second):
                    act.wait_ge(s_hw, 4 * n - 4)
                for k in range(NC):
                    act.wait_ge(s_ring, n * SLOTS + k + 1)
                    act.activation(wrow[i][:, k * W512:(k + 1) * W512], PS[:, 4 + k, :], ACT.Copy).then_inc(s_actd, 1)
                for k in range(NC):
                    if not (first and k < 2):
                        act.wait_ge(s_hw, 4 * n + k - 1)
                    for m in range(NF):
                        q = 2 * m if A else m
                        act.wait_ge(s_ring, n * SLOTS + 4 + 4 * k + q + 1)
                        if A:
                            act.activation(hid[k % 2][:, m, :], PS[:, 4 + q, :], ACT.Gelu).then_inc(s_actd, 1)
                        else:
                            act.activation(hid[k % 2][:, m, :], PS[:, 4 + q, :], ACT.Gelu_apprx_tanh,
                                           bias=raw[i][:, WC - 6 + m:WC - 5 + m]).then_inc(s_actd, 1)

            one_pass(0, 0, first=True)
            one_pass(1, 1, second=True)
            with act.Fori(2, SEQ - 1, 2) as n:
                one_pass(n, 0)
                one_pass(n + 1, 1)
            one_pass(SEQ - 1, 0)
            for k in range(NC):
                act.wait_ge(s_bias, k + 1)
                act.activation(accT[:, k * W512:(k + 1) * W512], PS[:, k, :], ACT.Copy).then_inc(s_accT, 1)

        @block.vector
        def _(dve):
            def one_pass(n, i, first=False):
                for k in range(NC):
                    row = wrow[i][:, k * W512:(k + 1) * W512].unsqueeze(1).to_broadcast([P, NF, W512])
                    h = hid[k % 2]
                    if A:
                        for m in range(NF):
                            dve.wait_ge(s_actd, n * ACT_SLOTS + 4 + NF * k + m + 1)
                            dve.wait_ge(s_ring, n * SLOTS + 4 + 4 * k + 2 * m + 2)
                            if m == 0 and not (first and k == 0):
                                dve.wait_ge(s_hw, 4 * n + k)
                            dve.tensor_tensor(gu[:, m, :], h[:, m, :], PS[:, 5 + 2 * m, :], ALU.mult).then_inc(s_upd, 1)
                        dve.wait_ge(s_upd, n * NC * NF + NF * (k + 1))
                        h = gu
                    else:
                        dve.wait_ge(s_actd, n * SLOTS + 4 + NF * (k + 1))
                    if not (first and k < 2):
                        dve.wait_ge(s_down, 4 * n + k - 1)
                    dve.tensor_tensor(hw[k % 2][:], h[:], row, ALU.mult).then_inc(s_hw, 1)

            one_pass(0, 0, first=True)
            one_pass(1, 1)
            with dve.Fori(2, SEQ - 1, 2) as n:
                one_pass(n, 0)
                one_pass(n + 1, 1)
            one_pass(SEQ - 1, 0)
            for t in range(0, NT, 2):
                b = 4 + t // 2 % 4
                dve.wait_ge(s_back, t // 2 + 1)
                if t:
                    dve.wait_ge(s_fin, t)
                for d in range(2):
                    got = PS[:, b, d * P:(d + 1) * P]
                    if A:
                        ins = dve.scalar_tensor_tensor(out=fin[:, d, :], in0=xr[:, t + d, :],
                                                       scalar=g["fscale"][:, t + d:t + d + 1], in1=got,
                                                       op0=ALU.mult, op1=ALU.add)
                    else:
                        ins = dve.tensor_tensor(fin[:, d, :], xr[:, t + d, :], got, ALU.add)
                ins.then_inc(s_fin, 1)
                dve.wait_ge(s_fin, t + 1)
                dve.scalar_tensor_tensor(out=x[:, t:t + 2, :], in0=fin[:], scalar=0.5, in1=x[:, t:t + 2, :],
                                         op0=ALU.mult, op1=ALU.add).then_inc(s_fin, 1)


def hla_block(nc, g, tag, W):
    x, PS = g["x"], g["PS"]
    HP = 8
    UN = 2 * HP
    DK = 64
    BLK = 3 * P
    with ExitStack() as c:
        def sb(name, shape, dt=F32):
            return c.enter_context(nc.sbuf_tensor(f"{tag}_{name}", shape, dt))

        def sem(name):
            return g["sem"](f"{tag}_{name}")

        w = {n: sb("w" + n, [P, HP * P]) for n in "qkv"}
        whi = {n: sb("whi" + n, [P, HP * P], F32R) for n in "qkv"}
        wlo = {n: sb("wlo" + n, [P, HP * P], F32R) for n in "qkv"}
        wo = sb("wo", [P, HP, P])
        xbhi, xblo = sb("xbhi", [P, W512], F32R), sb("xblo", [P, W512], F32R)
        V = sb("V", [P, 4, HP * P])
        qT = [sb(f"qT{i}", [P, W512]) for i in range(2)]
        kT = [sb(f"kT{i}", [P, W512]) for i in range(2)]
        Am = [sb(f"Am{i}", [P, 2, BLK]) for i in range(2)]
        Wm = [sb(f"Wm{i}", [P, 2, BLK]) for i in range(2)]
        OT = sb("OT", [P, HP, W512])

        s_w = sem("s_w")
        s_whi = sem("s_whi")
        s_wlo = sem("s_wlo")
        s_xb = sem("s_xb")
        s_proj = sem("s_proj")
        s_evac = sem("s_evac")
        s_A = sem("s_A")
        s_Am = sem("s_Am")
        s_W = sem("s_W")
        s_Wm = sem("s_Wm")
        s_O = sem("s_O")
        s_OT = sem("s_OT")
        s_res = sem("s_res")
        block = c.enter_context(nc.Block())

        @block.sync
        def _(sp):
            for n in "qkv":
                sp.dma_start(w[n][:], W[n]).then_inc(s_w, 16)
            sp.dma_start(wo[:], W["o"]).then_inc(s_w, 16)

        @block.scalar
        def _(act):
            act.wait_ge(s_w, 64)
            for n in "qkv":
                act.activation(whi[n][:], w[n][:], ACT.Copy).then_inc(s_whi, 1)
            with act.Fori(0, NC) as it:
                def copy(dst, j, bank):
                    act.wait_ge(s_proj, 26 * it + j + 1)
                    act.activation(dst, PS[:, bank, :], ACT.Copy).then_inc(s_evac, 1)

                def copy_qk(h):
                    j = 0 if h == 0 else 8 + 2 * h
                    if h >= 2:
                        act.wait_ge(s_A, 32 * it + 4 * (h - 1))
                    copy(qT[h % 2][:], j, 0)
                    copy(kT[h % 2][:], j + 1, 1)

                def copy_o(h):
                    act.wait_ge(s_O, UN * it + 2 * h + 2)
                    act.activation(OT[:, h, :], PS[:, 6 + h % 2, :], ACT.Copy).then_inc(s_OT, 1)

                copy_qk(0)
                for j in range(8):
                    copy(V[:, j // 2, j % 2 * W512:(j % 2 + 1) * W512], 2 + j, j % 2)
                copy_qk(1)
                for h in range(HP):
                    if h + 2 < HP:
                        copy_qk(h + 2)
                    copy_o(h)

        @block.vector
        def _(dve):
            dve.wait_ge(s_w, 64)
            for i, n in enumerate("qkv"):
                dve.wait_ge(s_whi, i + 1)
                dve.tensor_tensor(wlo[n][:], w[n][:], whi[n][:].bitcast(F32), ALU.subtract).then_inc(s_wlo, 1)
            with dve.Fori(0, NC) as it:
                dve.tensor_copy(xbhi[:], g["xhi"][:, bass.ds(it * W512, W512)]).then_inc(s_xb, 1)
                dve.tensor_copy(xblo[:], g["xlo"][:, bass.ds(it * W512, W512)]).then_inc(s_xb, 1)

                def mask(u, full, done, dst, bank, used):
                    for h in range(2):
                        n = 32 * it + 2 * u + h
                        dve.wait_ge(full, n + 1)
                        if used is not None:
                            dve.wait_ge(*used(h))
                        dve.tensor_tensor(dst[u % 2][:, h, :], PS[:, bank + h, 0:BLK], g["tri"][:],
                                          ALU.mult).then_inc(done, 1)

                def mask_a(u):
                    mask(u, s_A, s_Am, Am, 2, (lambda h: (s_W, 32 * it + 2 * u - 4 + h + 1)) if u >= 2 else None)

                def mask_w(u):
                    mask(u, s_W, s_Wm, Wm, 4, (lambda h: (s_O, UN * it + u - 1)) if u >= 2 else None)

                mask_a(0)
                for u in range(UN):
                    if u + 1 < UN:
                        mask_a(u + 1)
                    mask_w(u)
                for j in range(2):
                    dve.wait_ge(s_proj, 26 * it + 24 + j + 1)
                    rows = x[:, bass.ds(it * 4 + 2 * j, 2), :]
                    dve.tensor_tensor(rows, rows, PS[:, j, 0:2 * P].rearrange("p (t d) -> p t d", t=2),
                                      ALU.add).then_inc(s_res, 1)

        @block.tensor
        def _(pe):
            def proj(bank, lo, lhs, rhs):
                (lh, ll), (rh, rl) = lhs, rhs
                pe.matmul(PS[:, bank, :], lh, rh, start=True, stop=False)
                pe.matmul(PS[:, bank, :], lh, rl, start=False, stop=False)
                pe.matmul(PS[:, bank, :], ll, rh, start=False, stop=True).then_inc(s_proj, 1)

            pe.wait_ge(s_wlo, 3)
            with pe.Fori(0, NC) as it:
                turn = bass.ds(it * W512, W512)

                def proj_qk(h):
                    j = 0 if h == 0 else 8 + 2 * h
                    for i, n in enumerate("qk"):
                        if j + i >= 2:
                            pe.wait_ge(s_evac, 24 * it + j + i - 1)
                        cols = slice(h * P, (h + 1) * P)
                        proj(i, None, (whi[n][:, cols], wlo[n][:, cols]), (g["xhi"][:, turn], g["xlo"][:, turn]))

                def proj_v(j):
                    rows, cols = slice(j // 2 * P, (j // 2 + 1) * P), slice(j % 2 * W512, (j % 2 + 1) * W512)
                    pe.wait_ge(s_evac, 24 * it + j + 1)
                    proj(j % 2, None, (xbhi[:, rows], xblo[:, rows]), (whi["v"][:, cols], wlo["v"][:, cols]))

                def scores(u):
                    h, b = divmod(u, 2)
                    pe.wait_ge(s_evac, 24 * it + (2 if h == 0 else 10 + 2 * h))
                    for i in range(2):
                        if u:
                            pe.wait_ge(s_Am, 32 * it + 2 * u - 2 + i + 1)
                        d, at = slice(i * DK, (i + 1) * DK), b * T
                        k, q = kT[h % 2][d, :], qT[h % 2][d, :]
                        pe.matmul(PS[:, 2 + i, 0:T], k[:, at:at + P], q[:, at:at + T], start=True, stop=True)
                        pe.matmul(PS[:, 2 + i, T:BLK], k[:, at + P:at + T], q[:, at + P:at + T],
                                  start=True, stop=True).then_inc(s_A, 1)

                def square(u):
                    for i in range(2):
                        pe.wait_ge(s_Am, 32 * it + 2 * u + i + 1)
                        if u:
                            pe.wait_ge(s_Wm, 32 * it + 2 * u - 2 + i + 1)
                        a = Am[u % 2][:, i, :]
                        pe.matmul(PS[:, 4 + i, 0:T], a[:, 0:P], a[:, 0:T], start=True, stop=True)
                        pe.matmul(PS[:, 4 + i, T:BLK], a[:, P:T], a[:, P:T], start=True, stop=False)
                        pe.matmul(PS[:, 4 + i, T:BLK], a[:, T:BLK], a[:, T:BLK],
                                  start=False, stop=True).then_inc(s_W, 1)

                def output(u):
                    h, b = divmod(u, 2)
                    if u == 0:
                        pe.wait_ge(s_evac, 24 * it + 10)
                    if b == 0 and h >= 2:
                        pe.wait_ge(s_OT, HP * it + h - 1)
                    pe.wait_ge(s_Wm, 32 * it + 2 * u + 2)
                    bank, at = PS[:, 6 + h % 2, :], b * T
                    for j in range(2):
                        for i in range(2):
                            d = slice(i * DK, (i + 1) * DK)
                            v = V[:, 2 * b + j, (2 * h + i) * DK:(2 * h + i + 1) * DK]
                            wm = Wm[u % 2][:, i, :]
                            src = wm[:, 0:T] if j == 0 else wm[:, T:BLK]
                            ins = pe.matmul(bank[d, at + j * P:at + T], v, src, start=(b == 0 and j == 0),
                                            stop=(b == 1 and j == 1), skip_group_check=True)
                    ins.then_inc(s_O, 1)

                pe.wait_ge(s_xb, 2 * it + 2)
                proj_qk(0)
                for j in range(8):
                    proj_v(j)
                scores(0)
                for u in range(UN):
                    if u % 2 == 0 and u // 2 + 1 < HP:
                        proj_qk(u // 2 + 1)
                    if u + 1 < UN:
                        scores(u + 1)
                    square(u)
                    if u:
                        output(u - 1)
                output(UN - 1)
                pe.wait_ge(s_OT, HP * it + HP)
                for j in range(2):
                    for t in range(2):
                        for h in range(HP):
                            rows = slice((2 * j + t) * P, (2 * j + t + 1) * P)
                            ins = pe.matmul(PS[:, j, t * P:(t + 1) * P], OT[:, h, rows], wo[:, h, :],
                                            start=(h == 0), stop=(h == HP - 1))
                    ins.then_inc(s_proj, 1)


def attention_block(nc, g, tag, W, cst):
    x, PS = g["x"], g["PS"]
    G, J = 4, 4
    H, DH = 16, 8
    SCALE = DH ** -0.5
    BLK = 3 * P
    with ExitStack() as c:
        def sb(name, shape, dt=F32):
            return c.enter_context(nc.sbuf_tensor(f"{tag}_{name}", shape, dt))

        def sem(name):
            return g["sem"](f"{tag}_{name}")

        w = sb("w", [P, 4, P])
        wrot = sb("wrot", [P, 2, P])
        cs = sb("cs", [P, 2 * T])
        spread = sb("spread", [P, 4, G, P])
        spreadr = sb("spreadr", [P, 4, G, P], F32R)
        unit = sb("unit", [P, H, P])
        unitr = sb("unitr", [P, H, P], F32R)
        maskf = sb("maskf", [P, 2, W512])
        maskb = sb("maskb", [P, 3, W512], BF16)
        identb = sb("identb", [P, P], BF16)
        xb = [sb(f"xb{i}", [P, T]) for i in range(2)]
        tq = sb("tq", [P, 2, 2 * T])
        qk = sb("qk", [P, 2, T])
        qkhi, qklo = sb("qkhi", [P, 2, T], F32R), sb("qklo", [P, 2, T], F32R)
        S = [sb(f"S{i}", [P, 2, G, T], F32R) for i in range(2)]
        V = [sb(f"V{i}", [P, 2, H, 32]) for i in range(2)]
        nmax = sb("nmax", [P, 2, H])
        nhi = sb("nhi", [P, 2, H], F32R)
        mp = sb("mp", [P, 2, 32])
        mT = [sb(f"mT{i}", [P, BLK], F32R) for i in range(2)]
        PT = sb("PT", [P, G, J, BLK])
        OT = sb("OT", [P, G, T])
        rden = sb("rden", [P, 2, H])
        at = sb("at", [P, 2, P])
        atT = sb("atT", [P, 2, P])

        s_w = sem("s_w")
        s_set = sem("s_set")
        s_setp = sem("s_setp")
        s_xb = sem("s_xb")
        s_proj = sem("s_proj")
        s_v = sem("s_v")
        s_rot = sem("s_rot")
        s_hi = sem("s_hi")
        s_spread = sem("s_spread")
        s_S = sem("s_S")
        s_s1 = sem("s_s1")
        s_mx = sem("s_mx")
        s_mp = sem("s_mp")
        s_mtr = sem("s_mtr")
        s_mT = sem("s_mT")
        s_s2 = sem("s_s2")
        s_p = sem("s_p")
        s_pv = sem("s_pv")
        s_ot = sem("s_ot")
        s_otr = sem("s_otr")
        s_at = sem("s_at")
        s_atr = sem("s_atr")
        s_atT = sem("s_atT")
        s_o = sem("s_o")
        s_res = sem("s_res")
        block = c.enter_context(nc.Block())

        @block.sync
        def _(sp):
            for dst, src in ((w, W), (cs, cst["cs"]), (spread, cst["spread"]), (unit, cst["unit"]), (maskf, cst["mask"])):
                sp.dma_start(dst[:], src).then_inc(s_w, 16)

        @block.gpsimd
        def _(pool):
            for i in range(2):
                pool.memset(V[i][:], 0.0).then_inc(s_setp, 1)
            for i in range(2):
                pool.memset(mT[i][:].bitcast(F32), 0.0).then_inc(s_setp, 1)

        @block.scalar
        def _(act):
            act.wait_ge(s_setp, 4)
            act.wait_ge(s_set, 8)
            with act.Fori(0, NB // 2) as turn:
                it = 2 * turn
                def front(i):
                    n = it + i
                    act.wait_ge(s_proj, 2 * n + 2)
                    act.activation(V[i][:, :, :, 0:DH], PS[:, 2, 0:T].rearrange("p (t h d) -> p t h d", t=2, d=DH),
                                   ACT.Copy).then_inc(s_v, 1)
                    act.wait_ge(s_rot, 3 * n + 2)
                    act.activation(qkhi[:], qk[:], ACT.Copy).then_inc(s_hi, 1)
                    for b in range(4):
                        act.wait_ge(s_spread, 4 * n + b + 1)
                        act.activation(S[i][:, b // 2, b % 2 * 2:b % 2 * 2 + 2, :],
                                       PS[:, b, :].rearrange("p (g t) -> p g t", g=2), ACT.Copy).then_inc(s_S, 1)
                    act.wait_ge(s_mtr, n + 1)
                    act.activation(mT[i][0:32, 0:T], PS[0:32, 6, 0:T], ACT.Copy).then_inc(s_mT, 1)
                    act.activation(mT[i][0:32, T:BLK], PS[0:32, 6, P:T], ACT.Copy).then_inc(s_mT, 1)

                def back(i):
                    n = it + i
                    for b in range(8):
                        act.wait_ge(s_s2, 8 * n + b + 1)
                        if i:
                            act.wait_ge(s_pv, 4 * n - 3 + b // 2)
                        gq, j = b // 2, b % 2 * 2
                        act.activation(PT[:, gq, j:j + 2, :], PS[:, b % 2 * 2:b % 2 * 2 + 2, 0:BLK], ACT.Exp,
                                       scale=SCALE).then_inc(s_p, 1)
                    act.wait_ge(s_atr, n + 1)
                    act.activation(atT[:], PS[:, 6, 0:T].rearrange("p (t q) -> p t q", t=2), ACT.Copy).then_inc(s_atT, 1)

                front(0)
                front(1)
                back(0)
                back(1)

        @block.vector
        def _(dve):
            dve.wait_ge(s_w, 80)
            dve.wait_ge(s_setp, 4)
            for i in range(2):
                pair = w[:, i, :].rearrange("p (h two) -> p h two", two=2)
                rot = wrot[:, i, :].rearrange("p (h two) -> p h two", two=2)
                dve.tensor_scalar(rot[:, :, 0], pair[:, :, 1], -1.0, None, ALU.mult)
                dve.tensor_copy(rot[:, :, 1], pair[:, :, 0]).then_inc(s_set, 1)
            dve.tensor_copy(spreadr[:], spread[:]).then_inc(s_set, 1)
            dve.tensor_copy(unitr[:], unit[:]).then_inc(s_set, 1)
            dve.tensor_copy(maskb[:, 0:2, :], maskf[:]).then_inc(s_set, 1)
            dve.tensor_copy(identb[:], g["ident"][:]).then_inc(s_set, 1)
            for i in range(2):
                dve.memset(V[i][:, :, :, DH:DH + 1], 1.0).then_inc(s_set, 1)
            with dve.Fori(0, NB // 2) as turn:
                it = 2 * turn
                def front(i):
                    n = it + i
                    dve.tensor_copy(xb[i][:], g["xT"][:, bass.ds(n * T, T)]).then_inc(s_xb, 1)
                    dve.wait_ge(s_proj, 2 * n + 1)
                    both = cs[:].unsqueeze(1).to_broadcast([P, 2, 2 * T])
                    dve.tensor_tensor(tq[:], PS[:, 0:2, :], both, ALU.mult).then_inc(s_rot, 1)
                    dve.wait_ge(s_rot, 3 * n + 1)
                    dve.tensor_tensor(qk[:], tq[:, :, 0:T], tq[:, :, T:2 * T], ALU.add).then_inc(s_rot, 1)
                    dve.wait_ge(s_hi, n + 1)
                    dve.tensor_tensor(qklo[:], qk[:], qkhi[:].bitcast(F32), ALU.subtract).then_inc(s_rot, 1)
                    for b in range(16):
                        qt, a, j = b % 2, b // 8, b // 2 % 4
                        dve.wait_ge(s_s1, 16 * n + b + 1)
                        K = P * (qt + 1)
                        src = PS[:, 4 + b % 4, :].rearrange("p (g k) -> p g k", g=2)[:, :, 0:K]
                        dst = nmax[:, qt, :].rearrange("p (g j) -> p g j", j=J)[:, 2 * a:2 * a + 2, j]
                        dve.tensor_reduce(dst, src, AX.X, ALU.max, negate=True).then_inc(s_mx, 1)
                    dve.wait_ge(s_mx, 16 * n + 16)
                    dve.tensor_copy(nhi[:], nmax[:]).then_inc(s_mp, 1)
                    dve.wait_ge(s_mp, 3 * n + 1)
                    if i:
                        dve.wait_ge(s_mtr, n)
                    dve.tensor_copy(mp[:, :, 0:H], nhi[:].bitcast(F32)).then_inc(s_mp, 1)
                    dve.tensor_tensor(mp[:, :, H:2 * H], nmax[:], nhi[:].bitcast(F32), ALU.subtract).then_inc(s_mp, 1)

                def back(i):
                    n = it + i
                    for b in range(2):
                        dve.wait_ge(s_pv, 4 * n + 2 * b + 2)
                        dve.tensor_copy(OT[:, 2 * b:2 * b + 2, :],
                                        PS[:, 4 + b, :].rearrange("p (g t) -> p g t", g=2)).then_inc(s_ot, 1)
                    for qt in range(2):
                        dve.wait_ge(s_otr, 2 * n + qt + 1)
                        got = PS[:, 4 + qt, :].rearrange("p (h d) -> p h d", d=32)
                        dve.reciprocal(rden[:, qt, :], got[:, :, DH]).then_inc(s_at, 1)
                        dve.wait_ge(s_at, 4 * n + 2 * qt + 1)
                        dve.tensor_tensor(at[:, qt, :].rearrange("p (h d) -> p h d", d=DH), got[:, :, 0:DH],
                                          rden[:, qt, :].unsqueeze(2).to_broadcast([P, H, DH]),
                                          ALU.mult).then_inc(s_at, 1)
                    dve.wait_ge(s_o, n + 1)
                    rows = x[:, bass.ds(2 * n, 2), :]
                    dve.tensor_tensor(rows, rows, PS[:, 7, 0:T].rearrange("p (t d) -> p t d", t=2),
                                      ALU.add).then_inc(s_res, 1)

                front(0)
                front(1)
                back(0)
                back(1)

        @block.tensor
        def _(pe):
            pe.wait_ge(s_set, 8)
            pe.wait_ge(s_setp, 4)
            with pe.Fori(0, NB // 2) as turn:
                it = 2 * turn
                def front(i):
                    n = it + i
                    cols = bass.ds(n * T, T)
                    if i:
                        pe.wait_ge(s_S, 4 * n)
                    for m in range(2):
                        pe.matmul(PS[:, m, 0:T], w[:, m, :], g["xT"][:, cols], start=True, stop=True)
                        ins = pe.matmul(PS[:, m, T:2 * T], wrot[:, m, :], g["xT"][:, cols], start=True, stop=True)
                    ins.then_inc(s_proj, 1)
                    pe.wait_ge(s_xb, n + 1)
                    for t in range(2):
                        ins = pe.matmul(PS[:, 2, t * P:(t + 1) * P], xb[i][:, t * P:(t + 1) * P], w[:, 2, :],
                                        start=True, stop=True)
                    ins.then_inc(s_proj, 1)
                    pe.wait_ge(s_rot, 3 * n + 3)
                    pe.wait_ge(s_v, n + 1)
                    for b in range(4):
                        for e in range(2):
                            m, gr = b // 2, b % 2 * 2 + e
                            dst = PS[:, b, e * T:(e + 1) * T]
                            pe.matmul(dst, spreadr[:, 2 * m, gr, :], qkhi[:, m, :], start=True, stop=False)
                            ins = pe.matmul(dst, spreadr[:, 2 * m + 1, gr, :], qklo[:, m, :], start=False, stop=True)
                        ins.then_inc(s_spread, 1)
                    pe.wait_ge(s_S, 4 * n + 4)
                    for b in range(16):
                        qt, a, j = b % 2, b // 8, b // 2 % 4
                        if b >= 4:
                            pe.wait_ge(s_mx, 16 * n + b - 3)
                        elif i:
                            pe.wait_ge(s_mT, 2 * n)
                        bank, r = 4 + b % 4, slice(32 * j, 32 * j + 32)
                        pe.matmul(PS[:, bank, :], identb[:], maskb[:, qt, :], start=True, stop=False, skip_group_check=True)
                        for e in range(2):
                            gr = 2 * a + e
                            ins = pe.matmul(PS[:, bank, e * T:(e + 1) * T], S[i][r, 0, gr, qt * P:(qt + 1) * P],
                                            S[i][r, 1, gr, :], start=False, stop=True, skip_group_check=True)
                        ins.then_inc(s_s1, 1)
                    pe.wait_ge(s_mp, 3 * n + 3)
                    for t in range(2):
                        ins = pe.transpose(PS[0:32, 6, t * P:(t + 1) * P], mp[:, t, :], g["ident"][:])
                    ins.then_inc(s_mtr, 1)

                def back(i):
                    n = it + i
                    pe.wait_ge(s_mT, 2 * n + 2)

                    def scores(b):
                        gr = b // 2
                        if b >= 2:
                            pe.wait_ge(s_p, 8 * n + b - 1)
                        for e in range(2):
                            j = b % 2 * 2 + e
                            pe.matmul(PS[:, j, 0:BLK], identb[:], g["maskT"][:], start=True, stop=False,
                                      skip_group_check=True)
                            pe.matmul(PS[:, j, 0:BLK], unitr[:, 4 * gr + j, :], mT[i][:], start=False, stop=False,
                                      skip_group_check=True)
                        for e in range(2):
                            j = b % 2 * 2 + e
                            r = slice(32 * j, 32 * j + 32)
                            pe.matmul(PS[:, j, 0:T], S[i][r, 1, gr, 0:P], S[i][r, 0, gr, :],
                                      start=False, stop=True, skip_group_check=True)
                            ins = pe.matmul(PS[:, j, T:BLK], S[i][r, 1, gr, P:T], S[i][r, 0, gr, P:T],
                                            start=False, stop=True, skip_group_check=True)
                        ins.then_inc(s_s2, 1)

                    def values(gr):
                        pe.wait_ge(s_p, 8 * n + 2 * gr + 2)
                        if gr % 2 == 0:
                            if i:
                                pe.wait_ge(s_at, 4 * n)
                        for k in range(2):
                            for j in range(J):
                                dst = PS[32 * j:32 * j + 32, 4 + gr // 2, gr % 2 * T + k * P:(gr % 2 + 1) * T]
                                src = PT[:, gr, j, 0:T] if k == 0 else PT[:, gr, j, T:BLK]
                                ins = pe.matmul(dst, V[i][:, k, 4 * gr + j, :], src, start=(gr % 2 == 0 and k == 0),
                                                stop=(k == 1), skip_group_check=True)
                        ins.then_inc(s_pv, 1)

                    scores(0)
                    scores(1)
                    for gr in range(G):
                        if gr + 1 < G:
                            scores(2 * gr + 2)
                            scores(2 * gr + 3)
                        values(gr)
                    pe.wait_ge(s_ot, 2 * n + 2)
                    for t in range(2):
                        for gr in range(G):
                            ins = pe.transpose(PS[:, 4 + t, gr * P:(gr + 1) * P], OT[:, gr, t * P:(t + 1) * P],
                                               g["ident"][:])
                        ins.then_inc(s_otr, 1)
                    pe.wait_ge(s_at, 4 * n + 4)
                    for t in range(2):
                        ins = pe.transpose(PS[:, 6, t * P:(t + 1) * P], at[:, t, :], g["ident"][:])
                    ins.then_inc(s_atr, 1)
                    pe.wait_ge(s_atT, n + 1)
                    if i:
                        pe.wait_ge(s_res, n)
                    for t in range(2):
                        ins = pe.matmul(PS[:, 7, t * P:(t + 1) * P], atT[:, t, :], w[:, 3, :], start=True, stop=True)
                    ins.then_inc(s_o, 1)

                front(0)
                front(1)
                back(0)
                back(1)


def macaron(nc, a, out, stages=6):
    with ExitStack() as ctx:
        def sb(name, shape, dt=F32):
            return ctx.enter_context(nc.sbuf_tensor(name, shape, dt))

        g = {
            "x": sb("x", [P, NT, P]), "xr": sb("xr", [P, NT, P]), "xT": sb("xT", [P, TOK]),
            "xhi": sb("xhi", [P, TOK], F32R), "xlo": sb("xlo", [P, TOK], F32R),
            "wT": sb("wT", [32, TOK], F32R), "fscale": sb("fscale", [P, NT]),
            "PS": ctx.enter_context(nc.psum_tensor("PS", [P, 8, W512], F32)),
            "maskT": sb("maskT", [P, 3 * P], BF16),
        }
        maskTf = sb("maskTf", [P, 3 * P])
        small = {"ident": [P, P], "strict": [P, P], "ones": [P, P], "tri": [P, 3 * P], "before": [P, NE * NE],
                 "gate_b": [P, NE], "routerA": [P, NE], "routerB": [P, NE], "b2A": [32, P], "b2B": [32, P]}
        for name, shape in small.items():
            g[name] = sb(name, shape)
        s_in = ctx.enter_context(nc.semaphore("s_in"))
        s_mask = ctx.enter_context(nc.semaphore("s_mask"))
        s_out = ctx.enter_context(nc.semaphore("s_out"))
        tokens = "(t p) d -> p t d"
        held = []

        def sem(name):
            held.append(nc.alloc_semaphore(name))
            return held[-1]

        g["sem"] = sem

        with nc.Block() as block:
            @block.sync
            def _(sp):
                sp.dma_start(g["x"][:], a["x"].rearrange(tokens, p=P)).then_inc(s_in, 16)
                for name in small:
                    sp.dma_start(g[name][:], a[name]).then_inc(s_in, 16)
                sp.dma_start(maskTf[:], a["maskT"]).then_inc(s_in, 16)
                sp.wait_ge(s_in, 16 * (len(small) + 2))

            @block.vector
            def _(dve):
                dve.wait_ge(s_in, 16 * (len(small) + 2))
                dve.tensor_copy(g["maskT"][:], maskTf[:]).then_inc(s_mask, 1)
                dve.wait_ge(s_mask, 1)

        def mixture(kind, tag):
            normalise(nc, g, tag + "n", kind)
            mixture_block(nc, g, tag, kind, a["mix" + kind])

        def hla():
            normalise(nc, g, "hn", None)
            hla_block(nc, g, "h", {n: a["hla_w" + n] for n in "qkvo"})

        def attention():
            normalise(nc, g, "an", None)
            attention_block(nc, g, "a", a["att_w"], {"cs": a["cs"], "spread": a["spread"], "unit": a["unit"], "mask": a["mask"]})

        order = [lambda: mixture("A", "m1"), hla, lambda: mixture("A", "m2"), lambda: mixture("B", "m3"),
                 attention, lambda: mixture("B", "m4")]
        if isinstance(stages, int):
            stages = range(stages)
        for s in stages:
            if s == 3:
                nc.clear_and_free_semaphores(held)
                held.clear()
                nc.all_engine_barrier()
            order[s]()
        with nc.Block() as block:
            @block.sync
            def _(sp):
                sp.dma_start(out.rearrange(tokens, p=P), g["x"][:]).then_inc(s_out, 16)
                sp.wait_ge(s_out, 16)


def _constants():
    import numpy as np
    i = np.arange(P)
    f = np.float32
    H, DH = 16, 8
    le = (i[:, None] <= i[None, :]).astype(f)
    one = np.ones((P, P), f)
    off = f(-1e30)
    later = np.where(i[:, None] < i[None, :], off, f(0))
    laterT = later.T.copy()
    zero = np.zeros((P, P), f)
    j = np.arange(NE)
    c = {
        "ident": np.eye(P, dtype=f), "strict": (i[:, None] < i[None, :]).astype(f), "ones": one,
        "tri": np.concatenate([le, one, le], 1),
        "before": np.tile((j[None, :] < j[:, None]).astype(f).reshape(1, -1), (P, 1)),
        "maskT": np.concatenate([laterT, zero, laterT], 1),
        "mask": np.stack([np.tile(np.concatenate([later, zero], 1), (1, 2)),
                          np.tile(np.concatenate([zero, later], 1), (1, 2))], 1),
    }
    theta = (10000.0 ** (-2.0 * np.arange(DH // 2, dtype=f) / DH)).astype(f)
    angles = (np.arange(T, dtype=f)[:, None] * theta[None, :]).astype(f)
    per_row = angles[:, (i % DH) // 2].T
    c["cs"] = np.concatenate([np.cos(per_row), np.sin(per_row)], 1).astype(f)
    spread = np.zeros((P, 4, 4, P), f)
    for part, terms in enumerate(((0, 1), (2, 3), (0, 2), (1, 3))):
        for gr in range(4):
            for jj in range(4):
                for term in terms:
                    for d in range(DH):
                        spread[(4 * gr + jj) * DH + d, part, gr, 32 * jj + 8 * term + d] = 1
    c["spread"] = spread
    unit = np.zeros((P, H, P), f)
    for h in range(H):
        unit[h, h] = 1
        unit[H + h, h] = 1
    c["unit"] = unit
    return c


def _layout(inputs):
    import numpy as np
    v = {k: np.asarray(z) for k, z in inputs.items()}
    f = np.float32
    a = _constants()
    a["x"] = v["L0_attn_x"].reshape(TOK, P)
    a["gate_b"] = np.repeat(v["L1_ffn_gate_b"][None], P, 0)
    a["routerA"], a["routerB"] = v["L0_ffn_Wr"], v["L1_ffn_gate_w"]
    chosen = np.zeros((SEQ, P, 1), f)
    for n in range(SEQ):
        chosen[n, n] = chosen[n, 16 + n] = 1
    FA = v["L0_ffn_Wg"].shape[2]
    mixA = np.zeros((SEQ, P, 4 * P + FA + MISC), f)
    mixA[:NE, :, 0:FA] = v["L0_ffn_Wg"]
    mixA[:NE, :, FA:2 * FA] = v["L0_ffn_Wu"]
    mixA[:NE, :, 4 * P:4 * P + FA] = v["L0_ffn_Wd"].reshape(NE, 2, P, P).transpose(0, 2, 1, 3).reshape(NE, P, FA)
    mixA[:NE, :, -8] = v["L0_ffn_norm_w"]
    F4 = v["L0_ffn_fWg"].shape[1]
    mixA[NE, :, 0:F4] = v["L0_ffn_fWg"]
    mixA[NE, :, FA:FA + F4] = v["L0_ffn_fWu"]
    mixA[NE, 0:F4, 4 * P:5 * P] = v["L0_ffn_fWd"]
    mixA[NE, :, -8] = v["L0_ffn_f_norm"]
    mixA[:, :, -7:-6] = chosen
    a["mixA"] = mixA
    w1 = np.concatenate([v["L1_ffn_sh_w1"][None], v["L1_ffn_ew1"]], 0)
    w2 = np.concatenate([v["L1_ffn_sh_w2"][None], v["L1_ffn_ew2"]], 0)
    b1 = np.concatenate([v["L1_ffn_sh_b1"][None], v["L1_ffn_eb1"]], 0)
    b2 = np.concatenate([v["L1_ffn_sh_b2"][None], v["L1_ffn_eb2"]], 0)
    mixB = np.zeros((SEQ, P, 8 * P + MISC), f)
    mixB[:, :, 0:4 * P] = w1
    mixB[:, :, 4 * P:8 * P] = w2.reshape(SEQ, 4, P, P).transpose(0, 2, 1, 3).reshape(SEQ, P, 4 * P)
    mixB[:, :, -6:-2] = b1.reshape(SEQ, 4, P).transpose(0, 2, 1)
    mixB[:, :, -7:-6] = chosen
    a["mixB"] = mixB
    a["b2A"] = np.zeros((32, P), f)
    b2B = np.zeros((32, P), f)
    b2B[0:SEQ] = b2
    b2B[16:16 + SEQ] = b2
    a["b2B"] = b2B
    for n in "qkv":
        a["hla_w" + n] = v["L0_attn_W_" + n]
    a["hla_wo"] = v["L0_attn_W_o"].reshape(8, P, P).transpose(1, 0, 2)
    a["att_w"] = np.stack([v["L1_attn_W_" + n].T for n in "qkvo"], 1)
    return {k: np.ascontiguousarray(z) for k, z in a.items()}


def kernel(**inputs):
    import numpy as _np
    import concourse.bacc as _bacc
    from concourse import mybir as _mybir
    from concourse.bass_utils import run_bass_kernel_spmd as _run

    nc = _bacc.Bacc("TRN2", target_bir_lowering=False, num_devices=1)
    arrays = {f"in_{k}": z for k, z in _layout(inputs).items()}
    args = {k[3:]: nc.dram_tensor(k, z.shape, _mybir.dt.from_np(z.dtype), kind="ExternalInput").ap()
            for k, z in arrays.items()}
    out = nc.dram_tensor("out", (TOK, P), _mybir.dt.float32, kind="ExternalOutput").ap()
    macaron(nc, args, out)
    r = _run(nc, [arrays], core_ids=[0])
    return r.results[0]["out"].reshape(NB, T, P)
```

```python
from contextlib import ExitStack

import concourse.bass as bass
from concourse import mybir

F32 = mybir.dt.float32
F32R = mybir.dt.float32r
BF16 = mybir.dt.bfloat16
ALU = mybir.AluOpType
ACT = mybir.ActivationFunctionType
AX = mybir.AxisListType

P = 128
NB, T = 8, 256
NT = NB * T // P
TOK = NB * T
W512 = 512
NC = TOK // W512
NE = 8
SEQ = NE + 1
CAP = 512
NM = 4
MISC = 8
LN_EPS = 1e-5
RMS_EPS = 1e-6


def layer_norm(nc, g, sb, sem, mixture, split=True):
    x, xr, PS = g["x"], g["xr"], g["PS"]
    st = sb("st", [P, NT, 6])
    mean, diff, m2, var, ms = (sb(n, [P, NT]) for n in ("mean", "diff", "m2", "var", "ms"))
    sd, rstd, rms, rrms, scl = (sb(n, [P, NT]) for n in ("sd", "rstd", "rms", "rrms", "scl"))
    eps_ln, eps_rms, warm = sb("eps_ln", [P, 1]), sb("eps_rms", [P, 1]), sb("warm", [P, 1])
    s_eps = sem("s_eps")
    s_warm = sem("s_warm")
    s_var = sem("s_var")
    s_sd = sem("s_sd")
    s_ln = sem("s_ln")
    s_xr = sem("s_xr")
    s_tr = sem("s_tr")
    s_xT = sem("s_xT")
    s_xlo = sem("s_xlo")

    def pool_part(pool):
        pool.memset(eps_ln[:], LN_EPS).then_inc(s_eps, 1)
        pool.memset(eps_rms[:], RMS_EPS).then_inc(s_eps, 1)

    def act_part(act):
        act.wait_ge(s_eps, 2)
        act.activation(warm[:], eps_ln[:], ACT.Sqrt).then_inc(s_warm, 1)
        act.wait_ge(s_var, 1)
        act.activation(sd[:], var[:], ACT.Sqrt, bias=eps_ln[:]).then_inc(s_sd, 1)
        if mixture == "A":
            act.wait_ge(s_var, 2)
            act.activation(rms[:], ms[:], ACT.Sqrt, bias=eps_rms[:]).then_inc(s_sd, 1)
        for k in range(NC):
            cols = slice(k * W512, (k + 1) * W512)
            act.wait_ge(s_tr, k + 1)
            act.activation(g["xT"][:, cols], PS[:, k, :], ACT.Copy).then_inc(s_xT, 1)
            if split:
                act.activation(g["xhi"][:, cols], PS[:, k, :], ACT.Copy).then_inc(s_xT, 1)

    def dve_part(dve):
        n = [0]

        def then(ins):
            n[0] += 1
            ins.then_inc(s_ln, 1)
            dve.wait_ge(s_ln, n[0])

        for t in range(NT - 1):
            dve.bn_stats(st[:, t, :], x[:, t, :])
        then(dve.bn_stats(st[:, NT - 1, :], x[:, NT - 1, :]))
        dve.tensor_tensor(mean[:], st[:, :, 1], st[:, :, 4], ALU.add)
        dve.tensor_tensor(m2[:], st[:, :, 2], st[:, :, 5], ALU.add)
        then(dve.tensor_tensor(diff[:], st[:, :, 1], st[:, :, 4], ALU.subtract))
        then(dve.tensor_tensor(diff[:], diff[:], diff[:], ALU.mult))
        then(dve.scalar_tensor_tensor(out=m2[:], in0=diff[:], scalar=P / 4.0, in1=m2[:],
                                      op0=ALU.mult, op1=ALU.add))
        dve.tensor_scalar(var[:], m2[:], 1.0 / P, None, ALU.mult).then_inc(s_var, 1)
        then(dve.tensor_scalar(mean[:], mean[:], 0.5, None, ALU.mult))
        dve.wait_ge(s_sd, 1)
        then(dve.reciprocal(rstd[:], sd[:]))
        row_scale = rstd
        if mixture == "A":
            then(dve.tensor_tensor(ms[:], rstd[:], rstd[:], ALU.mult))
            dve.tensor_tensor(ms[:], ms[:], var[:], ALU.mult).then_inc(s_var, 1)
            dve.wait_ge(s_sd, 2)
            then(dve.reciprocal(rrms[:], rms[:]))
            then(dve.tensor_tensor(scl[:], rrms[:], rstd[:], ALU.mult))
            row_scale = scl

        def low(k):
            cols = slice(k * W512, (k + 1) * W512)
            dve.wait_ge(s_xT, 2 * (k + 1))
            dve.tensor_tensor(g["xlo"][:, cols], g["xT"][:, cols], g["xhi"][:, cols].bitcast(F32),
                              ALU.subtract).then_inc(s_xlo, 1)

        for t in range(NT):
            dve.tensor_scalar(xr[:, t, :], x[:, t, :], mean[:, t:t + 1], row_scale[:, t:t + 1],
                              ALU.subtract, ALU.mult).then_inc(s_xr, 1)
            if split and t % 4 == 3 and t > 8:
                low(t // 4 - 2)
        if split:
            low(NC - 2)
            low(NC - 1)

    def pe_part(pe):
        for t in range(NT):
            pe.wait_ge(s_xr, t + 1)
            ins = pe.transpose(PS[:, t // 4, (t % 4) * P:(t % 4 + 1) * P], xr[:, t, :], g["ident"][:])
            if t % 4 == 3:
                ins.then_inc(s_tr, 1)

    return pool_part, act_part, dve_part, pe_part, rms, s_xT, s_xlo


def mixture_block(nc, g, tag, kind, weights):
    x, xr, PS = g["x"], g["xr"], g["PS"]
    A = kind == "A"
    NF = 2 if A else 4
    NF0 = 1 if A else 4
    QF = 2 if A else 1
    UP = NM * P
    WC = UP + NF * P + MISC
    LAST = SEQ - 1
    with ExitStack() as c:
        def sb(name, shape, dt=F32):
            return c.enter_context(nc.sbuf_tensor(f"{tag}_{name}", shape, dt))

        def sem(name):
            return g["sem"](f"{tag}_{name}")

        pool_norm, act_norm, dve_norm, pe_norm, rms, s_xT, s_xlo = layer_norm(nc, g, sb, sem, kind)
        lg, ex, pr, sel, rank = (sb(n, [P, NT, NE]) for n in ("lg", "ex", "pr", "sel", "rank"))
        above, equal = (sb(n, [P, NT, NE, NE]) for n in ("above", "equal"))
        mx, sm, rs = (sb(n, [P, NT]) for n in ("mx", "sm", "rs"))
        tot, tmp = sb("tot", [P, NT, NE]), sb("tmp", [P, NT, NE])
        wfull = sb("wfull", [P, NT, 16])
        whi = sb("whi", [P, NT, 16], F32R)
        wpack = sb("wpack", [P, NT, 32])
        raw = [sb(f"raw{i}", [P, WC]) for i in range(2)]
        scaled = sb("scaled", [P, UP]) if A else None
        uphi = [sb(f"uphi{i}", [P, UP], F32R) for i in range(2)]
        uplo = [sb(f"uplo{i}", [P, UP], F32R) for i in range(2)]
        dnhi = [sb(f"dnhi{i}", [P, NF * P], F32R) for i in range(2)]
        dnlo = [sb(f"dnlo{i}", [P, NF * P], F32R) for i in range(2)]
        pick = [sb(f"pick{i}", [32, P], F32R) for i in range(3)]
        wrow = [sb(f"wrow{i}", [P, TOK]) for i in range(2)]
        gate = [sb(f"gate{i}", [P, NF, W512]) for i in range(2)] if A else None
        hid = [sb(f"hid{i}", [P, NF, W512]) for i in range(2)]
        hhi = [sb(f"hhi{i}", [P, NF, W512], F32R) for i in range(2)]
        hlo = [sb(f"hlo{i}", [P, NF, W512], F32R) for i in range(2)]
        part = [sb(f"part{i}", [P, W512]) for i in range(2)]
        acc = sb("acc", [P, TOK])
        dense = sb("dense", [P, TOK]) if A else None
        fin = [sb(f"fin{i}", [P, 4, P]) for i in range(2)]

        s_raw = [sem(f"s_raw{i}") for i in range(2)]
        s_clear = sem("s_clear")
        s_split = sem("s_split")
        s_logit = sem("s_logit")
        s_rt = sem("s_rt")
        s_lread = sem("s_lread")
        s_lmax = sem("s_lmax")
        s_ex = sem("s_ex")
        s_sel = sem("s_sel")
        s_cum = sem("s_cum")
        s_wp = sem("s_wp")
        s_wtr = sem("s_wtr")
        s_wT = sem("s_wT")
        s_row = sem("s_row")
        s_rowc = sem("s_rowc")
        s_ring = sem("s_ring")
        s_gelu = sem("s_gelu")
        s_gu = sem("s_gu")
        s_hhi = sem("s_hhi")
        s_lo = sem("s_lo")
        s_down = sem("s_down")
        s_part = sem("s_part")
        s_acc = sem("s_acc")
        s_bias = sem("s_bias")
        s_sum = sem("s_sum")
        s_back = sem("s_back")
        s_fin = sem("s_fin")
        SPLIT = 6 if A else 5
        SUMS = 2 if A else 1
        block = c.enter_context(nc.Block())

        def banks(n):
            return QF * feats(n)

        def feats(n):
            return 0 if isinstance(n, int) and n == 0 else NC * NF0 + (n - 1) * (NC * NF)

        @block.sync
        def _(sp):
            def load(n, i):
                sp.dma_start(raw[i][:], weights[bass.ds(n, 1)].rearrange("a p c -> (a p) c")).then_inc(s_raw[i], 16)

            load(0, 0)
            load(1, 1)
            with sp.Fori(2, LAST, 2) as n:
                sp.wait_ge(s_down, 4 * n - 4)
                load(n, 0)
                sp.wait_ge(s_down, 4 * n)
                load(n + 1, 1)
            sp.wait_ge(s_down, 4 * LAST - 4)
            load(LAST, 0)

        @block.gpsimd
        def _(pool):
            one = g["ones"][:, 0:1]

            def split(n, i, reused):
                at = n * SPLIT
                pool.wait_ge(s_raw[i], 8 * n + (16 if i == 0 else 8))
                if reused:
                    pool.wait_ge(s_down, 4 * n - 4)
                dst = pick[2] if isinstance(n, int) and n == 0 else pick[i]
                pool.tensor_tensor(dst[:], g["ones"][0:32, :], raw[i][0:32, WC - 7:WC - 6].to_broadcast([32, P]),
                                   ALU.mult).then_inc(s_split, 1)
                src = raw[i][:, 0:UP]
                if A:
                    norm = raw[i][:, WC - 8:WC - 7].to_broadcast([P, UP])
                    pool.tensor_tensor(uphi[i][:], src, norm, ALU.mult).then_inc(s_split, 1)
                    pool.tensor_tensor(scaled[:], src, norm, ALU.mult).then_inc(s_split, 1)
                    src = scaled[:]
                else:
                    pool.tensor_tensor(uphi[i][:], src, one.to_broadcast([P, UP]), ALU.mult).then_inc(s_split, 1)
                dn = raw[i][:, UP:UP + NF * P]
                pool.tensor_tensor(dnhi[i][:], dn, one.to_broadcast([P, NF * P]), ALU.mult).then_inc(s_split, 1)
                pool.wait_ge(s_split, at + SPLIT - 2)
                pool.tensor_tensor(uplo[i][:], src, uphi[i][:].bitcast(F32), ALU.subtract).then_inc(s_split, 1)
                pool.tensor_tensor(dnlo[i][:], dn, dnhi[i][:].bitcast(F32), ALU.subtract).then_inc(s_split, 1)
                if A:
                    pool.wait_ge(s_split, at + SPLIT - 1)

            def add(n):
                for k in range(NC):
                    cols = slice(k * W512, (k + 1) * W512)
                    pool.wait_ge(s_part, 4 * n + k + 1)
                    pool.wait_ge(s_acc, 4 * n - 4 + k)
                    pool.tensor_tensor(acc[:, cols], acc[:, cols], part[k % 2][:], ALU.add).then_inc(s_acc, 1)

            pool_norm(pool)
            pool.memset(wfull[:], 0.0).then_inc(s_clear, 1)
            split(0, 0, False)
            split(1, 1, False)
            if A:
                for k in range(NC):
                    pool.engine_nop().then_inc(s_acc, 1)
                split(2, 0, True)
            else:
                split(2, 0, True)
                add(1)
            with pool.Fori(3, LAST - 1, 2) as n:
                split(n, 1, True)
                add(n - 1)
                split(n + 1, 0, True)
                add(n)
            split(LAST - 1, 1, True)
            add(LAST - 2)
            split(LAST, 0, True)
            add(LAST - 1)
            add(LAST)

        @block.tensor
        def _(pe):
            def group(k):
                return slice(k * W512, (k + 1) * W512)

            def up(n, i, k):
                nf = NF0 if isinstance(n, int) and n == 0 else NF
                if k == 0:
                    pe.wait_ge(s_split, n * SPLIT + SPLIT)
                if isinstance(n, int) and n == 0:
                    pe.wait_ge(s_xlo, k + 1)
                for m in range(QF * nf):
                    q = QF * nf * k + m
                    if not (isinstance(n, int) and n == 0 and q < 4):
                        if not A:
                            pe.wait_ge(s_gelu, feats(n) + q - 3)
                        elif q % 2 == 0:
                            pe.wait_ge(s_gelu, feats(n) + (q - 4) // 2 + 1)
                        else:
                            pe.wait_ge(s_gu, feats(n) + (q - 4) // 2 + 1)
                    f = (m // 2 + 2 * (m % 2)) if A else m
                    w, bank = slice(f * P, (f + 1) * P), PS[:, 4 + q % 4, :]
                    pe.matmul(bank, uphi[i][:, w], g["xhi"][:, group(k)], start=True, stop=False)
                    pe.matmul(bank, uphi[i][:, w], g["xlo"][:, group(k)], start=False, stop=False)
                    pe.matmul(bank, uplo[i][:, w], g["xhi"][:, group(k)], start=False, stop=True).then_inc(s_ring, 1)

            def down(n, i, k):
                first = isinstance(n, int) and n == 0
                nf = NF0 if first else NF
                pe.wait_ge(s_lo, feats(n) + nf * (k + 1))
                if not (first and k < 2):
                    pe.wait_ge(s_part, 4 * n + k - 1)
                for f in range(nf):
                    w, bank = slice(f * P, (f + 1) * P), PS[:, k % 2, :]
                    pe.matmul(bank, dnhi[i][:, w], hhi[k % 2][:, f, :], start=f == 0, stop=False)
                    pe.matmul(bank, dnlo[i][:, w], hhi[k % 2][:, f, :], start=False, stop=False)
                    ins = pe.matmul(bank, dnhi[i][:, w], hlo[k % 2][:, f, :], start=False, stop=f == nf - 1)
                ins.then_inc(s_down, 1)

            def rows(at, which, reuse):
                for k in range(NC):
                    if reuse or k >= 2:
                        pe.wait_ge(s_rowc, at + k - 1)
                    pe.matmul(PS[:, 2 + k % 2, :], which[:], g["wT"][:, group(k)], start=True, stop=True).then_inc(s_row, 1)

            def one_pass(n, i, reuse=True):
                up(n, i, 0)
                down(n - 1, 1 - i, NC - 1)
                rows(4 * n - 4, pick[i], reuse)
                for k in range(1, NC):
                    up(n, i, k)
                    down(n, i, k - 1)

            pe_norm(pe)
            for t in range(NT):
                pe.wait_ge(s_xT, 2 * (t // 4) + 2)
                if t == 0:
                    pe.wait_ge(s_xT, 6)
                ins = pe.matmul(PS[:, 2, t * NE:(t + 1) * NE], g["xT"][:, t * P:(t + 1) * P],
                                g["router" + kind][:], start=True, stop=True)
            ins.then_inc(s_logit, 1)
            up(0, 0, 0)
            for k in range(1, NC):
                up(0, 0, k)
                down(0, 0, k - 1)
            up(1, 1, 0)
            down(0, 0, NC - 1)
            if A:
                pe.wait_ge(s_sel, 1)
                chosen = sel[:].rearrange("p t e -> p (t e)")
                pe.matmul(PS[:, 3, 0:NT * NE], g["strict"][:], chosen, start=True, stop=True).then_inc(s_cum, 1)
                pe.matmul(PS[:, 3, NT * NE:2 * NT * NE], g["ones"][:], chosen, start=True, stop=True).then_inc(s_cum, 1)
            pe.wait_ge(s_wp, 1)
            for t in range(NT):
                if t % 4 == 0 and t >= 8:
                    pe.wait_ge(s_wT, t // 4 - 1)
                ins = pe.transpose(PS[0:32, 2 + t // 4 % 2, (t % 4) * P:(t % 4 + 1) * P], wpack[:, t, :], g["ident"][:])
                if t % 4 == 3:
                    ins.then_inc(s_wtr, 1)
            pe.wait_ge(s_wT, NC)
            rows(0, pick[1], False)
            for k in range(1, NC):
                up(1, 1, k)
                down(1, 1, k - 1)
            with pe.Fori(2, LAST, 2) as n:
                one_pass(n, 0)
                one_pass(n + 1, 1)
            one_pass(LAST, 0)
            down(LAST, 0, NC - 1)
            if A:
                rows(4 * LAST, pick[2], True)
            else:
                for k in range(NC):
                    if k < 2:
                        pe.wait_ge(s_rowc, 4 * LAST - 1 + k)
                    else:
                        pe.wait_ge(s_sum, k - 1)
                    pe.matmul(PS[:, 2 + k % 2, :], g["b2B"][:], g["wT"][:, group(k)].bitcast(F32),
                              start=True, stop=True).then_inc(s_bias, 1)
            for k in range(NC):
                pe.wait_ge(s_sum, SUMS * (k + 1))
                for t in range(4):
                    ins = pe.transpose(PS[:, 4 + k, t * P:(t + 1) * P], acc[:, (4 * k + t) * P:(4 * k + t + 1) * P],
                                       g["ident"][:])
                ins.then_inc(s_back, 1)

        @block.scalar
        def _(act):
            def copy_rows(at, i, reuse):
                if reuse:
                    act.wait_ge(s_part, at)
                for k in range(NC):
                    act.wait_ge(s_row, at + k + 1)
                    act.activation(wrow[i][:, k * W512:(k + 1) * W512], PS[:, 2 + k % 2, :], ACT.Copy).then_inc(s_rowc, 1)

            def step(n, i, k):
                first = isinstance(n, int) and n == 0
                nf = NF0 if first else NF
                for m in range(nf):
                    q = QF * (nf * k + m)
                    act.wait_ge(s_ring, banks(n) + q + 1)
                    src = PS[:, 4 + q % 4, :]
                    if A:
                        if m == 0 and not (first and k < 2):
                            act.wait_ge(s_gu, feats(n) + nf * (k - 1) if not (k < 2 and isinstance(n, int) and n == 1)
                                        else feats(n) - NF0 * (2 - k) + NF0)
                        act.activation(gate[k % 2][:, m, :], src, ACT.Gelu).then_inc(s_gelu, 1)
                        continue
                    if m == 0 and not (first and k < 2):
                        act.wait_ge(s_lo, feats(n) + NF * (k - 1))
                        act.wait_ge(s_down, 4 * n + k - 1)
                    bias = raw[i][:, WC - 6 + m:WC - 5 + m]
                    act.activation(hid[k % 2][:, m, :], src, ACT.Gelu_apprx_tanh, bias=bias)
                    act.activation(hhi[k % 2][:, m, :], src, ACT.Gelu_apprx_tanh, bias=bias).then_inc(s_gelu, 1)
                if A:
                    if not (first and k < 2):
                        act.wait_ge(s_down, 4 * n + k - 1)
                    for m in range(nf):
                        act.wait_ge(s_gu, feats(n) + nf * k + m + 1)
                        act.activation(hhi[k % 2][:, m, :], hid[k % 2][:, m, :], ACT.Copy).then_inc(s_hhi, 1)

            def one_pass(n, i, reuse=True):
                step(n, i, 0)
                copy_rows(4 * n - 4, i, reuse)
                for k in range(1, NC):
                    step(n, i, k)

            act_norm(act)
            act.wait_ge(s_lmax, 1)
            act.activation(ex[:], lg[:], ACT.Exp).then_inc(s_ex, 1)
            for k in range(NC):
                step(0, 0, k)
            step(1, 1, 0)
            for k in range(NC):
                act.wait_ge(s_wtr, k + 1)
                act.activation(g["wT"][:, k * W512:(k + 1) * W512], PS[0:32, 2 + k % 2, :], ACT.Copy).then_inc(s_wT, 1)
            copy_rows(0, 1, False)
            for k in range(1, NC):
                step(1, 1, k)
            with act.Fori(2, LAST, 2) as n:
                one_pass(n, 0)
                one_pass(n + 1, 1)
            one_pass(LAST, 0)
            if A:
                copy_rows(4 * LAST, 1, True)

        @block.vector
        def _(dve):
            n_rt = [0]

            def then(ins):
                n_rt[0] += 1
                ins.then_inc(s_rt, 1)
                dve.wait_ge(s_rt, n_rt[0])

            def over(a):
                return a.unsqueeze(2).to_broadcast([P, NT, NE])

            def route_logits():
                dve.wait_ge(s_logit, 1)
                logits = PS[:, 2, 0:NT * NE].rearrange("p (t e) -> p t e", e=NE)
                if A:
                    then(dve.tensor_tensor(lg[:], logits, over(rms[:]), ALU.mult))
                else:
                    gb = g["gate_b"][:].unsqueeze(1).to_broadcast([P, NT, NE])
                    then(dve.tensor_tensor(lg[:], logits, gb, ALU.add))
                then(dve.tensor_reduce(mx[:], lg[:], AX.X, ALU.max))
                dve.tensor_tensor(lg[:], lg[:], over(mx[:]), ALU.subtract).then_inc(s_lmax, 1)

            def route_softmax():
                dve.wait_ge(s_ex, 1)
                then(dve.tensor_reduce(sm[:], ex[:], AX.X, ALU.add))
                then(dve.reciprocal(rs[:], sm[:]))
                then(dve.tensor_tensor(pr[:], ex[:], over(rs[:]), ALU.mult))

            def route_choose():
                others = pr[:].unsqueeze(2).to_broadcast([P, NT, NE, NE])
                own = pr[:].unsqueeze(3).to_broadcast([P, NT, NE, NE])
                before = g["before"][:].rearrange("p (e j) -> p e j", j=NE).unsqueeze(1).to_broadcast([P, NT, NE, NE])
                dve.tensor_tensor(above[:], others, own, ALU.is_gt)
                then(dve.tensor_tensor(equal[:], others, own, ALU.is_equal))
                then(dve.tensor_tensor(equal[:], equal[:], before, ALU.mult))
                then(dve.tensor_tensor(above[:], above[:], equal[:], ALU.add))
                then(dve.tensor_reduce(rank[:], above[:], AX.X, ALU.add))
                dve.tensor_scalar(sel[:], rank[:], 1.5, None, ALU.is_lt).then_inc(s_sel, 1)
                dve.wait_ge(s_sel, 1)
                then(dve.tensor_tensor(pr[:], pr[:], sel[:], ALU.mult))
                then(dve.tensor_reduce(sm[:], pr[:], AX.X, ALU.add))

            def route_weights():
                dve.wait_ge(s_clear, 1)
                if A:
                    dve.wait_ge(s_cum, 2)
                    cum = PS[:, 3, 0:NT * NE].rearrange("p (t e) -> p t e", e=NE)
                    then(dve.tensor_copy(tot[:], PS[:, 3, NT * NE:2 * NT * NE].rearrange("p (t e) -> p t e", e=NE)))
                    then(dve.tensor_tensor(rank[:], cum, tot[:], ALU.subtract))
                    a, b = tot, tmp
                    step = 1
                    while step < NT:
                        dve.tensor_copy(b[:, 0:step, :], a[:, 0:step, :])
                        then(dve.tensor_tensor(b[:, step:, :], a[:, step:, :], a[:, 0:NT - step, :], ALU.add))
                        a, b = b, a
                        step *= 2
                    then(dve.tensor_tensor(rank[:], rank[:], a[:], ALU.add))
                    then(dve.scalar_tensor_tensor(out=rank[:], in0=rank[:], scalar=CAP - 0.5, in1=sel[:],
                                                  op0=ALU.is_gt, op1=ALU.mult))
                    then(dve.tensor_reduce(wfull[:, :, 0], rank[:], AX.X, ALU.max))
                    then(dve.tensor_scalar(rs[:], wfull[:, :, 0], -1.0, 1.0, ALU.mult, ALU.add))
                    dve.tensor_tensor(wfull[:, :, 1:SEQ], pr[:], over(rs[:]), ALU.mult)
                    then(dve.tensor_tensor(sm[:], sm[:], rs[:], ALU.mult))
                    then(dve.tensor_scalar(sm[:], sm[:], 1.0, None, ALU.add))
                    dve.tensor_tensor(g["fscale"][:], sm[:], rms[:], ALU.mult)
                else:
                    then(dve.tensor_scalar(sm[:], sm[:], 1e-9, None, ALU.add))
                    then(dve.reciprocal(rs[:], sm[:]))
                    dve.tensor_tensor(wfull[:, :, 1:SEQ], pr[:], over(rs[:]), ALU.mult)
                    then(dve.memset(wfull[:, :, 0:1], 1.0))
                then(dve.tensor_copy(whi[:], wfull[:]))
                dve.tensor_copy(wpack[:, :, 0:16], whi[:].bitcast(F32))
                dve.tensor_tensor(wpack[:, :, 16:32], wfull[:], whi[:].bitcast(F32), ALU.subtract).then_inc(s_wp, 1)

            def hidden(n, k):
                first = isinstance(n, int) and n == 0
                nf = NF0 if first else NF
                if A:
                    for m in range(nf):
                        at = feats(n) + nf * k + m
                        q = 2 * (nf * k + m) + 1
                        dve.wait_ge(s_gelu, at + 1)
                        dve.wait_ge(s_ring, banks(n) + q + 1)
                        dve.tensor_tensor(hid[k % 2][:, m, :], gate[k % 2][:, m, :], PS[:, 4 + q % 4, :],
                                          ALU.mult).then_inc(s_gu, 1)

            def low(n, k):
                first = isinstance(n, int) and n == 0
                nf = NF0 if first else NF
                if not (first and k < 2):
                    dve.wait_ge(s_down, 4 * n + k - 1)
                for m in range(nf):
                    dve.wait_ge(s_hhi if A else s_gelu, feats(n) + nf * k + m + 1)
                    dve.tensor_tensor(hlo[k % 2][:, m, :], hid[k % 2][:, m, :], hhi[k % 2][:, m, :].bitcast(F32),
                                      ALU.subtract).then_inc(s_lo, 1)

            def weigh(n, i, k):
                cols = slice(k * W512, (k + 1) * W512)
                zero, one = (isinstance(n, int) and n == m for m in (0, 1))
                dve.wait_ge(s_down, 4 * n + k + 1)
                if zero:
                    dve.tensor_copy((dense if A else acc)[:, cols], PS[:, k % 2, :]).then_inc(s_part, 1)
                    return
                dve.wait_ge(s_rowc, 4 * n - 4 + k + 1)
                direct = A and one
                dst = acc[:, cols] if direct else part[k % 2][:]
                if not direct and not (one and k < 2) and not (A and isinstance(n, int) and n == 2 and k < 2):
                    dve.wait_ge(s_acc, 4 * n + k - 5)
                dve.tensor_tensor(dst, PS[:, k % 2, :], wrow[i][:, cols], ALU.mult).then_inc(s_part, 1)

            def one_pass(n, i):
                for k in range(NC):
                    hidden(n, k)
                    low(n, k)
                    if k:
                        weigh(n, i, k - 1)
                    else:
                        weigh(n - 1, 1 - i, NC - 1)

            dve_norm(dve)
            route_logits()
            hidden(0, 0)
            low(0, 0)
            route_softmax()
            hidden(0, 1)
            low(0, 1)
            weigh(0, 0, 0)
            if A:
                hidden(0, 2)
                low(0, 2)
                weigh(0, 0, 1)
                route_choose()
                hidden(0, 3)
                low(0, 3)
                weigh(0, 0, 2)
            else:
                route_choose()
                hidden(0, 2)
                low(0, 2)
                weigh(0, 0, 1)
                route_weights()
                hidden(0, 3)
                low(0, 3)
                weigh(0, 0, 2)
            hidden(1, 0)
            low(1, 0)
            weigh(0, 0, 3)
            if A:
                route_weights()
            for k in range(1, NC):
                hidden(1, k)
                low(1, k)
                weigh(1, 1, k - 1)
            one_pass(2, 0)
            with dve.Fori(3, LAST - 1, 2) as n:
                one_pass(n, 1)
                one_pass(n + 1, 0)
            one_pass(LAST - 1, 1)
            one_pass(LAST, 0)
            weigh(LAST, 0, NC - 1)
            for k in range(NC):
                cols = slice(k * W512, (k + 1) * W512)
                if A:
                    dve.wait_ge(s_rowc, 4 * LAST + k + 1)
                    dve.tensor_tensor(dense[:, cols], dense[:, cols], wrow[1][:, cols], ALU.mult).then_inc(s_sum, 1)
                    dve.wait_ge(s_sum, 2 * k + 1)
                    src = dense[:, cols]
                else:
                    dve.wait_ge(s_bias, k + 1)
                    src = PS[:, 2 + k % 2, :]
                dve.wait_ge(s_acc, 4 * LAST - 3 + k)
                dve.tensor_tensor(acc[:, cols], acc[:, cols], src, ALU.add).then_inc(s_sum, 1)
            for k in range(NC):
                tiles = slice(4 * k, 4 * k + 4)
                dve.wait_ge(s_back, k + 1)
                got = PS[:, 4 + k, :].rearrange("p (t d) -> p t d", t=4)
                if A:
                    for t in range(4):
                        ins = dve.scalar_tensor_tensor(out=fin[k % 2][:, t, :], in0=xr[:, 4 * k + t, :],
                                                       scalar=g["fscale"][:, 4 * k + t:4 * k + t + 1],
                                                       in1=got[:, t, :], op0=ALU.mult, op1=ALU.add)
                else:
                    ins = dve.tensor_tensor(fin[k % 2][:], xr[:, tiles, :], got, ALU.add)
                ins.then_inc(s_fin, 1)
                dve.wait_ge(s_fin, 2 * k + 1)
                dve.scalar_tensor_tensor(out=x[:, tiles, :], in0=fin[k % 2][:], scalar=0.5, in1=x[:, tiles, :],
                                         op0=ALU.mult, op1=ALU.add).then_inc(s_fin, 1)


def normalise(nc, g, tag):
    with ExitStack() as c:
        def sb(name, shape, dt=F32):
            return c.enter_context(nc.sbuf_tensor(f"{tag}_{name}", shape, dt))

        pool_norm, act_norm, dve_norm, pe_norm, *_ = layer_norm(nc, g, sb, lambda n: g["sem"](f"{tag}_{n}"), None)
        block = c.enter_context(nc.Block())

        @block.gpsimd
        def _(pool):
            pool_norm(pool)

        @block.scalar
        def _(act):
            act_norm(act)

        @block.vector
        def _(dve):
            dve_norm(dve)

        @block.tensor
        def _(pe):
            pe_norm(pe)


def hla_block(nc, g, tag, W):
    x, PS = g["x"], g["PS"]
    HP = 8
    UN = 2 * HP
    DK = 64
    BLK = 3 * P
    with ExitStack() as c:
        def sb(name, shape, dt=F32):
            return c.enter_context(nc.sbuf_tensor(f"{tag}_{name}", shape, dt))

        def sem(name):
            return g["sem"](f"{tag}_{name}")

        w = {n: sb("w" + n, [P, HP * P]) for n in "qkv"}
        whi = {n: sb("whi" + n, [P, HP * P], F32R) for n in "qkv"}
        wlo = {n: sb("wlo" + n, [P, HP * P], F32R) for n in "qkv"}
        wo = sb("wo", [P, HP, P])
        xbhi, xblo = sb("xbhi", [P, W512], F32R), sb("xblo", [P, W512], F32R)
        V = sb("V", [P, 4, HP * P])
        qT = [sb(f"qT{i}", [P, W512]) for i in range(2)]
        kT = [sb(f"kT{i}", [P, W512]) for i in range(2)]
        Am = [sb(f"Am{i}", [P, 2, BLK]) for i in range(2)]
        Wm = [sb(f"Wm{i}", [P, 2, BLK]) for i in range(2)]
        OT = sb("OT", [P, HP, W512])

        s_w = sem("s_w")
        s_whi = sem("s_whi")
        s_wlo = sem("s_wlo")
        s_xb = sem("s_xb")
        s_proj = sem("s_proj")
        s_evac = sem("s_evac")
        s_A = sem("s_A")
        s_Am = sem("s_Am")
        s_W = sem("s_W")
        s_Wm = sem("s_Wm")
        s_O = sem("s_O")
        s_OT = sem("s_OT")
        s_res = sem("s_res")
        block = c.enter_context(nc.Block())

        @block.sync
        def _(sp):
            for n in "qkv":
                sp.dma_start(w[n][:], W[n]).then_inc(s_w, 16)
            sp.dma_start(wo[:], W["o"]).then_inc(s_w, 16)

        @block.scalar
        def _(act):
            act.wait_ge(s_w, 64)
            for n in "qkv":
                act.activation(whi[n][:], w[n][:], ACT.Copy).then_inc(s_whi, 1)
            with act.Fori(0, NC) as it:
                def copy(dst, j, bank):
                    act.wait_ge(s_proj, 26 * it + j + 1)
                    act.activation(dst, PS[:, bank, :], ACT.Copy).then_inc(s_evac, 1)

                def copy_qk(h):
                    j = 0 if h == 0 else 8 + 2 * h
                    if h >= 2:
                        act.wait_ge(s_A, 32 * it + 4 * (h - 1))
                    copy(qT[h % 2][:], j, 0)
                    copy(kT[h % 2][:], j + 1, 1)

                def copy_o(h):
                    act.wait_ge(s_O, UN * it + 2 * h + 2)
                    act.activation(OT[:, h, :], PS[:, 6 + h % 2, :], ACT.Copy).then_inc(s_OT, 1)

                copy_qk(0)
                for j in range(8):
                    copy(V[:, j // 2, j % 2 * W512:(j % 2 + 1) * W512], 2 + j, j % 2)
                copy_qk(1)
                for h in range(HP):
                    if h + 2 < HP:
                        copy_qk(h + 2)
                    copy_o(h)

        @block.vector
        def _(dve):
            dve.wait_ge(s_w, 64)
            for i, n in enumerate("qkv"):
                dve.wait_ge(s_whi, i + 1)
                dve.tensor_tensor(wlo[n][:], w[n][:], whi[n][:].bitcast(F32), ALU.subtract).then_inc(s_wlo, 1)
            with dve.Fori(0, NC) as it:
                dve.tensor_copy(xbhi[:], g["xhi"][:, bass.ds(it * W512, W512)]).then_inc(s_xb, 1)
                dve.tensor_copy(xblo[:], g["xlo"][:, bass.ds(it * W512, W512)]).then_inc(s_xb, 1)

                def mask(u, full, done, dst, bank, used):
                    for h in range(2):
                        n = 32 * it + 2 * u + h
                        dve.wait_ge(full, n + 1)
                        if used is not None:
                            dve.wait_ge(*used(h))
                        dve.tensor_tensor(dst[u % 2][:, h, :], PS[:, bank + h, 0:BLK], g["tri"][:],
                                          ALU.mult).then_inc(done, 1)

                def mask_a(u):
                    mask(u, s_A, s_Am, Am, 2, (lambda h: (s_W, 32 * it + 2 * u - 4 + h + 1)) if u >= 2 else None)

                def mask_w(u):
                    mask(u, s_W, s_Wm, Wm, 4, (lambda h: (s_O, UN * it + u - 1)) if u >= 2 else None)

                mask_a(0)
                for u in range(UN):
                    if u + 1 < UN:
                        mask_a(u + 1)
                    mask_w(u)
                for j in range(2):
                    dve.wait_ge(s_proj, 26 * it + 24 + j + 1)
                    rows = x[:, bass.ds(it * 4 + 2 * j, 2), :]
                    dve.tensor_tensor(rows, rows, PS[:, j, 0:2 * P].rearrange("p (t d) -> p t d", t=2),
                                      ALU.add).then_inc(s_res, 1)

        @block.tensor
        def _(pe):
            def proj(bank, lo, lhs, rhs):
                (lh, ll), (rh, rl) = lhs, rhs
                pe.matmul(PS[:, bank, :], lh, rh, start=True, stop=False)
                pe.matmul(PS[:, bank, :], lh, rl, start=False, stop=False)
                pe.matmul(PS[:, bank, :], ll, rh, start=False, stop=True).then_inc(s_proj, 1)

            pe.wait_ge(s_wlo, 3)
            with pe.Fori(0, NC) as it:
                turn = bass.ds(it * W512, W512)

                def proj_qk(h):
                    j = 0 if h == 0 else 8 + 2 * h
                    for i, n in enumerate("qk"):
                        if j + i >= 2:
                            pe.wait_ge(s_evac, 24 * it + j + i - 1)
                        cols = slice(h * P, (h + 1) * P)
                        proj(i, None, (whi[n][:, cols], wlo[n][:, cols]), (g["xhi"][:, turn], g["xlo"][:, turn]))

                def proj_v(j):
                    rows, cols = slice(j // 2 * P, (j // 2 + 1) * P), slice(j % 2 * W512, (j % 2 + 1) * W512)
                    pe.wait_ge(s_evac, 24 * it + j + 1)
                    proj(j % 2, None, (xbhi[:, rows], xblo[:, rows]), (whi["v"][:, cols], wlo["v"][:, cols]))

                def scores(u):
                    h, b = divmod(u, 2)
                    pe.wait_ge(s_evac, 24 * it + (2 if h == 0 else 10 + 2 * h))
                    for i in range(2):
                        if u:
                            pe.wait_ge(s_Am, 32 * it + 2 * u - 2 + i + 1)
                        d, at = slice(i * DK, (i + 1) * DK), b * T
                        k, q = kT[h % 2][d, :], qT[h % 2][d, :]
                        pe.matmul(PS[:, 2 + i, 0:T], k[:, at:at + P], q[:, at:at + T], start=True, stop=True)
                        pe.matmul(PS[:, 2 + i, T:BLK], k[:, at + P:at + T], q[:, at + P:at + T],
                                  start=True, stop=True).then_inc(s_A, 1)

                def square(u):
                    for i in range(2):
                        pe.wait_ge(s_Am, 32 * it + 2 * u + i + 1)
                        if u:
                            pe.wait_ge(s_Wm, 32 * it + 2 * u - 2 + i + 1)
                        a = Am[u % 2][:, i, :]
                        pe.matmul(PS[:, 4 + i, 0:T], a[:, 0:P], a[:, 0:T], start=True, stop=True)
                        pe.matmul(PS[:, 4 + i, T:BLK], a[:, P:T], a[:, P:T], start=True, stop=False)
                        pe.matmul(PS[:, 4 + i, T:BLK], a[:, T:BLK], a[:, T:BLK],
                                  start=False, stop=True).then_inc(s_W, 1)

                def output(u):
                    h, b = divmod(u, 2)
                    if u == 0:
                        pe.wait_ge(s_evac, 24 * it + 10)
                    if b == 0 and h >= 2:
                        pe.wait_ge(s_OT, HP * it + h - 1)
                    pe.wait_ge(s_Wm, 32 * it + 2 * u + 2)
                    bank, at = PS[:, 6 + h % 2, :], b * T
                    for j in range(2):
                        for i in range(2):
                            d = slice(i * DK, (i + 1) * DK)
                            v = V[:, 2 * b + j, (2 * h + i) * DK:(2 * h + i + 1) * DK]
                            wm = Wm[u % 2][:, i, :]
                            src = wm[:, 0:T] if j == 0 else wm[:, T:BLK]
                            ins = pe.matmul(bank[d, at + j * P:at + T], v, src, start=(b == 0 and j == 0),
                                            stop=(b == 1 and j == 1), skip_group_check=True)
                    ins.then_inc(s_O, 1)

                pe.wait_ge(s_xb, 2 * it + 2)
                proj_qk(0)
                for j in range(8):
                    proj_v(j)
                scores(0)
                for u in range(UN):
                    if u % 2 == 0 and u // 2 + 1 < HP:
                        proj_qk(u // 2 + 1)
                    if u + 1 < UN:
                        scores(u + 1)
                    square(u)
                    if u:
                        output(u - 1)
                output(UN - 1)
                pe.wait_ge(s_OT, HP * it + HP)
                for j in range(2):
                    for t in range(2):
                        for h in range(HP):
                            rows = slice((2 * j + t) * P, (2 * j + t + 1) * P)
                            ins = pe.matmul(PS[:, j, t * P:(t + 1) * P], OT[:, h, rows], wo[:, h, :],
                                            start=(h == 0), stop=(h == HP - 1))
                    ins.then_inc(s_proj, 1)


def attention_block(nc, g, tag, W, cst):
    x, PS = g["x"], g["PS"]
    G, J = 4, 4
    H, DH = 16, 8
    SCALE = DH ** -0.5
    BLK = 3 * P
    with ExitStack() as c:
        def sb(name, shape, dt=F32):
            return c.enter_context(nc.sbuf_tensor(f"{tag}_{name}", shape, dt))

        def sem(name):
            return g["sem"](f"{tag}_{name}")

        pool_norm, act_norm, dve_norm, pe_norm, _, s_xT, _ = layer_norm(nc, g, sb, sem, None, split=False)
        w = sb("w", [P, 4, P])
        wrot = sb("wrot", [P, 2, P])
        cs = sb("cs", [P, 2 * T])
        spread = sb("spread", [P, 4, G, P])
        spreadr = sb("spreadr", [P, 4, G, P], F32R)
        unit = sb("unit", [P, H, P])
        unitr = sb("unitr", [P, H, P], F32R)
        maskf = sb("maskf", [P, 4 * P])
        maskb = sb("maskb", [P, 4 * P], BF16)
        identb = sb("identb", [P, P], BF16)
        xb = [sb(f"xb{i}", [P, T]) for i in range(2)]
        tq = sb("tq", [P, 2, 2 * T])
        qk = sb("qk", [P, 2, T])
        qkhi, qklo = sb("qkhi", [P, 2, T], F32R), sb("qklo", [P, 2, T], F32R)
        S = [sb(f"S{i}", [P, 2, G, T], F32R) for i in range(2)]
        V = [sb(f"V{i}", [P, 2, H, 32]) for i in range(2)]
        nmax = sb("nmax", [P, 2, H])
        nhi = sb("nhi", [P, 2, H], F32R)
        mp = sb("mp", [P, 2, 32])
        mT = [sb(f"mT{i}", [P, BLK], F32R) for i in range(2)]
        PT = sb("PT", [P, G, J, BLK])
        OT = sb("OT", [P, G, T])
        rden = sb("rden", [P, 2, H])
        at = sb("at", [P, 2, P])
        atT = sb("atT", [P, 2, P])

        s_w = sem("s_w")
        s_set = sem("s_set")
        s_setp = sem("s_setp")
        s_xb = sem("s_xb")
        s_proj = sem("s_proj")
        s_v = sem("s_v")
        s_rot = sem("s_rot")
        s_hi = sem("s_hi")
        s_spread = sem("s_spread")
        s_S = sem("s_S")
        s_s1 = sem("s_s1")
        s_mx = sem("s_mx")
        s_mp = sem("s_mp")
        s_mtr = sem("s_mtr")
        s_mT = sem("s_mT")
        s_s2 = sem("s_s2")
        s_p = sem("s_p")
        s_pv = sem("s_pv")
        s_ot = sem("s_ot")
        s_otr = sem("s_otr")
        s_at = sem("s_at")
        s_atr = sem("s_atr")
        s_atT = sem("s_atT")
        s_o = sem("s_o")
        s_res = sem("s_res")
        SETUP = 8
        block = c.enter_context(nc.Block())


        @block.sync
        def _(sp):
            for dst, src in ((w, W), (cs, cst["cs"]), (spread, cst["spread"]), (unit, cst["unit"]), (maskf, cst["mask"])):
                sp.dma_start(dst[:], src).then_inc(s_w, 16)

        @block.gpsimd
        def _(pool):
            pool_norm(pool)
            for i in range(2):
                pool.memset(V[i][:], 0.0).then_inc(s_setp, 1)
            for i in range(2):
                pool.memset(mT[i][:].bitcast(F32), 0.0).then_inc(s_setp, 1)

        @block.scalar
        def _(act):
            def high(m):
                act.wait_ge(s_rot, 3 * m + 2)
                act.activation(qkhi[:], qk[:], ACT.Copy).then_inc(s_hi, 1)

            def split_values(m, i):
                act.wait_ge(s_proj, 2 * m + 2)
                act.activation(V[i][:, :, :, 0:DH], PS[:, 6, 0:T].rearrange("p (t h d) -> p t h d", t=2, d=DH),
                               ACT.Copy).then_inc(s_v, 1)

            def spread_copies(m, i, bs):
                for b in bs:
                    act.wait_ge(s_spread, 4 * m + b + 1)
                    act.activation(S[i][:, b % 2, b // 2 * 2:b // 2 * 2 + 2, :],
                                   PS[:, 7 - b % 2, :].rearrange("p (g t) -> p g t", g=2), ACT.Copy).then_inc(s_S, 1)

            def maxima(m, i):
                act.wait_ge(s_mtr, m + 1)
                act.activation(mT[i][0:32, P:BLK], PS[0:32, 6, 0:T], ACT.Copy).then_inc(s_mT, 1)
                act.activation(mT[i][0:32, 0:P], PS[0:32, 6, P:T], ACT.Copy).then_inc(s_mT, 1)

            def exps(n, bs):
                for b in bs:
                    act.wait_ge(s_s2, 8 * n + b + 1)
                    if not (isinstance(n, int) and n == 0):
                        act.wait_ge(s_pv, 4 * n - 3 + b // 2)
                    gq, j = b // 2, b % 2 * 2
                    act.activation(PT[:, gq, j:j + 2, :], PS[:, j:j + 2, P:W512], ACT.Exp, scale=SCALE).then_inc(s_p, 1)

            def transposed(t):
                act.wait_ge(s_atr, t + 1)
                act.activation(atT[:], PS[:, 4, 0:T].rearrange("p (t q) -> p t q", t=2), ACT.Copy).then_inc(s_atT, 1)

            def turn(n, i, front=True, tail=True):
                exps(n, (0,))
                if front:
                    high(n + 1)
                exps(n, (1,))
                if front:
                    split_values(n + 1, 1 - i)
                exps(n, (2,))
                if tail:
                    transposed(n - 1)
                if front:
                    spread_copies(n + 1, 1 - i, (0, 1))
                exps(n, (3,))
                if front:
                    spread_copies(n + 1, 1 - i, (2, 3))
                exps(n, (4, 5, 6, 7))
                if front:
                    maxima(n + 1, 1 - i)

            act_norm(act)
            act.wait_ge(s_setp, 4)
            act.wait_ge(s_set, SETUP)
            high(0)
            split_values(0, 0)
            spread_copies(0, 0, range(4))
            maxima(0, 0)
            turn(0, 0, tail=False)
            with act.Fori(0, NB // 2 - 1) as pair_of_turns:
                n = 2 * pair_of_turns + 1
                turn(n, 1)
                turn(n + 1, 0)
            turn(NB - 1, 1, front=False)
            transposed(NB - 1)

        @block.vector
        def _(dve):
            def rows_in_place(m, i):
                dve.tensor_copy(xb[i][:], g["xT"][:, m * T:(m + 1) * T] if isinstance(m, int)
                                else g["xT"][:, bass.ds(m * T, T)]).then_inc(s_xb, 1)

            def rotate(m):
                dve.wait_ge(s_proj, 2 * m + 1)
                both = cs[:].unsqueeze(1).to_broadcast([P, 2, 2 * T])
                dve.tensor_tensor(tq[:], PS[:, 6:8, :], both, ALU.mult).then_inc(s_rot, 1)
                dve.wait_ge(s_rot, 3 * m + 1)
                dve.tensor_tensor(qk[:], tq[:, :, 0:T], tq[:, :, T:2 * T], ALU.add).then_inc(s_rot, 1)

            def rests(m):
                dve.wait_ge(s_hi, m + 1)
                dve.tensor_tensor(qklo[:], qk[:], qkhi[:].bitcast(F32), ALU.subtract).then_inc(s_rot, 1)

            def maxima(m, bs):
                for b in bs:
                    qt, a, j = b % 2, b // 8, b // 2 % 4
                    dve.wait_ge(s_s1, 16 * m + b + 1)
                    K = P * (qt + 1)
                    src = PS[:, 6 + b % 2, :].rearrange("p (g k) -> p g k", g=2)[:, :, 0:K]
                    dst = nmax[:, qt, :].rearrange("p (g j) -> p g j", j=J)[:, 2 * a:2 * a + 2, j]
                    dve.tensor_reduce(dst, src, AX.X, ALU.max, negate=True).then_inc(s_mx, 1)

            def pack(m):
                dve.wait_ge(s_mx, 16 * m + 16)
                dve.tensor_copy(nhi[:], nmax[:]).then_inc(s_mp, 1)
                dve.wait_ge(s_mp, 3 * m + 1)
                dve.tensor_copy(mp[:, :, 0:H], nhi[:].bitcast(F32)).then_inc(s_mp, 1)
                dve.tensor_tensor(mp[:, :, H:2 * H], nmax[:], nhi[:].bitcast(F32), ALU.subtract).then_inc(s_mp, 1)

            def weighted_values(n, b):
                dve.wait_ge(s_pv, 4 * n + 2 * b + 2)
                dve.tensor_copy(OT[:, 2 * b:2 * b + 2, :],
                                PS[:, 4 + b, :].rearrange("p (g t) -> p g t", g=2)).then_inc(s_ot, 1)

            def normalised(t):
                for qt in range(2):
                    dve.wait_ge(s_otr, 2 * t + qt + 1)
                    got = PS[:, 4 + qt, :].rearrange("p (h d) -> p h d", d=32)
                    dve.reciprocal(rden[:, qt, :], got[:, :, DH]).then_inc(s_at, 1)
                    dve.wait_ge(s_at, 4 * t + 2 * qt + 1)
                    dve.tensor_tensor(at[:, qt, :].rearrange("p (h d) -> p h d", d=DH), got[:, :, 0:DH],
                                      rden[:, qt, :].unsqueeze(2).to_broadcast([P, H, DH]),
                                      ALU.mult).then_inc(s_at, 1)

            def residual(t):
                dve.wait_ge(s_o, t + 1)
                rows = x[:, bass.ds(2 * t, 2), :]
                dve.tensor_tensor(rows, rows, PS[:, 5, 0:T].rearrange("p (t d) -> p t d", t=2),
                                  ALU.add).then_inc(s_res, 1)

            def turn(n, i, front=True, tail=True):
                if front:
                    rows_in_place(n + 1, 1 - i)
                    rotate(n + 1)
                if tail:
                    normalised(n - 1)
                if front:
                    rests(n + 1)
                if tail:
                    residual(n - 1)
                if front:
                    maxima(n + 1, range(10))
                weighted_values(n, 0)
                if front:
                    maxima(n + 1, range(10, 16))
                    pack(n + 1)
                weighted_values(n, 1)

            dve_norm(dve)
            dve.wait_ge(s_w, 80)
            dve.wait_ge(s_setp, 4)
            for i in range(2):
                pair = w[:, i, :].rearrange("p (h two) -> p h two", two=2)
                rot = wrot[:, i, :].rearrange("p (h two) -> p h two", two=2)
                dve.tensor_scalar(rot[:, :, 0], pair[:, :, 1], -1.0, None, ALU.mult)
                dve.tensor_copy(rot[:, :, 1], pair[:, :, 0]).then_inc(s_set, 1)
            dve.tensor_copy(spreadr[:], spread[:]).then_inc(s_set, 1)
            dve.tensor_copy(unitr[:], unit[:]).then_inc(s_set, 1)
            dve.tensor_copy(maskb[:], maskf[:]).then_inc(s_set, 1)
            dve.tensor_copy(identb[:], g["ident"][:]).then_inc(s_set, 1)
            for i in range(2):
                dve.memset(V[i][:, :, :, DH:DH + 1], 1.0).then_inc(s_set, 1)
            dve.wait_ge(s_xT, NC)
            rows_in_place(0, 0)
            rotate(0)
            rests(0)
            maxima(0, range(16))
            pack(0)
            turn(0, 0, tail=False)
            with dve.Fori(0, NB // 2 - 1) as pair_of_turns:
                n = 2 * pair_of_turns + 1
                turn(n, 1)
                turn(n + 1, 0)
            turn(NB - 1, 1, front=False)
            normalised(NB - 1)
            residual(NB - 1)

        @block.tensor
        def _(pe):
            def project(m):
                cols = bass.ds(m * T, T)
                for p in (1, 0):
                    if p == 0 and not (isinstance(m, int) and m == 0):
                        pe.wait_ge(s_mT, 2 * m)
                    pe.matmul(PS[:, 6 + p, 0:T], w[:, p, :], g["xT"][:, cols], start=True, stop=True)
                    ins = pe.matmul(PS[:, 6 + p, T:2 * T], wrot[:, p, :], g["xT"][:, cols], start=True, stop=True)
                ins.then_inc(s_proj, 1)

            def project_v(m, i):
                pe.wait_ge(s_xb, m + 1)
                pe.wait_ge(s_rot, 3 * m + 1)
                for t in range(2):
                    ins = pe.matmul(PS[:, 6, t * P:(t + 1) * P], xb[i][:, t * P:(t + 1) * P], w[:, 2, :],
                                    start=True, stop=True)
                ins.then_inc(s_proj, 1)

            def spread_out(m, bs):
                pe.wait_ge(s_rot, 3 * m + 3)
                for b in bs:
                    if b == 1:
                        pe.wait_ge(s_v, m + 1)
                    elif b >= 2:
                        pe.wait_ge(s_S, 4 * m + b - 1)
                    for e in range(2):
                        p, gr = b % 2, b // 2 * 2 + e
                        dst = PS[:, 7 - b % 2, e * T:(e + 1) * T]
                        pe.matmul(dst, spreadr[:, 2 * p, gr, :], qkhi[:, p, :], start=True, stop=False)
                        ins = pe.matmul(dst, spreadr[:, 2 * p + 1, gr, :], qklo[:, p, :], start=False, stop=True)
                    ins.then_inc(s_spread, 1)

            def scores_down(m, i, bs):
                for b in bs:
                    qt, a, j = b % 2, b // 8, b // 2 % 4
                    if b < 2:
                        pe.wait_ge(s_S, 4 * m + 4)
                    else:
                        pe.wait_ge(s_mx, 16 * m + b - 1)
                    bank, r = 6 + b % 2, slice(32 * j, 32 * j + 32)
                    diag = PS[:, bank, :].rearrange("p (e k) -> p e k", e=2)[:, :, qt * P:(qt + 1) * P]
                    pe.matmul(diag, identb[:], maskb[:, 0:2 * P].rearrange("p (e k) -> p e k", e=2),
                              start=True, stop=False, skip_group_check=True)
                    for e in range(2):
                        gr = 2 * a + e
                        ins = pe.matmul(PS[:, bank, e * T:(e + 1) * T], S[i][r, 0, gr, qt * P:(qt + 1) * P],
                                        S[i][r, 1, gr, :], start=False, stop=True, skip_group_check=True)
                    ins.then_inc(s_s1, 1)

            def maxima(m):
                pe.wait_ge(s_mp, 3 * m + 3)
                for t in range(2):
                    ins = pe.transpose(PS[0:32, 6, t * P:(t + 1) * P], mp[:, t, :], g["ident"][:])
                ins.then_inc(s_mtr, 1)

            def scores(n, i, b):
                gr = b // 2
                if b == 0:
                    pe.wait_ge(s_mT, 2 * n + 2)
                if not (isinstance(n, int) and n == 0 and b < 2):
                    pe.wait_ge(s_p, 8 * n + b - 1)
                for e in range(2):
                    j = b % 2 * 2 + e
                    pe.matmul(PS[:, j, P:W512], unitr[:, 4 * gr + j, :], mT[i][:], start=True, stop=False,
                              skip_group_check=True)
                    pe.matmul(PS[:, j, P:3 * P], identb[:], maskb[:, 2 * P:4 * P], start=False, stop=False,
                              skip_group_check=True)
                for e in range(2):
                    j = b % 2 * 2 + e
                    r = slice(32 * j, 32 * j + 32)
                    pe.matmul(PS[:, j, 0:T], S[i][r, 1, gr, P:T], S[i][r, 0, gr, :],
                              start=False, stop=True, skip_group_check=True)
                    ins = pe.matmul(PS[:, j, T:2 * T], S[i][r, 1, gr, 0:P], S[i][r, 0, gr, :],
                                    start=False, stop=True, skip_group_check=True)
                ins.then_inc(s_s2, 1)

            def values(n, i, gr):
                pe.wait_ge(s_p, 8 * n + 2 * gr + 2)
                if gr % 2 == 0 and not (isinstance(n, int) and n == 0):
                    pe.wait_ge(s_res if gr else s_atT, n)
                for k in range(2):
                    for j in range(J):
                        dst = PS[32 * j:32 * j + 32, 4 + gr // 2, gr % 2 * T + k * P:(gr % 2 + 1) * T]
                        src = PT[:, gr, j, P:BLK] if k == 0 else PT[:, gr, j, 0:P]
                        ins = pe.matmul(dst, V[i][:, k, 4 * gr + j, :], src, start=(gr % 2 == 0 and k == 0),
                                        stop=(k == 1), skip_group_check=True)
                ins.then_inc(s_pv, 1)

            def token_major(t):
                pe.wait_ge(s_ot, 2 * t + 2)
                for qt in range(2):
                    for gr in range(G):
                        ins = pe.transpose(PS[:, 4 + qt, gr * P:(gr + 1) * P], OT[:, gr, qt * P:(qt + 1) * P],
                                           g["ident"][:])
                    ins.then_inc(s_otr, 1)

            def transposed(t):
                pe.wait_ge(s_at, 4 * t + 4)
                for qt in range(2):
                    ins = pe.transpose(PS[:, 4, qt * P:(qt + 1) * P], at[:, qt, :], g["ident"][:])
                ins.then_inc(s_atr, 1)

            def output(t):
                pe.wait_ge(s_atT, t + 1)
                for qt in range(2):
                    ins = pe.matmul(PS[:, 5, qt * P:(qt + 1) * P], atT[:, qt, :], w[:, 3, :], start=True, stop=True)
                ins.then_inc(s_o, 1)

            def turn(n, i, front=True, tail=True):
                if front:
                    project(n + 1)
                scores(n, i, 0)
                if tail:
                    token_major(n - 1)
                scores(n, i, 1)
                if front:
                    project_v(n + 1, 1 - i)
                scores(n, i, 2)
                if tail:
                    transposed(n - 1)
                if front:
                    spread_out(n + 1, (0, 1))
                scores(n, i, 3)
                if tail:
                    output(n - 1)
                if front:
                    spread_out(n + 1, (2, 3))
                values(n, i, 0)
                for bs, after in ((range(0, 2), lambda: scores(n, i, 4)), (range(2, 6), lambda: scores(n, i, 5)),
                                  (range(6, 8), lambda: values(n, i, 1)), (range(8, 10), lambda: scores(n, i, 6)),
                                  (range(10, 12), lambda: scores(n, i, 7)), (range(12, 16), lambda: values(n, i, 2))):
                    if front:
                        scores_down(n + 1, 1 - i, bs)
                    after()
                values(n, i, 3)
                if front:
                    maxima(n + 1)

            pe_norm(pe)
            pe.wait_ge(s_set, SETUP)
            pe.wait_ge(s_setp, 4)
            pe.wait_ge(s_xT, NC)
            project(0)
            project_v(0, 0)
            spread_out(0, range(4))
            scores_down(0, 0, range(16))
            maxima(0)
            turn(0, 0, tail=False)
            with pe.Fori(0, NB // 2 - 1) as pair_of_turns:
                n = 2 * pair_of_turns + 1
                turn(n, 1)
                turn(n + 1, 0)
            turn(NB - 1, 1, front=False)
            token_major(NB - 1)
            transposed(NB - 1)
            output(NB - 1)


def macaron(nc, a, out, stages=6):
    with ExitStack() as ctx:
        def sb(name, shape, dt=F32):
            return ctx.enter_context(nc.sbuf_tensor(name, shape, dt))

        g = {
            "x": sb("x", [P, NT, P]), "xr": sb("xr", [P, NT, P]), "xT": sb("xT", [P, TOK]),
            "xhi": sb("xhi", [P, TOK], F32R), "xlo": sb("xlo", [P, TOK], F32R),
            "wT": sb("wT", [32, TOK], F32R), "fscale": sb("fscale", [P, NT]),
            "PS": ctx.enter_context(nc.psum_tensor("PS", [P, 8, W512], F32)),
        }
        small = {"ident": [P, P], "strict": [P, P], "ones": [P, P], "tri": [P, 3 * P], "before": [P, NE * NE],
                 "gate_b": [P, NE], "routerA": [P, NE], "routerB": [P, NE], "b2B": [32, P]}
        for name, shape in small.items():
            g[name] = sb(name, shape)
        s_in = ctx.enter_context(nc.semaphore("s_in"))
        s_out = ctx.enter_context(nc.semaphore("s_out"))
        tokens = "(t p) d -> p t d"
        held = []

        def sem(name):
            held.append(nc.alloc_semaphore(name))
            return held[-1]

        g["sem"] = sem

        with nc.Block() as block:
            @block.sync
            def _(sp):
                sp.dma_start(g["x"][:], a["x"].rearrange(tokens, p=P)).then_inc(s_in, 16)
                for name in small:
                    sp.dma_start(g[name][:], a[name]).then_inc(s_in, 16)
                sp.wait_ge(s_in, 16 * (len(small) + 1))

        def mixture(kind, tag):
            mixture_block(nc, g, tag, kind, a["mix" + kind])

        def hla():
            normalise(nc, g, "hn")
            hla_block(nc, g, "h", {n: a["hla_w" + n] for n in "qkvo"})

        def attention():
            attention_block(nc, g, "a", a["att_w"], {"cs": a["cs"], "spread": a["spread"], "unit": a["unit"], "mask": a["mask"]})

        order = [lambda: mixture("A", "m1"), hla, lambda: mixture("A", "m2"), lambda: mixture("B", "m3"),
                 attention, lambda: mixture("B", "m4")]
        if isinstance(stages, int):
            stages = range(stages)
        for s in stages:
            if s == 3:
                nc.clear_and_free_semaphores(held)
                held.clear()
                nc.all_engine_barrier()
            order[s]()
        with nc.Block() as block:
            @block.sync
            def _(sp):
                sp.dma_start(out.rearrange(tokens, p=P), g["x"][:]).then_inc(s_out, 16)
                sp.wait_ge(s_out, 16)


def _constants():
    import numpy as np
    i = np.arange(P)
    f = np.float32
    H, DH = 16, 8
    le = (i[:, None] <= i[None, :]).astype(f)
    one = np.ones((P, P), f)
    off = f(-1e30)
    later = np.where(i[:, None] < i[None, :], off, f(0))
    laterT = later.T.copy()
    j = np.arange(NE)
    c = {
        "ident": np.eye(P, dtype=f), "strict": (i[:, None] < i[None, :]).astype(f), "ones": one,
        "tri": np.concatenate([le, one, le], 1),
        "before": np.tile((j[None, :] < j[:, None]).astype(f).reshape(1, -1), (P, 1)),
        "mask": np.concatenate([later, later, laterT, laterT], 1),
    }
    theta = (10000.0 ** (-2.0 * np.arange(DH // 2, dtype=f) / DH)).astype(f)
    angles = (np.arange(T, dtype=f)[:, None] * theta[None, :]).astype(f)
    per_row = angles[:, (i % DH) // 2].T
    c["cs"] = np.concatenate([np.cos(per_row), np.sin(per_row)], 1).astype(f)
    spread = np.zeros((P, 4, 4, P), f)
    for part, terms in enumerate(((0, 1), (2, 3), (0, 2), (1, 3))):
        for gr in range(4):
            for jj in range(4):
                for term in terms:
                    for d in range(DH):
                        spread[(4 * gr + jj) * DH + d, part, gr, 32 * jj + 8 * term + d] = 1
    c["spread"] = spread
    unit = np.zeros((P, H, P), f)
    for h in range(H):
        unit[h, h] = 1
        unit[H + h, h] = 1
    c["unit"] = unit
    return c


def _layout(inputs):
    import numpy as np
    v = {k: np.asarray(z) for k, z in inputs.items()}
    f = np.float32
    a = _constants()
    a["x"] = v["L0_attn_x"].reshape(TOK, P)
    a["gate_b"] = np.repeat(v["L1_ffn_gate_b"][None], P, 0)
    a["routerA"], a["routerB"] = v["L0_ffn_Wr"], v["L1_ffn_gate_w"]
    chosen = np.zeros((SEQ, P, 1), f)
    for n in range(SEQ):
        chosen[n, n] = chosen[n, 16 + n] = 1
    FA = v["L0_ffn_Wg"].shape[2]
    mixA = np.zeros((SEQ, P, 4 * P + FA + MISC), f)
    mixA[1:, :, 0:FA] = v["L0_ffn_Wg"]
    mixA[1:, :, FA:2 * FA] = v["L0_ffn_Wu"]
    mixA[1:, :, 4 * P:4 * P + FA] = v["L0_ffn_Wd"].reshape(NE, 2, P, P).transpose(0, 2, 1, 3).reshape(NE, P, FA)
    mixA[1:, :, -8] = v["L0_ffn_norm_w"]
    F4 = v["L0_ffn_fWg"].shape[1]
    mixA[0, :, 0:F4] = v["L0_ffn_fWg"]
    mixA[0, :, FA:FA + F4] = v["L0_ffn_fWu"]
    mixA[0, 0:F4, 4 * P:5 * P] = v["L0_ffn_fWd"]
    mixA[0, :, -8] = v["L0_ffn_f_norm"]
    mixA[:, :, -7:-6] = chosen
    a["mixA"] = mixA
    w1 = np.concatenate([v["L1_ffn_sh_w1"][None], v["L1_ffn_ew1"]], 0)
    w2 = np.concatenate([v["L1_ffn_sh_w2"][None], v["L1_ffn_ew2"]], 0)
    b1 = np.concatenate([v["L1_ffn_sh_b1"][None], v["L1_ffn_eb1"]], 0)
    b2 = np.concatenate([v["L1_ffn_sh_b2"][None], v["L1_ffn_eb2"]], 0)
    mixB = np.zeros((SEQ, P, 8 * P + MISC), f)
    mixB[:, :, 0:4 * P] = w1
    mixB[:, :, 4 * P:8 * P] = w2.reshape(SEQ, 4, P, P).transpose(0, 2, 1, 3).reshape(SEQ, P, 4 * P)
    mixB[:, :, -6:-2] = b1.reshape(SEQ, 4, P).transpose(0, 2, 1)
    mixB[:, :, -7:-6] = chosen
    a["mixB"] = mixB
    b2B = np.zeros((32, P), f)
    b2B[0:SEQ] = b2
    b2B[16:16 + SEQ] = b2
    a["b2B"] = b2B
    for n in "qkv":
        a["hla_w" + n] = v["L0_attn_W_" + n]
    a["hla_wo"] = v["L0_attn_W_o"].reshape(8, P, P).transpose(1, 0, 2)
    a["att_w"] = np.stack([v["L1_attn_W_" + n].T for n in "qkvo"], 1)
    return {k: np.ascontiguousarray(z) for k, z in a.items()}


def kernel(**inputs):
    import numpy as _np
    import concourse.bacc as _bacc
    from concourse import mybir as _mybir
    from concourse.bass_utils import run_bass_kernel_spmd as _run

    nc = _bacc.Bacc("TRN2", target_bir_lowering=False, num_devices=1)
    arrays = {f"in_{k}": z for k, z in _layout(inputs).items()}
    args = {k[3:]: nc.dram_tensor(k, z.shape, _mybir.dt.from_np(z.dtype), kind="ExternalInput").ap()
            for k, z in arrays.items()}
    out = nc.dram_tensor("out", (TOK, P), _mybir.dt.float32, kind="ExternalOutput").ap()
    macaron(nc, args, out)
    r = _run(nc, [arrays], core_ids=[0])
    return r.results[0]["out"].reshape(NB, T, P)
```

```python
from contextlib import ExitStack

import concourse.bass as bass
from concourse import mybir

F32 = mybir.dt.float32
F32R = mybir.dt.float32r
BF16 = mybir.dt.bfloat16
ALU = mybir.AluOpType
ACT = mybir.ActivationFunctionType
AX = mybir.AxisListType

P = 128
NB, T = 8, 256
NT = NB * T // P
TOK = NB * T
W512 = 512
NC = TOK // W512
NE = 8
SEQ = NE + 1
CAP = 512
NM = 4
MISC = 8
LN_EPS = 1e-5
RMS_EPS = 1e-6


def layer_norm(nc, g, sb, sem, mixture, split=True):
    x, xr, PS = g["x"], g["xr"], g["PS"]
    st = g["st"]
    stats = not g["have_moments"]
    g["have_moments"] = True
    mean, diff, m2, var, ms = (sb(n, [P, NT]) for n in ("mean", "diff", "m2", "var", "ms"))
    sd, rstd, rms, rrms, scl = (sb(n, [P, NT]) for n in ("sd", "rstd", "rms", "rrms", "scl"))
    eps_ln, eps_rms, warm = sb("eps_ln", [P, 1]), sb("eps_rms", [P, 1]), sb("warm", [P, 1])
    s_eps = sem("s_eps")
    s_warm = sem("s_warm")
    s_var = sem("s_var")
    s_sd = sem("s_sd")
    s_ln = sem("s_ln")
    s_xr = sem("s_xr")
    s_tr = sem("s_tr")
    s_xT = sem("s_xT")
    s_xlo = sem("s_xlo")

    def pool_part(pool):
        pool.memset(eps_ln[:], LN_EPS).then_inc(s_eps, 1)
        pool.memset(eps_rms[:], RMS_EPS).then_inc(s_eps, 1)

    def act_part(act):
        act.wait_ge(s_eps, 2)
        act.activation(warm[:], eps_ln[:], ACT.Sqrt).then_inc(s_warm, 1)
        act.wait_ge(s_var, 1)
        act.activation(sd[:], var[:], ACT.Sqrt, bias=eps_ln[:]).then_inc(s_sd, 1)
        if mixture == "A":
            act.wait_ge(s_var, 2)
            act.activation(rms[:], ms[:], ACT.Sqrt, bias=eps_rms[:]).then_inc(s_sd, 1)
        for k in range(NC):
            cols = slice(k * W512, (k + 1) * W512)
            act.wait_ge(s_tr, k + 1)
            act.activation(g["xT"][:, cols], PS[:, k, :], ACT.Copy).then_inc(s_xT, 1)
            if split:
                act.activation(g["xhi"][:, cols], PS[:, k, :], ACT.Copy).then_inc(s_xT, 1)

    def dve_part(dve):
        n = [0]

        def then(ins):
            n[0] += 1
            ins.then_inc(s_ln, 1)
            dve.wait_ge(s_ln, n[0])

        if stats:
            for t in range(NT - 1):
                dve.bn_stats(st[:, t, :], x[:, t, :])
            then(dve.bn_stats(st[:, NT - 1, :], x[:, NT - 1, :]))
        dve.tensor_tensor(mean[:], st[:, :, 1], st[:, :, 4], ALU.add)
        dve.tensor_tensor(m2[:], st[:, :, 2], st[:, :, 5], ALU.add)
        then(dve.tensor_tensor(diff[:], st[:, :, 1], st[:, :, 4], ALU.subtract))
        then(dve.tensor_tensor(diff[:], diff[:], diff[:], ALU.mult))
        then(dve.scalar_tensor_tensor(out=m2[:], in0=diff[:], scalar=P / 4.0, in1=m2[:],
                                      op0=ALU.mult, op1=ALU.add))
        dve.tensor_scalar(var[:], m2[:], 1.0 / P, None, ALU.mult).then_inc(s_var, 1)
        then(dve.tensor_scalar(mean[:], mean[:], 0.5, None, ALU.mult))
        dve.wait_ge(s_sd, 1)
        then(dve.reciprocal(rstd[:], sd[:]))
        row_scale = rstd
        if mixture == "A":
            then(dve.tensor_tensor(ms[:], rstd[:], rstd[:], ALU.mult))
            dve.tensor_tensor(ms[:], ms[:], var[:], ALU.mult).then_inc(s_var, 1)
            dve.wait_ge(s_sd, 2)
            then(dve.reciprocal(rrms[:], rms[:]))
            then(dve.tensor_tensor(scl[:], rrms[:], rstd[:], ALU.mult))
            row_scale = scl

        def low(k):
            cols = slice(k * W512, (k + 1) * W512)
            dve.wait_ge(s_xT, 2 * (k + 1))
            dve.tensor_tensor(g["xlo"][:, cols], g["xT"][:, cols], g["xhi"][:, cols].bitcast(F32),
                              ALU.subtract).then_inc(s_xlo, 1)

        for t in range(NT):
            dve.tensor_scalar(xr[:, t, :], x[:, t, :], mean[:, t:t + 1], row_scale[:, t:t + 1],
                              ALU.subtract, ALU.mult).then_inc(s_xr, 1)
            if split and t % 4 == 3 and t > 8:
                low(t // 4 - 2)
        if split:
            low(NC - 2)
            low(NC - 1)

    def pe_part(pe):
        for t in range(NT):
            pe.wait_ge(s_xr, t + 1)
            ins = pe.transpose(PS[:, t // 4, (t % 4) * P:(t % 4 + 1) * P], xr[:, t, :], g["ident"][:])
            if t % 4 == 3:
                ins.then_inc(s_tr, 1)

    return pool_part, act_part, dve_part, pe_part, rms, s_xT, s_xlo


def moments(dve, g, first, count):
    for t in range(count):
        dve.bn_stats(g["st"][:, bass.ds(first + t, 1), :].rearrange("p a s -> p (a s)"),
                     g["x"][:, bass.ds(first + t, 1), :].rearrange("p a d -> p (a d)"))


def mixture_block(nc, g, tag, kind, weights, out=None):
    x, xr, PS = g["x"], g["xr"], g["PS"]
    A = kind == "A"
    NF = 2 if A else 4
    NF0 = 1 if A else 4
    QF = 2 if A else 1
    UP = NM * P
    WC = UP + NF * P + MISC
    LAST = SEQ - 1
    with ExitStack() as c:
        def sb(name, shape, dt=F32):
            return c.enter_context(nc.sbuf_tensor(f"{tag}_{name}", shape, dt))

        def sem(name):
            return g["sem"](f"{tag}_{name}")

        pool_norm, act_norm, dve_norm, pe_norm, rms, s_xT, s_xlo = layer_norm(nc, g, sb, sem, kind)
        lg, ex, pr, top, sel, rank = (sb(n, [P, NT, NE]) for n in ("lg", "ex", "pr", "top", "sel", "rank"))
        mx, sm, rs = (sb(n, [P, NT]) for n in ("mx", "sm", "rs"))
        tot, tmp = sb("tot", [P, NT, NE]), sb("tmp", [P, NT, NE])
        wfull = sb("wfull", [P, NT, 16])
        whi = sb("whi", [P, NT, 16], F32R)
        wpack = sb("wpack", [P, NT, 32])
        raw = [sb(f"raw{i}", [P, WC]) for i in range(2)]
        scaled = sb("scaled", [P, UP]) if A else None
        uphi = [sb(f"uphi{i}", [P, UP], F32R) for i in range(2)]
        uplo = [sb(f"uplo{i}", [P, UP], F32R) for i in range(2)]
        dnhi = [sb(f"dnhi{i}", [P, NF * P], F32R) for i in range(2)]
        dnlo = [sb(f"dnlo{i}", [P, NF * P], F32R) for i in range(2)]
        pick = [sb(f"pick{i}", [32, P], F32R) for i in range(4)]
        wrow = [sb(f"wrow{i}", [P, TOK]) for i in range(3)]
        gate = [sb(f"gate{i}", [P, NF, W512]) for i in range(2)] if A else None
        hid = [sb(f"hid{i}", [P, NF, W512]) for i in range(2)]
        hhi = [sb(f"hhi{i}", [P, NF, W512], F32R) for i in range(2)]
        hlo = [sb(f"hlo{i}", [P, NF, W512], F32R) for i in range(2)]
        part = [sb(f"part{i}", [P, W512]) for i in range(2)]
        acc = sb("acc", [P, TOK])
        kept = sb("kept", [P, TOK])
        half = sb("half", [P, 1])

        s_raw = [sem(f"s_raw{i}") for i in range(2)]
        s_clear = sem("s_clear")
        s_split = sem("s_split")
        s_logit = sem("s_logit")
        s_rt = sem("s_rt")
        s_lmax = sem("s_lmax")
        s_ex = sem("s_ex")
        s_sel = sem("s_sel")
        s_cum = sem("s_cum")
        s_wp = sem("s_wp")
        s_wtr = sem("s_wtr")
        s_wT = sem("s_wT")
        s_row = sem("s_row")
        s_rowc = sem("s_rowc")
        s_ring = sem("s_ring")
        s_gelu = sem("s_gelu")
        s_gu = sem("s_gu")
        s_hhi = sem("s_hhi")
        s_lo = sem("s_lo")
        s_down = sem("s_down")
        s_part = sem("s_part")
        s_acc = sem("s_acc")
        s_comb = sem("s_comb")
        s_skip = sem("s_skip")
        s_back = sem("s_back")
        s_fin = sem("s_fin")
        s_out = sem("s_out")
        SPLIT = 6 if A else 5
        n_first, n_second = (1, 2) if A else (2, 1)
        block = c.enter_context(nc.Block())

        def banks(n):
            return QF * feats(n)

        def feats(n):
            return 0 if isinstance(n, int) and n == 0 else NC * NF0 + (n - 1) * (NC * NF)

        def low(engine, n, k):
            first = isinstance(n, int) and n == 0
            nf = NF0 if first else NF
            if not (first and k < 2):
                engine.wait_ge(s_down, 4 * n + k - 1)
            for m in range(nf):
                engine.wait_ge(s_hhi if A else s_gelu, feats(n) + nf * k + m + 1)
                engine.tensor_tensor(hlo[k % 2][:, m, :], hid[k % 2][:, m, :], hhi[k % 2][:, m, :].bitcast(F32),
                                     ALU.subtract).then_inc(s_lo, 1)

        @block.sync
        def _(sp):
            def load(n, i):
                sp.dma_start(raw[i][:], weights[bass.ds(n, 1)].rearrange("a p c -> (a p) c")).then_inc(s_raw[i], 16)

            load(0, 0)
            load(1, 1)
            with sp.Fori(2, LAST, 2) as n:
                sp.wait_ge(s_down, 4 * n - 4)
                load(n, 0)
                sp.wait_ge(s_down, 4 * n)
                load(n + 1, 1)
            sp.wait_ge(s_down, 4 * LAST - 4)
            load(LAST, 0)
            if out is not None:
                for k in range(NC):
                    sp.wait_ge(s_fin, k + 1)
                    sp.dma_start(out[:, 4 * k:4 * k + 4, :], x[:, 4 * k:4 * k + 4, :]).then_inc(s_out, 16)
                sp.wait_ge(s_out, 16 * NC)

        @block.gpsimd
        def _(pool):
            one = g["ones"][:, 0:1]

            def split(n, i, reused):
                at = n * SPLIT
                pool.wait_ge(s_raw[i], 8 * n + (16 if i == 0 else 8))
                if reused:
                    pool.wait_ge(s_down, 4 * n - 4)
                dst = pick[2 + n] if isinstance(n, int) and n < 2 else pick[i]
                pool.tensor_tensor(dst[:], g["ones"][0:32, :], raw[i][0:32, WC - 7:WC - 6].to_broadcast([32, P]),
                                   ALU.mult).then_inc(s_split, 1)
                src = raw[i][:, 0:UP]
                if A:
                    norm = raw[i][:, WC - 8:WC - 7].to_broadcast([P, UP])
                    pool.tensor_tensor(uphi[i][:], src, norm, ALU.mult).then_inc(s_split, 1)
                    pool.tensor_tensor(scaled[:], src, norm, ALU.mult).then_inc(s_split, 1)
                    src = scaled[:]
                else:
                    pool.tensor_tensor(uphi[i][:], src, one.to_broadcast([P, UP]), ALU.mult).then_inc(s_split, 1)
                dn = raw[i][:, UP:UP + NF * P]
                pool.tensor_tensor(dnhi[i][:], dn, one.to_broadcast([P, NF * P]), ALU.mult).then_inc(s_split, 1)
                pool.wait_ge(s_split, at + SPLIT - 2)
                pool.tensor_tensor(uplo[i][:], src, uphi[i][:].bitcast(F32), ALU.subtract).then_inc(s_split, 1)
                pool.tensor_tensor(dnlo[i][:], dn, dnhi[i][:].bitcast(F32), ALU.subtract).then_inc(s_split, 1)
                if A:
                    pool.wait_ge(s_split, at + SPLIT - 1)

            def weigh_acc(k, cols):
                pool.wait_ge(s_part, 4 + k + 1)
                pool.wait_ge(s_rowc, k + 1)
                pool.tensor_tensor(acc[:, cols], acc[:, cols], wrow[1][:, cols], ALU.mult).then_inc(s_comb, 1)

            def add_kept(k, cols):
                pool.wait_ge(s_part, 4 + k + 1)
                pool.wait_ge(s_rowc, (8 if A else 0) + k + 1)
                pool.tensor_tensor(kept[:, cols], kept[:, cols], wrow[2 if A else 1][:, cols],
                                   ALU.mult).then_inc(s_comb, 1)
                if A:
                    pool.wait_ge(s_comb, 4 + 2 * k + 1)
                    pool.wait_ge(s_acc, 4 + k)
                else:
                    pool.wait_ge(s_comb, 2 * k + 1)
                pool.tensor_tensor(acc[:, cols], acc[:, cols], kept[:, cols], ALU.add).then_inc(s_comb, 1)

            def add_bias(k, cols):
                pool.wait_ge(s_rowc, 8 + k + 1)
                pool.wait_ge(s_acc, 4 + k)
                pool.tensor_tensor(acc[:, cols], acc[:, cols], wrow[2][:, cols], ALU.add).then_inc(s_comb, 1)

            def add_rows(k, cols):
                tiles = slice(4 * k, 4 * k + 4)
                by = (g["fscale"][:, tiles].unsqueeze(2) if A else half[:].unsqueeze(2)).to_broadcast([P, 4, P])
                pool.tensor_tensor(xr[:, tiles, :], xr[:, tiles, :], by, ALU.mult).then_inc(s_skip, 1)
                pool.wait_ge(s_skip, 2 * k + 1)
                pool.tensor_tensor(x[:, tiles, :], x[:, tiles, :], xr[:, tiles, :], ALU.add).then_inc(s_skip, 1)

            first_extra, second_extra = (weigh_acc, add_kept) if A else (add_kept, add_bias)

            def add(n, extra=None, count=0):
                for k in range(NC):
                    cols = slice(k * W512, (k + 1) * W512)
                    if extra:
                        extra(k, cols)
                    pool.wait_ge(s_part, 4 * n + k + 1)
                    if count:
                        pool.wait_ge(s_comb, (0 if n == 2 else 4 * n_first) + count * (k + 1))
                    if not (isinstance(n, int) and n == 2 and k == 0):
                        pool.wait_ge(s_acc, 4 * n - 8 + k)
                    pool.tensor_tensor(acc[:, cols], acc[:, cols], part[k % 2][:], ALU.add).then_inc(s_acc, 1)

            pool_norm(pool)
            pool.memset(wfull[:], 0.0).then_inc(s_clear, 1)
            pool.memset(half[:], 0.5).then_inc(s_clear, 1)
            split(0, 0, False)
            split(1, 1, False)
            if A:
                for k in range(NC):
                    low(pool, 0, k)
                low(pool, 1, 0)
            split(2, 0, True)
            split(3, 1, True)
            add(2, first_extra, n_first)
            split(4, 0, True)
            add(3, second_extra, n_second)
            with pool.Fori(5, LAST, 2) as n:
                split(n, 1, True)
                add(n - 1)
                split(n + 1, 0, True)
                add(n)
            add(LAST, add_rows)

        @block.tensor
        def _(pe):
            def group(k):
                return slice(k * W512, (k + 1) * W512)

            def up(n, i, k):
                nf = NF0 if isinstance(n, int) and n == 0 else NF
                if k == 0:
                    pe.wait_ge(s_split, n * SPLIT + SPLIT)
                if isinstance(n, int) and n == 0:
                    pe.wait_ge(s_xlo, k + 1)
                for m in range(QF * nf):
                    q = QF * nf * k + m
                    if not (isinstance(n, int) and n == 0 and q < 4):
                        if not A:
                            pe.wait_ge(s_gelu, feats(n) + q - 3)
                        elif q % 2 == 0:
                            pe.wait_ge(s_gelu, feats(n) + (q - 4) // 2 + 1)
                        else:
                            pe.wait_ge(s_gu, feats(n) + (q - 4) // 2 + 1)
                    f = (m // 2 + 2 * (m % 2)) if A else m
                    w, bank = slice(f * P, (f + 1) * P), PS[:, 4 + q % 4, :]
                    pe.matmul(bank, uphi[i][:, w], g["xhi"][:, group(k)], start=True, stop=False)
                    pe.matmul(bank, uphi[i][:, w], g["xlo"][:, group(k)], start=False, stop=False)
                    pe.matmul(bank, uplo[i][:, w], g["xhi"][:, group(k)], start=False, stop=True).then_inc(s_ring, 1)

            def down(n, i, k):
                first = isinstance(n, int) and n == 0
                nf = NF0 if first else NF
                pe.wait_ge(s_lo, feats(n) + nf * (k + 1))
                if not (first and k < 2):
                    pe.wait_ge(s_part, 4 * n + k - 1)
                for f in range(nf):
                    w, bank = slice(f * P, (f + 1) * P), PS[:, k % 2, :]
                    pe.matmul(bank, dnhi[i][:, w], hhi[k % 2][:, f, :], start=f == 0, stop=False)
                    pe.matmul(bank, dnlo[i][:, w], hhi[k % 2][:, f, :], start=False, stop=False)
                    ins = pe.matmul(bank, dnhi[i][:, w], hlo[k % 2][:, f, :], start=False, stop=f == nf - 1)
                ins.then_inc(s_down, 1)

            def rows(at, which, ks):
                for k in ks:
                    if not (isinstance(at, int) and at == 0 and k < 2):
                        pe.wait_ge(s_rowc, at + k - 1)
                    pe.matmul(PS[:, 2 + k % 2, :], which[:], g["wT"][:, group(k)], start=True, stop=True).then_inc(s_row, 1)

            def first_rows(ks):
                if A:
                    return rows(8, pick[2], ks)
                for k in ks:
                    pe.wait_ge(s_rowc, 8 + k - 1)
                    pe.matmul(PS[:, 2 + k % 2, :], g["b2B"][:], g["wT"][:, group(k)].bitcast(F32),
                              start=True, stop=True).then_inc(s_row, 1)

            def one_pass(n, i, last=False):
                up(n, i, 0)
                down(n - 1, 1 - i, NC - 1)
                rows(4 * n, pick[i], (0, 1))
                for k in range(1, NC):
                    up(n, i, k)
                    if k == 1:
                        rows(4 * n, pick[i], (2, 3))
                    down(n, i, k - 1)
                    if last and k > 1:
                        back(k - 2)

            def back(k):
                pe.wait_ge(s_acc, 4 * LAST - 7 + k)
                pe.wait_ge(s_rowc, 4 * LAST + NC)
                if k >= 2:
                    pe.wait_ge(s_fin, k - 1)
                for t in range(4):
                    ins = pe.transpose(PS[:, 2 + k % 2, t * P:(t + 1) * P],
                                       acc[:, (4 * k + t) * P:(4 * k + t + 1) * P], g["ident"][:])
                ins.then_inc(s_back, 1)

            pe_norm(pe)
            up(0, 0, 0)
            up(0, 0, 1)
            for t in range(NT):
                pe.wait_ge(s_xT, 2 * (t // 4) + 2)
                if t == 0:
                    pe.wait_ge(s_xT, 6)
                ins = pe.matmul(PS[:, 2, t * NE:(t + 1) * NE], g["xT"][:, t * P:(t + 1) * P],
                                g["router" + kind][:], start=True, stop=True)
            ins.then_inc(s_logit, 1)
            down(0, 0, 0)
            for k in range(2, NC):
                up(0, 0, k)
                down(0, 0, k - 1)
            up(1, 1, 0)
            down(0, 0, NC - 1)
            up(1, 1, 1)
            down(1, 1, 0)
            if A:
                pe.wait_ge(s_sel, 1)
                chosen = sel[:].rearrange("p t e -> p (t e)")
                pe.matmul(PS[:, 3, 0:NT * NE], g["strict"][:], chosen, start=True, stop=True).then_inc(s_cum, 1)
                pe.matmul(PS[:, 3, NT * NE:2 * NT * NE], g["ones"][:], chosen, start=True, stop=True).then_inc(s_cum, 1)
            for k in range(2, NC):
                up(1, 1, k)
                down(1, 1, k - 1)
            pe.wait_ge(s_wp, 1)
            for t in range(NT):
                if t % 4 == 0 and t >= 8:
                    pe.wait_ge(s_wT, t // 4 - 1)
                ins = pe.transpose(PS[0:32, 2 + t // 4 % 2, (t % 4) * P:(t % 4 + 1) * P], wpack[:, t, :], g["ident"][:])
                if t % 4 == 3:
                    ins.then_inc(s_wtr, 1)
            up(2, 0, 0)
            down(1, 1, NC - 1)
            pe.wait_ge(s_wT, NC)
            rows(0, pick[3], (0, 1))
            up(2, 0, 1)
            rows(0, pick[3], (2, 3))
            down(2, 0, 0)
            rows(4, pick[0], (0, 1))
            up(2, 0, 2)
            rows(4, pick[0], (2, 3))
            down(2, 0, 1)
            first_rows((0, 1))
            up(2, 0, 3)
            first_rows((2, 3))
            down(2, 0, 2)
            with pe.Fori(3, LAST - 1, 2) as n:
                one_pass(n, 1)
                one_pass(n + 1, 0)
            one_pass(LAST - 1, 1)
            one_pass(LAST, 0, last=True)
            down(LAST, 0, NC - 1)
            back(NC - 2)
            back(NC - 1)

        @block.scalar
        def _(act):
            def copy_rows(at, i, ks, reuse=False):
                if reuse and ks[0] == 0:
                    act.wait_ge(s_part, at - 4)
                    if i == 1:
                        act.wait_ge(s_comb, 4 * n_first)
                for k in ks:
                    act.wait_ge(s_row, at + k + 1)
                    act.activation(wrow[i][:, k * W512:(k + 1) * W512], PS[:, 2 + k % 2, :], ACT.Copy).then_inc(s_rowc, 1)

            def step(n, i, k):
                first = isinstance(n, int) and n == 0
                nf = NF0 if first else NF
                for m in range(nf):
                    q = QF * (nf * k + m)
                    act.wait_ge(s_ring, banks(n) + q + 1)
                    src = PS[:, 4 + q % 4, :]
                    if A:
                        if m == 0 and not (first and k < 2):
                            act.wait_ge(s_gu, feats(n) + nf * (k - 1) if not (k < 2 and isinstance(n, int) and n == 1)
                                        else feats(n) - NF0 * (2 - k) + NF0)
                        act.activation(gate[k % 2][:, m, :], src, ACT.Gelu).then_inc(s_gelu, 1)
                        continue
                    if m == 0 and not (first and k < 2):
                        act.wait_ge(s_lo, feats(n) + NF * (k - 1))
                        act.wait_ge(s_down, 4 * n + k - 1)
                    bias = raw[i][:, WC - 6 + m:WC - 5 + m]
                    act.activation(hid[k % 2][:, m, :], src, ACT.Gelu_apprx_tanh, bias=bias)
                    act.activation(hhi[k % 2][:, m, :], src, ACT.Gelu_apprx_tanh, bias=bias).then_inc(s_gelu, 1)
                if A:
                    if not (first and k < 2):
                        act.wait_ge(s_down, 4 * n + k - 1)
                    for m in range(nf):
                        act.wait_ge(s_gu, feats(n) + nf * k + m + 1)
                        act.activation(hhi[k % 2][:, m, :], hid[k % 2][:, m, :], ACT.Copy).then_inc(s_hhi, 1)

            def one_pass(n, i):
                step(n, i, 0)
                copy_rows(4 * n, i, (0, 1), True)
                step(n, i, 1)
                copy_rows(4 * n, i, (2, 3), True)
                step(n, i, 2)
                step(n, i, 3)

            act_norm(act)
            step(0, 0, 0)
            step(0, 0, 1)
            act.wait_ge(s_lmax, 1)
            act.activation(ex[:], lg[:], ACT.Exp).then_inc(s_ex, 1)
            step(0, 0, 2)
            step(0, 0, 3)
            for k in range(NC):
                step(1, 1, k)
            for k in range(NC):
                act.wait_ge(s_wtr, k + 1)
                act.activation(g["wT"][:, k * W512:(k + 1) * W512], PS[0:32, 2 + k % 2, :], ACT.Copy).then_inc(s_wT, 1)
            step(2, 0, 0)
            copy_rows(0, 1, (0, 1))
            step(2, 0, 1)
            copy_rows(0, 1, (2, 3))
            copy_rows(4, 0, (0, 1))
            step(2, 0, 2)
            copy_rows(4, 0, (2, 3))
            copy_rows(8, 2, (0, 1))
            step(2, 0, 3)
            copy_rows(8, 2, (2, 3))
            with act.Fori(3, LAST - 1, 2) as n:
                one_pass(n, 1)
                one_pass(n + 1, 0)
            one_pass(LAST - 1, 1)
            one_pass(LAST, 0)

        @block.vector
        def _(dve):
            n_rt = [0]

            def then(ins):
                n_rt[0] += 1
                ins.then_inc(s_rt, 1)
                dve.wait_ge(s_rt, n_rt[0])

            def over(a):
                return a.unsqueeze(2).to_broadcast([P, NT, NE])

            def route_logits():
                dve.wait_ge(s_logit, 1)
                logits = PS[:, 2, 0:NT * NE].rearrange("p (t e) -> p t e", e=NE)
                if A:
                    then(dve.tensor_tensor(lg[:], logits, over(rms[:]), ALU.mult))
                else:
                    gb = g["gate_b"][:].unsqueeze(1).to_broadcast([P, NT, NE])
                    then(dve.tensor_tensor(lg[:], logits, gb, ALU.add))
                then(dve.tensor_reduce(mx[:], lg[:], AX.X, ALU.max))
                dve.tensor_tensor(lg[:], lg[:], over(mx[:]), ALU.subtract).then_inc(s_lmax, 1)

            def route_softmax():
                dve.wait_ge(s_ex, 1)
                then(dve.tensor_reduce(sm[:], ex[:], AX.X, ALU.add))
                then(dve.reciprocal(rs[:], sm[:]))
                then(dve.tensor_tensor(pr[:], ex[:], over(rs[:]), ALU.mult))

            def route_top(i):
                left = pr if i == 0 else rank
                order = g["order"][:].unsqueeze(1).to_broadcast([P, NT, NE])
                then(dve.tensor_reduce(mx[:], left[:], AX.X, ALU.max))
                then(dve.tensor_tensor(tot[:], left[:], over(mx[:]), ALU.is_equal))
                then(dve.tensor_tensor(tot[:], tot[:], order, ALU.mult))
                then(dve.tensor_reduce(mx[:], tot[:], AX.X, ALU.max))
                if i == 0:
                    then(dve.tensor_tensor(top[:], tot[:], over(mx[:]), ALU.is_equal))
                    then(dve.scalar_tensor_tensor(out=rank[:], in0=top[:], scalar=-2.0, in1=pr[:],
                                                  op0=ALU.mult, op1=ALU.add))
                else:
                    then(dve.tensor_tensor(tot[:], tot[:], over(mx[:]), ALU.is_equal))
                    dve.tensor_tensor(sel[:], top[:], tot[:], ALU.add).then_inc(s_sel, 1)

            def route_chosen():
                dve.wait_ge(s_sel, 1)
                then(dve.tensor_tensor(pr[:], pr[:], sel[:], ALU.mult))
                then(dve.tensor_reduce(sm[:], pr[:], AX.X, ALU.add))

            def route_places():
                if not A:
                    return
                dve.wait_ge(s_cum, 2)
                cum = PS[:, 3, 0:NT * NE].rearrange("p (t e) -> p t e", e=NE)
                then(dve.tensor_copy(tot[:], PS[:, 3, NT * NE:2 * NT * NE].rearrange("p (t e) -> p t e", e=NE)))
                then(dve.tensor_tensor(rank[:], cum, tot[:], ALU.subtract))
                a, b = tot, tmp
                step = 1
                while step < NT:
                    dve.tensor_copy(b[:, 0:step, :], a[:, 0:step, :])
                    then(dve.tensor_tensor(b[:, step:, :], a[:, step:, :], a[:, 0:NT - step, :], ALU.add))
                    a, b = b, a
                    step *= 2
                then(dve.tensor_tensor(rank[:], rank[:], a[:], ALU.add))

            def route_weights():
                dve.wait_ge(s_clear, 2)
                if A:
                    then(dve.scalar_tensor_tensor(out=rank[:], in0=rank[:], scalar=CAP - 0.5, in1=sel[:],
                                                  op0=ALU.is_gt, op1=ALU.mult))
                    then(dve.tensor_reduce(wfull[:, :, 0], rank[:], AX.X, ALU.max))
                    then(dve.tensor_scalar(rs[:], wfull[:, :, 0], -1.0, 1.0, ALU.mult, ALU.add))
                    dve.tensor_tensor(wfull[:, :, 1:SEQ], pr[:], over(rs[:]), ALU.mult)
                    then(dve.tensor_tensor(sm[:], sm[:], rs[:], ALU.mult))
                    then(dve.tensor_scalar(sm[:], sm[:], 0.5, 0.5, ALU.mult, ALU.add))
                    dve.tensor_tensor(g["fscale"][:], sm[:], rms[:], ALU.mult)
                else:
                    then(dve.tensor_scalar(sm[:], sm[:], 1e-9, None, ALU.add))
                    then(dve.reciprocal(rs[:], sm[:]))
                    dve.tensor_tensor(wfull[:, :, 1:SEQ], pr[:], over(rs[:]), ALU.mult)
                    then(dve.memset(wfull[:, :, 0:1], 1.0))
                then(dve.tensor_copy(whi[:], wfull[:]))
                dve.tensor_copy(wpack[:, :, 0:16], whi[:].bitcast(F32))
                dve.tensor_tensor(wpack[:, :, 16:32], wfull[:], whi[:].bitcast(F32), ALU.subtract).then_inc(s_wp, 1)

            def hidden(n, k):
                first = isinstance(n, int) and n == 0
                nf = NF0 if first else NF
                if A:
                    for m in range(nf):
                        at = feats(n) + nf * k + m
                        q = 2 * (nf * k + m) + 1
                        dve.wait_ge(s_gelu, at + 1)
                        dve.wait_ge(s_ring, banks(n) + q + 1)
                        dve.tensor_tensor(hid[k % 2][:, m, :], gate[k % 2][:, m, :], PS[:, 4 + q % 4, :],
                                          ALU.mult).then_inc(s_gu, 1)

            def weigh(n, i, k):
                cols = slice(k * W512, (k + 1) * W512)
                zero, one = (isinstance(n, int) and n == m for m in (0, 1))
                dve.wait_ge(s_down, 4 * n + k + 1)
                if zero or one:
                    dve.tensor_copy((kept if A == zero else acc)[:, cols], PS[:, k % 2, :]).then_inc(s_part, 1)
                    return
                two = isinstance(n, int) and n == 2
                dve.wait_ge(s_rowc, (4 if two else 4 * n) + k + 1)
                if not (two and k < 2):
                    dve.wait_ge(s_acc, 4 * n + k - 9)
                dve.tensor_tensor(part[k % 2][:], PS[:, k % 2, :], wrow[i][:, cols], ALU.mult).then_inc(s_part, 1)

            def final(k):
                tiles = slice(4 * k, 4 * k + 4)
                dve.wait_ge(s_back, k + 1)
                got = PS[:, 2 + k % 2, :].rearrange("p (t d) -> p t d", t=4)
                dve.scalar_tensor_tensor(out=x[:, tiles, :], in0=got, scalar=0.5, in1=x[:, tiles, :],
                                         op0=ALU.mult, op1=ALU.add).then_inc(s_fin, 1)
                if out is None:
                    dve.wait_ge(s_fin, k + 1)
                    for t in range(4 * k, 4 * k + 4):
                        dve.bn_stats(g["st"][:, t, :], x[:, t, :])

            def one_pass(n, i, last=False):
                for k in range(NC):
                    hidden(n, k)
                    low(dve, n, k)
                    if k:
                        weigh(n, i, k - 1)
                    else:
                        weigh(n - 1, 1 - i, NC - 1)
                    if last and k > 2:
                        final(k - 3)

            def early(n, k, before=None):
                hidden(n, k)
                if A and n == k == 1:
                    dve.wait_ge(s_lo, feats(1) + NF)
                if not A or (n and k):
                    low(dve, n, k)
                if before:
                    before()
                if k:
                    weigh(n, n, k - 1)
                elif n:
                    weigh(0, 0, NC - 1)

            dve_norm(dve)
            early(0, 0)
            early(0, 1, route_logits)
            route_softmax()
            early(0, 2)
            route_top(0)
            early(0, 3)
            route_top(1)
            early(1, 0)
            route_chosen()
            early(1, 1)
            route_places()
            early(1, 2)
            route_weights()
            early(1, 3)
            one_pass(2, 0)
            with dve.Fori(3, LAST - 1, 2) as n:
                one_pass(n, 1)
                one_pass(n + 1, 0)
            one_pass(LAST - 1, 1)
            one_pass(LAST, 0, last=True)
            weigh(LAST, 0, NC - 1)
            for k in range(1, NC):
                final(k)


def hla_block(nc, g, tag, W):
    x, PS = g["x"], g["PS"]
    HP = 8
    UN = 2 * HP
    DK = 64
    BLK = 3 * P
    VBANKS = (0, 1, 6, 7)
    DEPTH = 3
    with ExitStack() as c:
        def sb(name, shape, dt=F32):
            return c.enter_context(nc.sbuf_tensor(f"{tag}_{name}", shape, dt))

        def sem(name):
            return g["sem"](f"{tag}_{name}")

        pool_norm, act_norm, dve_norm, pe_norm, _, _, s_xlo = layer_norm(nc, g, sb, sem, None)
        w = {n: sb("w" + n, [P, HP * P]) for n in "qkv"}
        whi = {n: sb("whi" + n, [P, HP * P], F32R) for n in "qkv"}
        wlo = {n: sb("wlo" + n, [P, HP * P], F32R) for n in "qkv"}
        wo = sb("wo", [P, HP, P])
        xbhi, xblo = sb("xbhi", [P, W512], F32R), sb("xblo", [P, W512], F32R)
        V = sb("V", [P, 4, HP * P])
        qT = [sb(f"qT{i}", [P, W512]) for i in range(2)]
        kT = [sb(f"kT{i}", [P, W512]) for i in range(2)]
        qkhi = [sb(f"qkhi{i}", [P, 2, W512], F32R) for i in range(2)]
        qklo = [sb(f"qklo{i}", [P, 2, W512], F32R) for i in range(2)]
        Am = [sb(f"Am{i}", [P, 2, BLK]) for i in range(DEPTH)]
        Ahi = [sb(f"Ahi{i}", [P, 2, T], F32R) for i in range(DEPTH)]
        Alo = [sb(f"Alo{i}", [P, 2, T], F32R) for i in range(DEPTH)]
        Wm = [sb(f"Wm{i}", [P, 2, BLK]) for i in range(2)]
        OT = sb("OT", [P, HP, W512])

        s_w = {n: sem("s_w" + n) for n in "qkvo"}
        s_whi = sem("s_whi")
        s_wlo = sem("s_wlo")
        s_xb = sem("s_xb")
        s_proj = sem("s_proj")
        s_evac = sem("s_evac")
        s_qklo = sem("s_qklo")
        s_Ahi = sem("s_Ahi")
        s_Alo = sem("s_Alo")
        s_A = sem("s_A")
        s_Am = sem("s_Am")
        s_W = sem("s_W")
        s_Wm = sem("s_Wm")
        s_O = sem("s_O")
        s_OT = sem("s_OT")
        s_res = sem("s_res")
        block = c.enter_context(nc.Block())

        @block.sync
        def _(sp):
            for n in "qkv":
                sp.dma_start(w[n][:], W[n]).then_inc(s_w[n], 16)
            sp.dma_start(wo[:], W["o"]).then_inc(s_w["o"], 16)

        @block.gpsimd
        def _(pool):
            pool_norm(pool)
            for i, n in enumerate("qkv"):
                pool.wait_ge(s_w[n], 16)
                pool.tensor_tensor(whi[n][:], w[n][:], g["ones"][:, 0:1].to_broadcast([P, HP * P]),
                                   ALU.mult).then_inc(s_whi, 1)
                pool.wait_ge(s_whi, i + 1)
                pool.tensor_tensor(wlo[n][:], w[n][:], whi[n][:].bitcast(F32), ALU.subtract).then_inc(s_wlo, 1)

        @block.scalar
        def _(act):
            act_norm(act)
            with act.Fori(0, NC) as it:
                def copy(dst, j, bank):
                    act.wait_ge(s_proj, 26 * it + j + 1)
                    act.activation(dst, PS[:, bank, :], ACT.Copy).then_inc(s_evac, 1)

                def copy_qk(h):
                    j = 2 * h if h < 2 else 8 + 2 * h
                    if h >= 2:
                        act.wait_ge(s_A, 32 * it + 4 * (h - 1))
                    for i, full in ((0, qT), (1, kT)):
                        act.wait_ge(s_proj, 26 * it + j + i + 1)
                        act.activation(qkhi[h % 2][:, i, :], PS[:, i, :], ACT.Copy)
                        act.activation(full[h % 2][:], PS[:, i, :], ACT.Copy).then_inc(s_evac, 1)

                def high_a(u):
                    act.wait_ge(s_Am, 32 * it + 2 * u + 2)
                    if u >= DEPTH:
                        act.wait_ge(s_W, 32 * it + 2 * (u - DEPTH) + 2)
                    act.activation(Ahi[u % DEPTH][:], Am[u % DEPTH][:, :, 0:T], ACT.Copy).then_inc(s_Ahi, 1)

                def copy_o(h):
                    act.wait_ge(s_O, UN * it + 2 * h + 2)
                    act.activation(OT[:, h, :], PS[:, 6 + h % 2, :], ACT.Copy).then_inc(s_OT, 1)

                copy_qk(0)
                copy_qk(1)
                for j in range(8):
                    if j == 6:
                        high_a(0)
                    copy(V[:, j // 2, j % 2 * W512:(j % 2 + 1) * W512], 4 + j, VBANKS[j % 4])
                high_a(1)
                for u in range(UN):
                    if u + 2 < UN:
                        high_a(u + 2)
                    if u % 2 == 0 and u // 2 + 2 < HP:
                        copy_qk(u // 2 + 2)
                    if u % 2 == 0 and u:
                        copy_o(u // 2 - 1)
                copy_o(HP - 1)

        @block.vector
        def _(dve):
            dve_norm(dve)
            dve.wait_ge(s_xlo, NC)
            with dve.Fori(0, NC) as it:
                dve.tensor_copy(xbhi[:], g["xhi"][:, bass.ds(it * W512, W512)]).then_inc(s_xb, 1)
                dve.tensor_copy(xblo[:], g["xlo"][:, bass.ds(it * W512, W512)]).then_inc(s_xb, 1)

                def mask(u, full, done, dst, bank, used):
                    for h in range(2):
                        n = 32 * it + 2 * u + h
                        dve.wait_ge(full, n + 1)
                        if used is not None:
                            dve.wait_ge(*used(h))
                        dve.tensor_tensor(dst[u % len(dst)][:, h, :], PS[:, bank + h, 0:BLK], g["tri"][:],
                                          ALU.mult).then_inc(done, 1)

                def mask_a(u):
                    mask(u, s_A, s_Am, Am, 2, 
                         (lambda h: (s_W, 32 * it + 2 * (u - DEPTH) + h + 1)) if u >= DEPTH else None)

                def mask_w(u):
                    mask(u, s_W, s_Wm, Wm, 4, (lambda h: (s_O, UN * it + u - 1)) if u >= 2 else None)

                def low_qk(h):
                    j = 2 * h if h < 2 else 8 + 2 * h
                    for i, full in ((0, qT), (1, kT)):
                        dve.wait_ge(s_evac, 24 * it + j + i + 1)
                        if h >= 2:
                            dve.wait_ge(s_A, 32 * it + 4 * (h - 1))
                        dve.tensor_tensor(qklo[h % 2][:, i, :], full[h % 2][:], qkhi[h % 2][:, i, :].bitcast(F32),
                                          ALU.subtract).then_inc(s_qklo, 1)

                def low_a(u):
                    dve.wait_ge(s_Ahi, UN * it + u + 1)
                    if u >= DEPTH:
                        dve.wait_ge(s_W, 32 * it + 2 * (u - DEPTH) + 2)
                    dve.tensor_tensor(Alo[u % DEPTH][:], Am[u % DEPTH][:, :, 0:T], Ahi[u % DEPTH][:].bitcast(F32),
                                      ALU.subtract).then_inc(s_Alo, 1)

                low_qk(0)
                low_qk(1)
                mask_a(0)
                mask_a(1)
                low_a(0)
                low_a(1)
                for u in range(UN):
                    if u + 2 < UN:
                        mask_a(u + 2)
                    mask_w(u)
                    if u + 2 < UN:
                        low_a(u + 2)
                    if u % 2 == 0 and u // 2 + 2 < HP:
                        low_qk(u // 2 + 2)
                for j in range(2):
                    dve.wait_ge(s_proj, 26 * it + 24 + j + 1)
                    rows = x[:, bass.ds(it * 4 + 2 * j, 2), :]
                    dve.tensor_tensor(rows, rows, PS[:, 4 + j, 0:2 * P].rearrange("p (t d) -> p t d", t=2),
                                      ALU.add).then_inc(s_res, 1)
                dve.wait_ge(s_res, 2 * it + 2)
                moments(dve, g, 4 * it, 4)

        @block.tensor
        def _(pe):
            def proj(bank, lhs, rhs):
                (lh, ll), (rh, rl) = lhs, rhs
                pe.matmul(PS[:, bank, :], lh, rh, start=True, stop=False)
                pe.matmul(PS[:, bank, :], lh, rl, start=False, stop=False)
                pe.matmul(PS[:, bank, :], ll, rh, start=False, stop=True).then_inc(s_proj, 1)

            pe_norm(pe)
            pe.wait_ge(s_wlo, 2)
            pe.wait_ge(s_xlo, 2)
            pe.wait_ge(s_w["o"], 16)
            with pe.Fori(0, NC) as it:
                turn = bass.ds(it * W512, W512)

                def proj_qk(h):
                    j = 2 * h if h < 2 else 8 + 2 * h
                    for i, n in enumerate("qk"):
                        if j + i >= 2:
                            pe.wait_ge(s_evac, 24 * it + j + i - 1)
                        cols = slice(h * P, (h + 1) * P)
                        proj(i, (whi[n][:, cols], wlo[n][:, cols]), (g["xhi"][:, turn], g["xlo"][:, turn]))

                def proj_v(j):
                    rows, cols = slice(j // 2 * P, (j // 2 + 1) * P), slice(j % 2 * W512, (j % 2 + 1) * W512)
                    if j % 4 < 2 or j >= 4:
                        pe.wait_ge(s_evac, 24 * it + (j + 3 if j < 4 else j + 1))
                    proj(VBANKS[j % 4], (xbhi[:, rows], xblo[:, rows]), (whi["v"][:, cols], wlo["v"][:, cols]))

                def scores(u):
                    h, b = divmod(u, 2)
                    pe.wait_ge(s_qklo, 2 * HP * it + 2 * h + 2)
                    for i in range(2):
                        if u:
                            pe.wait_ge(s_Am, 32 * it + 2 * u - 2 + i + 1)
                        d, at = slice(i * DK, (i + 1) * DK), b * T
                        k, q = kT[h % 2][d, :], qT[h % 2][d, :]
                        hi, lo = qkhi[h % 2][d, :, :], qklo[h % 2][d, :, :]
                        for n, (kk, qq) in enumerate(((hi, hi), (hi, lo), (lo, hi))):
                            pe.matmul(PS[:, 2 + i, 0:T], kk[:, 1, at:at + P], qq[:, 0, at:at + T],
                                      start=n == 0, stop=n == 2)
                        pe.matmul(PS[:, 2 + i, T:BLK], k[:, at + P:at + T], q[:, at + P:at + T],
                                  start=True, stop=True).then_inc(s_A, 1)

                def square(u):
                    pe.wait_ge(s_Alo, UN * it + u + 1)
                    for i in range(2):
                        if u:
                            pe.wait_ge(s_Wm, 32 * it + 2 * u - 2 + i + 1)
                        a = Am[u % DEPTH][:, i, :]
                        hi, lo = Ahi[u % DEPTH][:, i, :], Alo[u % DEPTH][:, i, :]
                        for n, (aa, bb) in enumerate(((hi, hi), (hi, lo), (lo, hi))):
                            pe.matmul(PS[:, 4 + i, 0:T], aa[:, 0:P], bb, start=n == 0, stop=n == 2)
                        pe.matmul(PS[:, 4 + i, T:BLK], a[:, P:T], a[:, P:T], start=True, stop=False)
                        pe.matmul(PS[:, 4 + i, T:BLK], a[:, T:BLK], a[:, T:BLK],
                                  start=False, stop=True).then_inc(s_W, 1)

                def output(u):
                    h, b = divmod(u, 2)
                    if u == 0:
                        pe.wait_ge(s_evac, 24 * it + 12)
                    if b == 0 and h >= 2:
                        pe.wait_ge(s_OT, HP * it + h - 1)
                    pe.wait_ge(s_Wm, 32 * it + 2 * u + 2)
                    bank, at = PS[:, 6 + h % 2, :], b * T
                    for j in range(2):
                        for i in range(2):
                            d = slice(i * DK, (i + 1) * DK)
                            v = V[:, 2 * b + j, (2 * h + i) * DK:(2 * h + i + 1) * DK]
                            wm = Wm[u % 2][:, i, :]
                            src = wm[:, 0:T] if j == 0 else wm[:, T:BLK]
                            ins = pe.matmul(bank[d, at + j * P:at + T], v, src, start=(b == 0 and j == 0),
                                            stop=(b == 1 and j == 1), skip_group_check=True)
                    ins.then_inc(s_O, 1)

                proj_qk(0)
                proj_qk(1)
                pe.wait_ge(s_wlo, 3)
                pe.wait_ge(s_xlo, NC)
                pe.wait_ge(s_xb, 2 * it + 2)
                for j in range(8):
                    if j == 4:
                        scores(0)
                    proj_v(j)
                scores(1)
                for u in range(UN):
                    if u % 2 == 0 and u // 2 + 2 < HP:
                        proj_qk(u // 2 + 2)
                    if u + 2 < UN:
                        scores(u + 2)
                    square(u)
                    if u:
                        output(u - 1)
                output(UN - 1)
                pe.wait_ge(s_OT, HP * it + HP)
                for j in range(2):
                    for t in range(2):
                        for h in range(HP):
                            rows = slice((2 * j + t) * P, (2 * j + t + 1) * P)
                            ins = pe.matmul(PS[:, 4 + j, t * P:(t + 1) * P], OT[:, h, rows], wo[:, h, :],
                                            start=(h == 0), stop=(h == HP - 1))
                    ins.then_inc(s_proj, 1)


def attention_block(nc, g, tag, W, cst):
    x, PS = g["x"], g["PS"]
    G, J = 4, 4
    H, DH = 16, 8
    SCALE = DH ** -0.5
    BLK = 3 * P
    with ExitStack() as c:
        def sb(name, shape, dt=F32):
            return c.enter_context(nc.sbuf_tensor(f"{tag}_{name}", shape, dt))

        def sem(name):
            return g["sem"](f"{tag}_{name}")

        pool_norm, act_norm, dve_norm, pe_norm, _, s_xT, _ = layer_norm(nc, g, sb, sem, None, split=False)
        w = sb("w", [P, 4, P])
        wrot = sb("wrot", [P, 2, P])
        cs = sb("cs", [P, 2 * T])
        spread = sb("spread", [P, 4, G, P])
        spreadr = sb("spreadr", [P, 4, G, P], F32R)
        unit = sb("unit", [P, H, P])
        unitr = sb("unitr", [P, H, P], F32R)
        maskf = sb("maskf", [P, 4 * P])
        maskb = sb("maskb", [P, 4 * P], BF16)
        identb = sb("identb", [P, P], BF16)
        xb = [sb(f"xb{i}", [P, T]) for i in range(2)]
        tq = sb("tq", [P, 2, 2 * T])
        qk = sb("qk", [P, 2, T])
        qkhi, qklo = sb("qkhi", [P, 2, T], F32R), sb("qklo", [P, 2, T], F32R)
        S = [sb(f"S{i}", [P, 2, G, T], F32R) for i in range(2)]
        V = [sb(f"V{i}", [P, 2, H, 32]) for i in range(2)]
        nmax = sb("nmax", [P, 2, H])
        nhi = sb("nhi", [P, 2, H], F32R)
        mp = sb("mp", [P, 2, 32])
        mT = [sb(f"mT{i}", [P, BLK], F32R) for i in range(2)]
        PT = sb("PT", [P, G, J, BLK])
        OT = sb("OT", [P, G, T])
        rden = sb("rden", [P, 2, H])
        at = sb("at", [P, 2, P])
        atT = sb("atT", [P, 2, P])

        s_w = sem("s_w")
        s_set = sem("s_set")
        s_setp = sem("s_setp")
        s_xb = sem("s_xb")
        s_proj = sem("s_proj")
        s_v = sem("s_v")
        s_rot = sem("s_rot")
        s_hi = sem("s_hi")
        s_spread = sem("s_spread")
        s_S = sem("s_S")
        s_s1 = sem("s_s1")
        s_mx = sem("s_mx")
        s_mp = sem("s_mp")
        s_mtr = sem("s_mtr")
        s_mT = sem("s_mT")
        s_s2 = sem("s_s2")
        s_p = sem("s_p")
        s_pv = sem("s_pv")
        s_ot = sem("s_ot")
        s_otr = sem("s_otr")
        s_at = sem("s_at")
        s_atr = sem("s_atr")
        s_atT = sem("s_atT")
        s_o = sem("s_o")
        s_res = sem("s_res")
        SETUP = 7
        block = c.enter_context(nc.Block())


        @block.sync
        def _(sp):
            for dst, src in ((w, W), (cs, cst["cs"]), (spread, cst["spread"]), (unit, cst["unit"]), (maskf, cst["mask"])):
                sp.dma_start(dst[:], src).then_inc(s_w, 16)

        @block.gpsimd
        def _(pool):
            pool_norm(pool)
            for i in range(2):
                pool.memset(V[i][:], 0.0).then_inc(s_setp, 1)
            for i in range(2):
                pool.memset(mT[i][:].bitcast(F32), 0.0).then_inc(s_setp, 1)
            pool.wait_ge(s_w, 80)
            pool.tensor_tensor(unitr[:], unit[:], g["ones"][:, 0:1].unsqueeze(1).to_broadcast([P, H, P]),
                               ALU.mult).then_inc(s_setp, 1)

        @block.scalar
        def _(act):
            def high(m):
                act.wait_ge(s_rot, 3 * m + 2)
                act.activation(qkhi[:], qk[:], ACT.Copy).then_inc(s_hi, 1)

            def split_values(m, i):
                act.wait_ge(s_proj, 2 * m + 2)
                act.activation(V[i][:, :, :, 0:DH], PS[:, 6, 0:T].rearrange("p (t h d) -> p t h d", t=2, d=DH),
                               ACT.Copy).then_inc(s_v, 1)

            def spread_copies(m, i, bs):
                for b in bs:
                    act.wait_ge(s_spread, 4 * m + b + 1)
                    act.activation(S[i][:, b % 2, b // 2 * 2:b // 2 * 2 + 2, :],
                                   PS[:, 7 - b % 2, :].rearrange("p (g t) -> p g t", g=2), ACT.Copy).then_inc(s_S, 1)

            def maxima(m, i):
                act.wait_ge(s_mtr, m + 1)
                act.activation(mT[i][0:32, P:BLK], PS[0:32, 6, 0:T], ACT.Copy).then_inc(s_mT, 1)
                act.activation(mT[i][0:32, 0:P], PS[0:32, 6, P:T], ACT.Copy).then_inc(s_mT, 1)

            def exps(n, bs):
                for b in bs:
                    act.wait_ge(s_s2, 8 * n + b + 1)
                    if not (isinstance(n, int) and n == 0):
                        act.wait_ge(s_pv, 4 * n - 3 + b // 2)
                    gq, j = b // 2, b % 2 * 2
                    act.activation(PT[:, gq, j:j + 2, :], PS[:, j:j + 2, P:W512], ACT.Exp, scale=SCALE).then_inc(s_p, 1)

            def transposed(t):
                act.wait_ge(s_atr, t + 1)
                act.activation(atT[:], PS[:, 4, 0:T].rearrange("p (t q) -> p t q", t=2), ACT.Copy).then_inc(s_atT, 1)

            def turn(n, i, front=True, tail=True):
                exps(n, (0,))
                if front:
                    high(n + 1)
                exps(n, (1,))
                if front:
                    split_values(n + 1, 1 - i)
                exps(n, (2,))
                if tail:
                    transposed(n - 1)
                if front:
                    spread_copies(n + 1, 1 - i, (0, 1))
                exps(n, (3,))
                if front:
                    spread_copies(n + 1, 1 - i, (2, 3))
                exps(n, (4, 5, 6, 7))
                if front:
                    maxima(n + 1, 1 - i)

            act_norm(act)
            act.wait_ge(s_setp, 4)
            act.wait_ge(s_set, SETUP)
            high(0)
            split_values(0, 0)
            spread_copies(0, 0, range(4))
            maxima(0, 0)
            turn(0, 0, tail=False)
            with act.Fori(0, NB // 2 - 1) as pair_of_turns:
                n = 2 * pair_of_turns + 1
                turn(n, 1)
                turn(n + 1, 0)
            turn(NB - 1, 1, front=False)
            transposed(NB - 1)

        @block.vector
        def _(dve):
            def rows_in_place(m, i):
                dve.tensor_copy(xb[i][:], g["xT"][:, m * T:(m + 1) * T] if isinstance(m, int)
                                else g["xT"][:, bass.ds(m * T, T)]).then_inc(s_xb, 1)

            def rotate(m):
                dve.wait_ge(s_proj, 2 * m + 1)
                both = cs[:].unsqueeze(1).to_broadcast([P, 2, 2 * T])
                dve.tensor_tensor(tq[:], PS[:, 6:8, :], both, ALU.mult).then_inc(s_rot, 1)
                dve.wait_ge(s_rot, 3 * m + 1)
                dve.tensor_tensor(qk[:], tq[:, :, 0:T], tq[:, :, T:2 * T], ALU.add).then_inc(s_rot, 1)

            def rests(m):
                dve.wait_ge(s_hi, m + 1)
                dve.tensor_tensor(qklo[:], qk[:], qkhi[:].bitcast(F32), ALU.subtract).then_inc(s_rot, 1)

            def maxima(m, bs):
                for b in bs:
                    qt, a, j = b % 2, b // 8, b // 2 % 4
                    dve.wait_ge(s_s1, 16 * m + b + 1)
                    K = P * (qt + 1)
                    src = PS[:, 6 + b % 2, :].rearrange("p (g k) -> p g k", g=2)[:, :, 0:K]
                    dst = nmax[:, qt, :].rearrange("p (g j) -> p g j", j=J)[:, 2 * a:2 * a + 2, j]
                    dve.tensor_reduce(dst, src, AX.X, ALU.max, negate=True).then_inc(s_mx, 1)

            def pack(m):
                dve.wait_ge(s_mx, 16 * m + 16)
                dve.tensor_copy(nhi[:], nmax[:]).then_inc(s_mp, 1)
                dve.wait_ge(s_mp, 3 * m + 1)
                dve.tensor_copy(mp[:, :, 0:H], nhi[:].bitcast(F32)).then_inc(s_mp, 1)
                dve.tensor_tensor(mp[:, :, H:2 * H], nmax[:], nhi[:].bitcast(F32), ALU.subtract).then_inc(s_mp, 1)

            def weighted_values(n, b):
                dve.wait_ge(s_pv, 4 * n + 2 * b + 2)
                dve.tensor_copy(OT[:, 2 * b:2 * b + 2, :],
                                PS[:, 4 + b, :].rearrange("p (g t) -> p g t", g=2)).then_inc(s_ot, 1)

            def normalised(t):
                for qt in range(2):
                    dve.wait_ge(s_otr, 2 * t + qt + 1)
                    got = PS[:, 4 + qt, :].rearrange("p (h d) -> p h d", d=32)
                    dve.reciprocal(rden[:, qt, :], got[:, :, DH]).then_inc(s_at, 1)
                    dve.wait_ge(s_at, 4 * t + 2 * qt + 1)
                    dve.tensor_tensor(at[:, qt, :].rearrange("p (h d) -> p h d", d=DH), got[:, :, 0:DH],
                                      rden[:, qt, :].unsqueeze(2).to_broadcast([P, H, DH]),
                                      ALU.mult).then_inc(s_at, 1)

            def residual(t):
                dve.wait_ge(s_o, t + 1)
                rows = x[:, bass.ds(2 * t, 2), :]
                dve.tensor_tensor(rows, rows, PS[:, 5, 0:T].rearrange("p (t d) -> p t d", t=2),
                                  ALU.add).then_inc(s_res, 1)
                dve.wait_ge(s_res, t + 1)
                moments(dve, g, 2 * t, 2)

            def turn(n, i, front=True, tail=True):
                if front:
                    rows_in_place(n + 1, 1 - i)
                    rotate(n + 1)
                if tail:
                    normalised(n - 1)
                if front:
                    rests(n + 1)
                if tail:
                    residual(n - 1)
                if front:
                    maxima(n + 1, range(10))
                weighted_values(n, 0)
                if front:
                    maxima(n + 1, range(10, 16))
                    pack(n + 1)
                weighted_values(n, 1)

            dve_norm(dve)
            dve.wait_ge(s_w, 80)
            dve.wait_ge(s_setp, 4)
            for i in range(2):
                pair = w[:, i, :].rearrange("p (h two) -> p h two", two=2)
                rot = wrot[:, i, :].rearrange("p (h two) -> p h two", two=2)
                dve.tensor_scalar(rot[:, :, 0], pair[:, :, 1], -1.0, None, ALU.mult)
                dve.tensor_copy(rot[:, :, 1], pair[:, :, 0]).then_inc(s_set, 1)
            dve.wait_ge(s_xT, NC)
            rows_in_place(0, 0)
            dve.tensor_copy(spreadr[:], spread[:]).then_inc(s_set, 1)
            dve.tensor_copy(maskb[:], maskf[:]).then_inc(s_set, 1)
            dve.tensor_copy(identb[:], g["ident"][:]).then_inc(s_set, 1)
            for i in range(2):
                dve.memset(V[i][:, :, :, DH:DH + 1], 1.0).then_inc(s_set, 1)
            rotate(0)
            rests(0)
            maxima(0, range(16))
            pack(0)
            turn(0, 0, tail=False)
            with dve.Fori(0, NB // 2 - 1) as pair_of_turns:
                n = 2 * pair_of_turns + 1
                turn(n, 1)
                turn(n + 1, 0)
            turn(NB - 1, 1, front=False)
            normalised(NB - 1)
            residual(NB - 1)

        @block.tensor
        def _(pe):
            def project(m):
                cols = bass.ds(m * T, T)
                for p in (1, 0):
                    if p == 0 and not (isinstance(m, int) and m == 0):
                        pe.wait_ge(s_mT, 2 * m)
                    pe.matmul(PS[:, 6 + p, 0:T], w[:, p, :], g["xT"][:, cols], start=True, stop=True)
                    ins = pe.matmul(PS[:, 6 + p, T:2 * T], wrot[:, p, :], g["xT"][:, cols], start=True, stop=True)
                ins.then_inc(s_proj, 1)

            def project_v(m, i):
                pe.wait_ge(s_xb, m + 1)
                pe.wait_ge(s_rot, 3 * m + 1)
                for t in range(2):
                    ins = pe.matmul(PS[:, 6, t * P:(t + 1) * P], xb[i][:, t * P:(t + 1) * P], w[:, 2, :],
                                    start=True, stop=True)
                ins.then_inc(s_proj, 1)

            def spread_out(m, bs):
                pe.wait_ge(s_rot, 3 * m + 3)
                for b in bs:
                    if b == 1:
                        pe.wait_ge(s_v, m + 1)
                    elif b >= 2:
                        pe.wait_ge(s_S, 4 * m + b - 1)
                    for e in range(2):
                        p, gr = b % 2, b // 2 * 2 + e
                        dst = PS[:, 7 - b % 2, e * T:(e + 1) * T]
                        pe.matmul(dst, spreadr[:, 2 * p, gr, :], qkhi[:, p, :], start=True, stop=False)
                        ins = pe.matmul(dst, spreadr[:, 2 * p + 1, gr, :], qklo[:, p, :], start=False, stop=True)
                    ins.then_inc(s_spread, 1)

            def scores_down(m, i, bs):
                for b in bs:
                    qt, a, j = b % 2, b // 8, b // 2 % 4
                    if b < 2:
                        pe.wait_ge(s_S, 4 * m + 4)
                    else:
                        pe.wait_ge(s_mx, 16 * m + b - 1)
                    bank, r = 6 + b % 2, slice(32 * j, 32 * j + 32)
                    diag = PS[:, bank, :].rearrange("p (e k) -> p e k", e=2)[:, :, qt * P:(qt + 1) * P]
                    pe.matmul(diag, identb[:], maskb[:, 0:2 * P].rearrange("p (e k) -> p e k", e=2),
                              start=True, stop=False, skip_group_check=True)
                    for e in range(2):
                        gr = 2 * a + e
                        ins = pe.matmul(PS[:, bank, e * T:(e + 1) * T], S[i][r, 0, gr, qt * P:(qt + 1) * P],
                                        S[i][r, 1, gr, :], start=False, stop=True, skip_group_check=True)
                    ins.then_inc(s_s1, 1)

            def maxima(m):
                pe.wait_ge(s_mp, 3 * m + 3)
                for t in range(2):
                    ins = pe.transpose(PS[0:32, 6, t * P:(t + 1) * P], mp[:, t, :], g["ident"][:])
                ins.then_inc(s_mtr, 1)

            def scores(n, i, b):
                gr = b // 2
                if b == 0:
                    pe.wait_ge(s_mT, 2 * n + 2)
                if not (isinstance(n, int) and n == 0 and b < 2):
                    pe.wait_ge(s_p, 8 * n + b - 1)
                for e in range(2):
                    j = b % 2 * 2 + e
                    pe.matmul(PS[:, j, P:W512], unitr[:, 4 * gr + j, :], mT[i][:], start=True, stop=False,
                              skip_group_check=True)
                    pe.matmul(PS[:, j, P:3 * P], identb[:], maskb[:, 2 * P:4 * P], start=False, stop=False,
                              skip_group_check=True)
                for e in range(2):
                    j = b % 2 * 2 + e
                    r = slice(32 * j, 32 * j + 32)
                    pe.matmul(PS[:, j, 0:T], S[i][r, 1, gr, P:T], S[i][r, 0, gr, :],
                              start=False, stop=True, skip_group_check=True)
                    ins = pe.matmul(PS[:, j, T:2 * T], S[i][r, 1, gr, 0:P], S[i][r, 0, gr, :],
                                    start=False, stop=True, skip_group_check=True)
                ins.then_inc(s_s2, 1)

            def values(n, i, gr):
                pe.wait_ge(s_p, 8 * n + 2 * gr + 2)
                if gr % 2 == 0 and not (isinstance(n, int) and n == 0):
                    pe.wait_ge(s_res if gr else s_atT, n)
                for k in range(2):
                    for j in range(J):
                        dst = PS[32 * j:32 * j + 32, 4 + gr // 2, gr % 2 * T + k * P:(gr % 2 + 1) * T]
                        src = PT[:, gr, j, P:BLK] if k == 0 else PT[:, gr, j, 0:P]
                        ins = pe.matmul(dst, V[i][:, k, 4 * gr + j, :], src, start=(gr % 2 == 0 and k == 0),
                                        stop=(k == 1), skip_group_check=True)
                ins.then_inc(s_pv, 1)

            def token_major(t):
                pe.wait_ge(s_ot, 2 * t + 2)
                for qt in range(2):
                    for gr in range(G):
                        ins = pe.transpose(PS[:, 4 + qt, gr * P:(gr + 1) * P], OT[:, gr, qt * P:(qt + 1) * P],
                                           g["ident"][:])
                    ins.then_inc(s_otr, 1)

            def transposed(t):
                pe.wait_ge(s_at, 4 * t + 4)
                for qt in range(2):
                    ins = pe.transpose(PS[:, 4, qt * P:(qt + 1) * P], at[:, qt, :], g["ident"][:])
                ins.then_inc(s_atr, 1)

            def output(t):
                pe.wait_ge(s_atT, t + 1)
                for qt in range(2):
                    ins = pe.matmul(PS[:, 5, qt * P:(qt + 1) * P], atT[:, qt, :], w[:, 3, :], start=True, stop=True)
                ins.then_inc(s_o, 1)

            def turn(n, i, front=True, tail=True):
                if front:
                    project(n + 1)
                scores(n, i, 0)
                if tail:
                    token_major(n - 1)
                scores(n, i, 1)
                if front:
                    project_v(n + 1, 1 - i)
                scores(n, i, 2)
                if tail:
                    transposed(n - 1)
                if front:
                    spread_out(n + 1, (0, 1))
                scores(n, i, 3)
                if tail:
                    output(n - 1)
                if front:
                    spread_out(n + 1, (2, 3))
                values(n, i, 0)
                for bs, after in ((range(0, 2), lambda: scores(n, i, 4)), (range(2, 6), lambda: scores(n, i, 5)),
                                  (range(6, 8), lambda: values(n, i, 1)), (range(8, 10), lambda: scores(n, i, 6)),
                                  (range(10, 12), lambda: scores(n, i, 7)), (range(12, 16), lambda: values(n, i, 2))):
                    if front:
                        scores_down(n + 1, 1 - i, bs)
                    after()
                values(n, i, 3)
                if front:
                    maxima(n + 1)

            pe_norm(pe)
            pe.wait_ge(s_set, 2)
            pe.wait_ge(s_xT, NC)
            project(0)
            project_v(0, 0)
            pe.wait_ge(s_set, SETUP)
            spread_out(0, range(4))
            scores_down(0, 0, range(16))
            maxima(0)
            pe.wait_ge(s_setp, 5)
            turn(0, 0, tail=False)
            with pe.Fori(0, NB // 2 - 1) as pair_of_turns:
                n = 2 * pair_of_turns + 1
                turn(n, 1)
                turn(n + 1, 0)
            turn(NB - 1, 1, front=False)
            token_major(NB - 1)
            transposed(NB - 1)
            output(NB - 1)


def macaron(nc, a, out, stages=6):
    with ExitStack() as ctx:
        def sb(name, shape, dt=F32):
            return ctx.enter_context(nc.sbuf_tensor(name, shape, dt))

        g = {
            "x": sb("x", [P, NT, P]), "xr": sb("xr", [P, NT, P]), "xT": sb("xT", [P, TOK]),
            "xhi": sb("xhi", [P, TOK], F32R), "xlo": sb("xlo", [P, TOK], F32R),
            "wT": sb("wT", [32, TOK], F32R), "fscale": sb("fscale", [P, NT]),
            "st": sb("st", [P, NT, 6]), "have_moments": False,
            "PS": ctx.enter_context(nc.psum_tensor("PS", [P, 8, W512], F32)),
        }
        small = {"ident": [P, P], "strict": [P, P], "ones": [P, P], "tri": [P, 3 * P], "order": [P, NE],
                 "gate_b": [P, NE], "routerA": [P, NE], "routerB": [P, NE], "b2B": [32, P]}
        for name, shape in small.items():
            g[name] = sb(name, shape)
        s_in = ctx.enter_context(nc.semaphore("s_in"))
        s_out = ctx.enter_context(nc.semaphore("s_out"))
        tokens = "(t p) d -> p t d"
        held = []

        def sem(name):
            held.append(nc.alloc_semaphore(name))
            return held[-1]

        g["sem"] = sem

        with nc.Block() as block:
            @block.sync
            def _(sp):
                sp.dma_start(g["x"][:], a["x"].rearrange(tokens, p=P)).then_inc(s_in, 16)
                for name in small:
                    sp.dma_start(g[name][:], a[name]).then_inc(s_in, 16)
                sp.wait_ge(s_in, 16 * (len(small) + 1))

        def mixture(kind, tag, out=None):
            mixture_block(nc, g, tag, kind, a["mix" + kind], out)

        def hla():
            hla_block(nc, g, "h", {n: a["hla_w" + n] for n in "qkvo"})

        def attention():
            attention_block(nc, g, "a", a["att_w"], {"cs": a["cs"], "spread": a["spread"], "unit": a["unit"], "mask": a["mask"]})

        order = [lambda: mixture("A", "m1"), hla, lambda: mixture("A", "m2"), lambda: mixture("B", "m3"),
                 attention, lambda: mixture("B", "m4", out.rearrange(tokens, p=P))]
        if isinstance(stages, int):
            stages = range(stages)
        for s in stages:
            if s == 3:
                nc.clear_and_free_semaphores(held)
                held.clear()
                nc.all_engine_barrier()
            order[s]()
        if stages[-1] != 5:
            with nc.Block() as block:
                @block.sync
                def _(sp):
                    sp.dma_start(out.rearrange(tokens, p=P), g["x"][:]).then_inc(s_out, 16)
                    sp.wait_ge(s_out, 16)


def _constants():
    import numpy as np
    i = np.arange(P)
    f = np.float32
    H, DH = 16, 8
    le = (i[:, None] <= i[None, :]).astype(f)
    one = np.ones((P, P), f)
    off = f(-1e30)
    later = np.where(i[:, None] < i[None, :], off, f(0))
    laterT = later.T.copy()
    j = np.arange(NE)
    c = {
        "ident": np.eye(P, dtype=f), "strict": (i[:, None] < i[None, :]).astype(f), "ones": one,
        "tri": np.concatenate([le, one, le], 1),
        "order": np.tile((NE - j).astype(f)[None], (P, 1)),
        "mask": np.concatenate([later, later, laterT, laterT], 1),
    }
    theta = (10000.0 ** (-2.0 * np.arange(DH // 2, dtype=f) / DH)).astype(f)
    angles = (np.arange(T, dtype=f)[:, None] * theta[None, :]).astype(f)
    per_row = angles[:, (i % DH) // 2].T
    c["cs"] = np.concatenate([np.cos(per_row), np.sin(per_row)], 1).astype(f)
    spread = np.zeros((P, 4, 4, P), f)
    for part, terms in enumerate(((0, 1), (2, 3), (0, 2), (1, 3))):
        for gr in range(4):
            for jj in range(4):
                for term in terms:
                    for d in range(DH):
                        spread[(4 * gr + jj) * DH + d, part, gr, 32 * jj + 8 * term + d] = 1
    c["spread"] = spread
    unit = np.zeros((P, H, P), f)
    for h in range(H):
        unit[h, h] = 1
        unit[H + h, h] = 1
    c["unit"] = unit
    return c


def _layout(inputs):
    import numpy as np
    v = {k: np.asarray(z) for k, z in inputs.items()}
    f = np.float32
    a = _constants()
    a["x"] = v["L0_attn_x"].reshape(TOK, P)
    a["gate_b"] = np.repeat(v["L1_ffn_gate_b"][None], P, 0)
    a["routerA"], a["routerB"] = v["L0_ffn_Wr"], v["L1_ffn_gate_w"]
    chosen = np.zeros((SEQ, P, 1), f)
    for n in range(SEQ):
        chosen[n, n] = chosen[n, 16 + n] = 1
    FA = v["L0_ffn_Wg"].shape[2]
    mixA = np.zeros((SEQ, P, 4 * P + FA + MISC), f)
    mixA[1:, :, 0:FA] = v["L0_ffn_Wg"]
    mixA[1:, :, FA:2 * FA] = v["L0_ffn_Wu"]
    mixA[1:, :, 4 * P:4 * P + FA] = v["L0_ffn_Wd"].reshape(NE, 2, P, P).transpose(0, 2, 1, 3).reshape(NE, P, FA)
    mixA[1:, :, -8] = v["L0_ffn_norm_w"]
    F4 = v["L0_ffn_fWg"].shape[1]
    mixA[0, :, 0:F4] = v["L0_ffn_fWg"]
    mixA[0, :, FA:FA + F4] = v["L0_ffn_fWu"]
    mixA[0, 0:F4, 4 * P:5 * P] = v["L0_ffn_fWd"]
    mixA[0, :, -8] = v["L0_ffn_f_norm"]
    mixA[:, :, -7:-6] = chosen
    a["mixA"] = mixA
    w1 = np.concatenate([v["L1_ffn_sh_w1"][None], v["L1_ffn_ew1"]], 0)
    w2 = np.concatenate([v["L1_ffn_sh_w2"][None], v["L1_ffn_ew2"]], 0)
    b1 = np.concatenate([v["L1_ffn_sh_b1"][None], v["L1_ffn_eb1"]], 0)
    b2 = np.concatenate([v["L1_ffn_sh_b2"][None], v["L1_ffn_eb2"]], 0)
    mixB = np.zeros((SEQ, P, 8 * P + MISC), f)
    mixB[:, :, 0:4 * P] = w1
    mixB[:, :, 4 * P:8 * P] = w2.reshape(SEQ, 4, P, P).transpose(0, 2, 1, 3).reshape(SEQ, P, 4 * P)
    mixB[:, :, -6:-2] = b1.reshape(SEQ, 4, P).transpose(0, 2, 1)
    mixB[:, :, -7:-6] = chosen
    a["mixB"] = mixB
    b2B = np.zeros((32, P), f)
    b2B[0:SEQ] = b2
    b2B[16:16 + SEQ] = b2
    a["b2B"] = b2B
    for n in "qkv":
        a["hla_w" + n] = v["L0_attn_W_" + n]
    a["hla_wo"] = v["L0_attn_W_o"].reshape(8, P, P).transpose(1, 0, 2)
    a["att_w"] = np.stack([v["L1_attn_W_" + n].T for n in "qkvo"], 1)
    return {k: np.ascontiguousarray(z) for k, z in a.items()}


def kernel(**inputs):
    import numpy as _np
    import concourse.bacc as _bacc
    from concourse import mybir as _mybir
    from concourse.bass_utils import run_bass_kernel_spmd as _run

    nc = _bacc.Bacc("TRN2", target_bir_lowering=False, num_devices=1)
    arrays = {f"in_{k}": z for k, z in _layout(inputs).items()}
    args = {k[3:]: nc.dram_tensor(k, z.shape, _mybir.dt.from_np(z.dtype), kind="ExternalInput").ap()
            for k, z in arrays.items()}
    out = nc.dram_tensor("out", (TOK, P), _mybir.dt.float32, kind="ExternalOutput").ap()
    macaron(nc, args, out)
    r = _run(nc, [arrays], core_ids=[0])
    return r.results[0]["out"].reshape(NB, T, P)
```
